# Optimizing a Trainium2 kernel written in Bass

```python
import numpy as np
import jax
import jax.numpy as jnp

def _softmax(x, axis=-1):
    return jax.nn.softmax(x, axis=axis)

def _gelu(x):
    return jax.nn.gelu(x, approximate=True)

def _silu(x):
    return jax.nn.silu(x)

def _sigmoid(x):
    return jax.nn.sigmoid(x)

def _layernorm(x, axis=-1, eps=1e-05):
    m = jnp.mean(x, axis=axis, keepdims=True)
    v = jnp.var(x, axis=axis, keepdims=True)
    return (x - m) / jnp.sqrt(v + eps)

def _scatter_add(tgt, idx, src, axis=0):
    return tgt.at[idx].add(src)

def _segment_sum(src, seg, n):
    return jax.ops.segment_sum(src, seg, n)
kernel_name = 'mk_gnn_preln_d2_gnn_r64_697ec9'

def setup_inputs(seed: int=0):
    np.random.seed(seed)
    _w = jnp.asarray

    def _rec_inputs():
        import jax
        import jax.numpy as jnp
        _gk = jax.random.key(seed)
        x = -0.0006008 + 1.001 * jax.random.normal(jax.random.fold_in(_gk, 1), (50000, 256), jnp.float32)
        src = jax.random.randint(jax.random.fold_in(_gk, 2), (25000,), 0, 50000, jnp.int32)
        dst = jnp.minimum((50000 * jax.random.uniform(jax.random.fold_in(_gk, 3), (25000,)) ** 2.0).astype(jnp.int32), 49999)
        _o = jnp.argsort(dst, stable=True)
        src = src[_o]
        dst = dst[_o]
        return (x, src, dst)
    x, src, dst = _rec_inputs()

    def _L0_gnn_setup():
        import jax, jax.numpy as jnp
        import numpy as np
        N_ATOM = 10000
        D = 256
        N_EDGE = 2500
        BN_EPS = 1e-06

        def _bn_eval(x, g, b, m, v):
            return (x - m) * jax.lax.rsqrt(v + BN_EPS) * g + b
        key = jax.random.key(seed)
        ks = jax.random.split(key, 12)

        def glorot(k, shape):
            fan_in = shape[-1]
            return jax.random.normal(k, shape, dtype=jnp.float32) / np.sqrt(fan_in)
        inp = {'atom': jax.random.normal(ks[0], (N_ATOM, D), dtype=jnp.float32), 'bond_index': jax.random.randint(ks[1], (2, N_EDGE), 0, N_ATOM, dtype=jnp.int32), 'W_align': glorot(ks[2], (1, 2 * D)), 'b_align': jnp.zeros((1,), jnp.float32), 'bn_a_g': jnp.ones((1,), jnp.float32), 'bn_a_b': jnp.zeros((1,), jnp.float32), 'bn_a_m': jnp.zeros((1,), jnp.float32), 'bn_a_v': jnp.ones((1,), jnp.float32), 'W_att': glorot(ks[3], (D, D)), 'b_att': jnp.zeros((D,), jnp.float32), 'bn_t_g': jnp.ones((D,), jnp.float32), 'bn_t_b': jnp.zeros((D,), jnp.float32), 'bn_t_m': jnp.zeros((D,), jnp.float32), 'bn_t_v': jnp.ones((D,), jnp.float32), 'W_ih': glorot(ks[4], (3 * D, D)), 'W_hh': glorot(ks[5], (3 * D, D)), 'b_ih': jnp.zeros((3 * D,), jnp.float32), 'b_hh': jnp.zeros((3 * D,), jnp.float32)}
        return inp
    _L0_gnn_all = _L0_gnn_setup()
    _L0_gnn_in = {k: v for k, v in _L0_gnn_all.items() if k in ('W_align', 'b_align', 'bn_a_g', 'bn_a_b', 'bn_a_m', 'bn_a_v', 'W_att', 'b_att', 'bn_t_g', 'bn_t_b', 'bn_t_m', 'bn_t_v', 'W_ih', 'W_hh', 'b_ih', 'b_hh')}
    del _L0_gnn_all

    def _L1_gnn_setup():
        import jax, jax.numpy as jnp
        import numpy as np
        N = 100000
        E = 25000
        D = 256
        BN_EPS = 1e-05

        def _batchnorm(x, gamma, beta):
            mu = jnp.mean(x, axis=0)
            var = jnp.var(x, axis=0)
            return (x - mu) * jax.lax.rsqrt(var + BN_EPS) * gamma + beta

        def _gin_conv(x, src, dst, n, W1, b1, gamma, beta, W2, b2):
            agg = jax.ops.segment_sum(x[src], dst, num_segments=n)
            h = x + agg
            h = jax.nn.relu(_batchnorm(h @ W1 + b1, gamma, beta))
            return jax.nn.relu(h @ W2 + b2)
        key = jax.random.key(seed)
        ks = jax.random.split(key, 8)
        x = jax.random.normal(ks[0], (N, D), dtype=jnp.float32)
        edge_index = jax.random.randint(ks[1], (2, E), 0, N, dtype=jnp.int64)
        s = 0.02
        inp = {'x': x, 'edge_index': edge_index, 'g0': jnp.ones((D,), jnp.float32), 'b0': jnp.zeros((D,), jnp.float32), 'W1a': jax.random.normal(ks[2], (D, D), jnp.float32) * s, 'b1a': jnp.zeros((D,), jnp.float32), 'g1': jnp.ones((D,), jnp.float32), 'bt1': jnp.zeros((D,), jnp.float32), 'W1b': jax.random.normal(ks[3], (D, D), jnp.float32) * s, 'b1b': jnp.zeros((D,), jnp.float32), 'W2a': jax.random.normal(ks[4], (D, D), jnp.float32) * s, 'b2a': jnp.zeros((D,), jnp.float32), 'g2': jnp.ones((D,), jnp.float32), 'bt2': jnp.zeros((D,), jnp.float32), 'W2b': jax.random.normal(ks[5], (D, D), jnp.float32) * s, 'b2b': jnp.zeros((D,), jnp.float32)}
        return inp
    _L1_gnn_all = _L1_gnn_setup()
    _L1_gnn_in = {k: v for k, v in _L1_gnn_all.items() if k in ('g0', 'b0', 'W1a', 'b1a', 'g1', 'bt1', 'W1b', 'b1b', 'W2a', 'b2a', 'g2', 'bt2', 'W2b', 'b2b')}
    del _L1_gnn_all
    return {'x': x, 'src': src, 'dst': dst, 'L0_gnn_W_align': _L0_gnn_in['W_align'], 'L0_gnn_b_align': _L0_gnn_in['b_align'], 'L0_gnn_bn_a_g': _L0_gnn_in['bn_a_g'], 'L0_gnn_bn_a_b': _L0_gnn_in['bn_a_b'], 'L0_gnn_bn_a_m': _L0_gnn_in['bn_a_m'], 'L0_gnn_bn_a_v': _L0_gnn_in['bn_a_v'], 'L0_gnn_W_att': _L0_gnn_in['W_att'], 'L0_gnn_b_att': _L0_gnn_in['b_att'], 'L0_gnn_bn_t_g': _L0_gnn_in['bn_t_g'], 'L0_gnn_bn_t_b': _L0_gnn_in['bn_t_b'], 'L0_gnn_bn_t_m': _L0_gnn_in['bn_t_m'], 'L0_gnn_bn_t_v': _L0_gnn_in['bn_t_v'], 'L0_gnn_W_ih': _L0_gnn_in['W_ih'], 'L0_gnn_W_hh': _L0_gnn_in['W_hh'], 'L0_gnn_b_ih': _L0_gnn_in['b_ih'], 'L0_gnn_b_hh': _L0_gnn_in['b_hh'], 'L1_gnn_g0': _L1_gnn_in['g0'], 'L1_gnn_b0': _L1_gnn_in['b0'], 'L1_gnn_W1a': _L1_gnn_in['W1a'], 'L1_gnn_b1a': _L1_gnn_in['b1a'], 'L1_gnn_g1': _L1_gnn_in['g1'], 'L1_gnn_bt1': _L1_gnn_in['bt1'], 'L1_gnn_W1b': _L1_gnn_in['W1b'], 'L1_gnn_b1b': _L1_gnn_in['b1b'], 'L1_gnn_W2a': _L1_gnn_in['W2a'], 'L1_gnn_b2a': _L1_gnn_in['b2a'], 'L1_gnn_g2': _L1_gnn_in['g2'], 'L1_gnn_bt2': _L1_gnn_in['bt2'], 'L1_gnn_W2b': _L1_gnn_in['W2b'], 'L1_gnn_b2b': _L1_gnn_in['b2b']}

def reference(x, src, dst, L0_gnn_W_align, L0_gnn_b_align, L0_gnn_bn_a_g, L0_gnn_bn_a_b, L0_gnn_bn_a_m, L0_gnn_bn_a_v, L0_gnn_W_att, L0_gnn_b_att, L0_gnn_bn_t_g, L0_gnn_bn_t_b, L0_gnn_bn_t_m, L0_gnn_bn_t_v, L0_gnn_W_ih, L0_gnn_W_hh, L0_gnn_b_ih, L0_gnn_b_hh, L1_gnn_g0, L1_gnn_b0, L1_gnn_W1a, L1_gnn_b1a, L1_gnn_g1, L1_gnn_bt1, L1_gnn_W1b, L1_gnn_b1b, L1_gnn_W2a, L1_gnn_b2a, L1_gnn_g2, L1_gnn_bt2, L1_gnn_W2b, L1_gnn_b2b):
    import jax
    import jax.numpy as jnp

    def _L0_gnn_ref(atom, bond_index, W_align, b_align, bn_a_g, bn_a_b, bn_a_m, bn_a_v, W_att, b_att, bn_t_g, bn_t_b, bn_t_m, bn_t_v, W_ih, W_hh, b_ih, b_hh):
        import jax, jax.numpy as jnp
        import numpy as np
        N_ATOM = 10000
        D = 256
        N_EDGE = 2500
        BN_EPS = 1e-06

        def _bn_eval(x, g, b, m, v):
            return (x - m) * jax.lax.rsqrt(v + BN_EPS) * g + b
        num_atom = atom.shape[0]
        src = bond_index[0]
        dst = bond_index[1]
        feat_align = jnp.concatenate([atom[src], atom[dst]], axis=-1)
        s = feat_align @ W_align.T + b_align
        s = _bn_eval(s, bn_a_g, bn_a_b, bn_a_m, bn_a_v)
        s = jax.nn.leaky_relu(s, negative_slope=0.01)
        seg_max = jax.ops.segment_max(s, src, num_segments=num_atom)
        e = jnp.exp(s - seg_max[src])
        denom = jax.ops.segment_sum(e, src, num_segments=num_atom)
        attn = e / (denom[src] + 1e-08)
        h = atom[dst] @ W_att.T + b_att
        h = _bn_eval(h, bn_t_g, bn_t_b, bn_t_m, bn_t_v)
        context = jax.ops.segment_sum(attn * h, src, num_segments=num_atom)
        context = jax.nn.elu(context)
        gi = context @ W_ih.T + b_ih
        gh = atom @ W_hh.T + b_hh
        i_r, i_z, i_n = jnp.split(gi, 3, axis=-1)
        h_r, h_z, h_n = jnp.split(gh, 3, axis=-1)
        r = jax.nn.sigmoid(i_r + h_r)
        z = jax.nn.sigmoid(i_z + h_z)
        n = jnp.tanh(i_n + r * h_n)
        update = (1.0 - z) * n + z * atom
        return update

    def _L1_gnn_ref(x, edge_index, g0, b0, W1a, b1a, g1, bt1, W1b, b1b, W2a, b2a, g2, bt2, W2b, b2b):
        import jax, jax.numpy as jnp
        import numpy as np
        N = 100000
        E = 25000
        D = 256
        BN_EPS = 1e-05

        def _batchnorm(x, gamma, beta):
            mu = jnp.mean(x, axis=0)
            var = jnp.var(x, axis=0)
            return (x - mu) * jax.lax.rsqrt(var + BN_EPS) * gamma + beta

        def _gin_conv(x, src, dst, n, W1, b1, gamma, beta, W2, b2):
            agg = jax.ops.segment_sum(x[src], dst, num_segments=n)
            h = x + agg
            h = jax.nn.relu(_batchnorm(h @ W1 + b1, gamma, beta))
            return jax.nn.relu(h @ W2 + b2)
        n = x.shape[0]
        src, dst = (edge_index[0], edge_index[1])
        h = _batchnorm(x, g0, b0)
        h = _gin_conv(h, src, dst, n, W1a, b1a, g1, bt1, W1b, b1b)
        h = jax.nn.relu(h)
        h = _gin_conv(h, src, dst, n, W2a, b2a, g2, bt2, W2b, b2b)
        return jax.nn.relu(h)
    edge_index = jnp.stack([src, dst])
    h = jnp.maximum(_layernorm(x, axis=-1), 0.0)
    x = x + _L0_gnn_ref(h, edge_index, L0_gnn_W_align, L0_gnn_b_align, L0_gnn_bn_a_g, L0_gnn_bn_a_b, L0_gnn_bn_a_m, L0_gnn_bn_a_v, L0_gnn_W_att, L0_gnn_b_att, L0_gnn_bn_t_g, L0_gnn_bn_t_b, L0_gnn_bn_t_m, L0_gnn_bn_t_v, L0_gnn_W_ih, L0_gnn_W_hh, L0_gnn_b_ih, L0_gnn_b_hh)
    h = jnp.maximum(_layernorm(x, axis=-1), 0.0)
    x = x + _L1_gnn_ref(h, edge_index, L1_gnn_g0, L1_gnn_b0, L1_gnn_W1a, L1_gnn_b1a, L1_gnn_g1, L1_gnn_bt1, L1_gnn_W1b, L1_gnn_b1b, L1_gnn_W2a, L1_gnn_b2a, L1_gnn_g2, L1_gnn_bt2, L1_gnn_W2b, L1_gnn_b2b)
    return x

_drawn_inputs = setup_inputs


def setup_inputs(seed=0):
    import zlib

    import numpy as np

    out = dict(_drawn_inputs(seed))
    spreads = {'L0_gnn_b_att': (0.0, 0.404),
     'L0_gnn_bn_t_g': (1.0, 0.6),
     'L0_gnn_bn_t_b': (0.0, 0.437),
     'L0_gnn_bn_t_m': (0.0, 0.395),
     'L0_gnn_bn_t_v': (1.0, 0.6),
     'L0_gnn_b_ih': (0.0, 0.1),
     'L0_gnn_b_hh': (0.0, 0.341),
     'L1_gnn_g0': (1.0, 0.6),
     'L1_gnn_b0': (0.0, 0.8),
     'L1_gnn_b1a': (0.0, 0.8),
     'L1_gnn_g1': (1.0, 0.6),
     'L1_gnn_bt1': (0.0, 0.748),
     'L1_gnn_b1b': (0.0, 0.1),
     'L1_gnn_b2a': (0.0, 0.8),
     'L1_gnn_g2': (1.0, 0.6),
     'L1_gnn_bt2': (0.0, 0.651),
     'L1_gnn_b2b': (0.0, 0.1)}
    factors = {'L0_gnn_W_align': 7.3}
    for name, (base, spread) in spreads.items():
        noise = np.random.default_rng([zlib.crc32(name.encode()), seed]).standard_normal(out[name].shape)
        drawn = base * np.exp(spread * noise) if base else spread * noise
        out[name] = jnp.asarray(drawn.astype(out[name].dtype))
    for name, factor in factors.items():
        out[name] = (out[name] * factor).astype(out[name].dtype)
    return out
```

```python
from contextlib import ExitStack

import concourse.bass as bass
import numpy as np
from concourse import mybir

F32, I32, BF16, F16 = mybir.dt.float32, mybir.dt.int32, mybir.dt.bfloat16, mybir.dt.float16
ALU = mybir.AluOpType
ACT = mybir.ActivationFunctionType

P = 128
D = 256
KC = D // P
T = 4
ROWS = P * T
LN_EPS = 1e-5
BN_A_EPS = 1e-6
BN_B_EPS = 1e-5
NO_ROW = 1 << 20
BELOW_ALL = -1e30


class Dims:

    def __init__(self, nodes, edges):
        self.N, self.E = nodes, edges
        self.NG = -(-nodes // ROWS)
        self.AC = self.NG * T
        self.NPAD = self.AC * P
        self.WIDE = max(self.AC, P)
        self.FULL = nodes // ROWS
        self.TAIL = [min(P, nodes - r) for r in range(self.FULL * ROWS, nodes, P)]
        self.ET = -(-edges // P)
        self.EG = self.ET // T
        self.EPAD = self.ET * P
        self.TH = self.ET // 2
        assert self.FULL == self.NG - 1 and self.FULL % 2 == 1 and self.TAIL
        assert self.ET % T == 0 and self.EG % 2 == 1 and self.TH <= P and self.AC <= 512


class Link:

    def __init__(self, eng, sem, base=0):
        self.eng, self.sem, self.base, self.n = eng, sem, base, 0

    def __call__(self, ins):
        ins.then_inc(self.sem, 1)
        self.n += 1
        self.eng.wait_ge(self.sem, self.base + self.n)


class Space:

    def __init__(self, nc, ctx, tag):
        self.nc, self.ctx, self.tag, self.own = nc, ctx, tag, []

    def sb(self, name, shape, dt=F32):
        return self.ctx.enter_context(self.nc.sbuf_tensor(f"{self.tag}_{name}", shape, dt))

    def ps(self, name, shape, dt=F32):
        bank = self.ctx.enter_context(self.nc.psum_tensor(f"{self.tag}_{name}", [P, 512 if dt == F32 else 1024], dt))
        view = bank[0:shape[0], 0:int(np.prod(shape[1:]))]
        names = "abc"[:len(shape) - 1]
        return view if len(shape) == 2 else view.rearrange(
            f"p ({' '.join(names)}) -> p {' '.join(names)}", **dict(zip(names, shape[1:])))

    def sem(self, name):
        sem = self.nc.alloc_semaphore(f"{self.tag}_{name}")
        if not self.own:
            self.ctx.callback(self.clear)
        self.own.append(sem)
        return sem

    def clear(self):
        self.nc.clear_and_free_semaphores(self.own)
        self.nc.all_engine_barrier()

    def sems(self, name, n=2):
        return [self.sem(f"{name}{k}") for k in range(n)]


def over_groups(eng, full, body, tail=False, peeled=0):
    for g in range(3):
        body(g, g % 2, g // 2, False)
    if full - peeled > 3:
        with eng.Fori(1, (full - peeled - 1) // 2) as i:
            body(2 * i + 1, 1, i, False)
            body(2 * i + 2, 0, i + 1, False)
    for g in range(full - peeled, full):
        body(g, g % 2, g // 2, False)
    if tail:
        body(full, full % 2, full // 2, True)


def uses(groups, slot):
    return (groups + 1 - slot) // 2


def first_group(g):
    return isinstance(g, int) and g == 0


def wait_alone(eng, sem, value, held):
    eng.wait_ge(sem, value)
    if not isinstance(value, int):
        eng.sem_inc(held, 1)


def tile_rows(dm, is_tail):
    return dm.TAIL if is_tail else [P] * T


def rows_dma(eng, dram, sbuf, g, dm, is_tail, sem, store=False):
    def move(d, s, inc):
        eng.dma_start(*((d, s) if store else (s, d))).then_inc(sem, inc)
    if not is_tail:
        move(dram[bass.ds(g * ROWS, ROWS), :].rearrange("(k p) c -> p k c", p=P), sbuf[:, :, :], 32)
        return
    n = len(dm.TAIL) - 1
    assert n >= 1
    move(dram[g * ROWS:g * ROWS + n * P, :].rearrange("(k p) c -> p k c", p=P), sbuf[:, 0:n, :], 16)
    move(dram[g * ROWS + n * P:dm.N, :], sbuf[0:dm.TAIL[-1], n, :], 16)


def parts_of(dm, is_tail):
    n = len(dm.TAIL) - 1
    return [(0, n, P), (n, n + 1, dm.TAIL[-1])] if is_tail else [(0, T, P)]



def constants_phase(nc, dm, C):
    with ExitStack() as ctx:
        sp = Space(nc, ctx, "cst")
        s_held = sp.sem("held")
        iota_i = sp.sb("iota_i", [P, dm.WIDE], I32)
        col_i = sp.sb("col_i", [P, 1], I32)
        s_mem, s_sel, s_iota = sp.sem("mem"), sp.sem("sel"), sp.sem("iota")
        s_conv = sp.sem("conv")
        with nc.Block() as block:
            @block.gpsimd
            def _(pool):
                pool.iota(iota_i[:, :], pattern=[[1, dm.WIDE]], base=0, channel_multiplier=0).then_inc(s_iota, 1)
                pool.iota(col_i[:, :], pattern=[[0, 1]], base=0, channel_multiplier=1).then_inc(s_iota, 1)
                pool.memset(C.ident[:, :], 0.0).then_inc(s_mem, 1)
                pool.memset(C.lower[:, :], 1.0).then_inc(s_mem, 1)
                pool.memset(C.upper[:, :], 1.0).then_inc(s_mem, 1)
                pool.memset(C.minus_half[:, :], -0.5).then_inc(s_mem, 1)
                pool.memset(C.ones[:, :], 1.0).then_inc(s_mem, 1)
                pool.wait_ge(s_mem, 5)
                pool.affine_select(out=C.ident[:, :], in_=C.ident[:, :], compare_op=ALU.not_equal, fill=1.0,
                                   base=0, pattern=[[-1, P]], channel_multiplier=1).then_inc(s_sel, 1)
                pool.affine_select(out=C.lower[:, :], in_=C.lower[:, :], compare_op=ALU.is_gt, fill=0.0,
                                   base=0, pattern=[[-1, P]], channel_multiplier=1).then_inc(s_sel, 1)
                pool.affine_select(out=C.upper[:, :], in_=C.upper[:, :], compare_op=ALU.is_gt, fill=0.0,
                                   base=0, pattern=[[1, P]], channel_multiplier=-1).then_inc(s_sel, 1)
                pool.wait_ge(s_sel, 3)

            @block.vector
            def _(dve):
                dve.wait_ge(s_iota, 2)
                dve.tensor_copy(C.iota[:, :], iota_i[:, :]).then_inc(s_conv, 1)
                dve.tensor_copy(C.col[:, :], col_i[:, :]).then_inc(s_conv, 1)
                dve.wait_ge(s_sel, 3)
                dve.tensor_copy(C.ident_h[:, :], C.ident[:, :]).then_inc(s_conv, 1)
                dve.wait_ge(s_conv, 3)



def edges_phase(nc, dm, C, src, dst, src_edges, dst_edges):
    with ExitStack() as ctx:
        sp = Space(nc, ctx, "edg")
        s_held = sp.sem("held")
        raw = [sp.sb(f"raw{k}", [P, dm.ET], I32) for k in range(2)]
        part = [sp.sb(f"part{k}", [P, dm.ET], I32) for k in range(2)]
        key = [sp.sb(f"key{k}", [P, dm.ET]) for k in range(2)]
        s_fill, s_load, s_link = sp.sem("fill"), sp.sem("load"), sp.sem("link")
        whole = dm.E // dm.ET
        rest = dm.E - whole * dm.ET
        with nc.Block() as block:
            @block.vector
            def _(dve):
                link = Link(dve, s_link)
                for k in range(2):
                    dve.memset(raw[k][:, :], dm.NPAD - 1).then_inc(s_fill, 1)
                dve.wait_ge(s_load, 16 * (4 if rest else 2))
                for k in range(2):
                    link(dve.tensor_copy(key[k][:, :], raw[k][:, :]))
                for k, edges in enumerate((src_edges, dst_edges)):
                    link(dve.tensor_scalar(part[0][:, :], raw[k][:, :], 7, None, ALU.arith_shift_right))
                    link(dve.tensor_scalar(part[1][:, :], raw[k][:, :], P - 1, None, ALU.bitwise_and))
                    link(dve.tensor_copy(edges.hi[:, :], part[0][:, :]))
                    link(dve.tensor_copy(edges.lo[:, :], part[1][:, :]))
                    link(dve.tensor_copy(edges.pay[:, :, 0], key[k][:, :]))
                    other = key[1 - k]
                    link(dve.scalar_tensor_tensor(out=edges.pay[:, :, 1], in0=other[:, :], scalar=float(dm.N),
                                                  in1=other[:, :], op0=ALU.is_lt, op1=ALU.mult))

            @block.sync
            def _(sync):
                sync.wait_ge(s_fill, 2)
                for k, e in enumerate((src, dst)):
                    sync.dma_start(raw[k][0:whole, :],
                                   e[0:whole * dm.ET].rearrange("(p f) -> p f", f=dm.ET)).then_inc(s_load, 16)
                    if rest:
                        sync.dma_start(raw[k][whole:whole + 1, 0:rest],
                                       e[whole * dm.ET:dm.E].rearrange("(p f) -> p f", p=1)).then_inc(s_load, 16)
                sync.wait_ge(s_load, 16 * (4 if rest else 2))



def sort_phase(nc, dm, C, edges, tag):
    AC = dm.AC
    with ExitStack() as ctx:
        sp = Space(nc, ctx, tag)
        s_held = sp.sem("held")
        ohl = [sp.sb(f"ohl{s}", [P, T, P], BF16) for s in range(2)]
        ohh = [sp.sb(f"ohh{s}", [P, T, AC], BF16) for s in range(2)]
        ohlT = [sp.sb(f"ohlT{s}", [P, T, P]) for s in range(2)]
        keys = [sp.sb(f"keys{s}", [P, T]) for s in range(2)]
        start_at = sp.sb("start_at", [P, AC])
        scanned = sp.sb("scanned", [P, AC])
        zeros = sp.sb("zeros", [P, AC])
        run = [sp.sb(f"run{k}", [P, AC]) for k in range(2)]
        waste = [sp.sb(f"waste{k}", [P, AC + P]) for k in range(2)]
        tmp = sp.sb("tmp", [P, AC])
        before = sp.sb("before", [P, T])
        inside = sp.sb("inside", [P, T])
        place = [sp.sb(f"place{s}", [P, T], I32) for s in range(2)]
        pay = [sp.sb(f"pay{s}", [P, T, 2]) for s in range(2)]
        zero_h = sp.sb("zero_h", [P, dm.WIDE], BF16)
        hist = sp.ps("hist", [P, 512])
        look = [sp.ps(f"look{k}", [P, 512]) for k in range(2)]
        keyrow = [sp.ps(f"keyrow{s}", [P, T, P]) for s in range(2)]
        turned = [sp.ps(f"turned{s}", [P, T, P], BF16) for s in range(2)]
        H = hist[:, 0:AC]

        s_zero, s_oh1, s_hist1, s_link = sp.sem("zero"), sp.sem("oh1"), sp.sem("hist1"), sp.sem("link")
        s_rowsum, s_base, s_start, s_seed = sp.sem("rowsum"), sp.sem("base"), sp.sem("start"), sp.sem("seed")
        s_oh, s_keys, s_turn, s_turned, s_look = sp.sem("oh"), sp.sem("keys"), sp.sem("turn"), sp.sem("turned"), sp.sem("look")
        s_hist, s_run, s_cnt, s_place = sp.sem("hist"), sp.sem("run"), sp.sem("cnt"), sp.sem("place")
        s_pay, s_scat = sp.sems("pay"), sp.sems("scat")
        s_link2, s_in = sp.sem("link2"), sp.sem("in")

        with nc.Block() as block:
            @block.vector
            def _(dve):
                def one_hots(g, s, k, ready):
                    dve.tensor_scalar(ohl[s][:, k, :], C.iota[:, 0:P], edges.lo[:, bass.ds(T * g + k, 1)], None,
                                      ALU.is_equal).then_inc(ready, 1)
                    dve.tensor_scalar(ohh[s][:, k, :], C.iota[:, 0:AC], edges.hi[:, bass.ds(T * g + k, 1)], None,
                                      ALU.is_equal).then_inc(ready, 1)

                dve.memset(zero_h[:, :], 0.0).then_inc(s_zero, 1)
                dve.memset(zeros[:, :], 0.0).then_inc(s_zero, 1)
                def count(g, s, u, is_tail):
                    if not first_group(g):
                        dve.wait_ge(s_hist1, T * (g - 1) + 1)
                    for k in range(T):
                        one_hots(g, s, k, s_oh1)
                over_groups(dve, dm.EG, count)
                link = Link(dve, s_link)
                dve.wait_ge(s_hist1, dm.ET + 1)
                link(dve.tensor_copy(edges.count[:, :], H))
                link(dve.tensor_tensor_scan(scanned[:, :], edges.count[:, :], zeros[:, :], 0.0, ALU.add, ALU.add))
                dve.tensor_copy(before[:, 0:1], scanned[:, AC - 1:AC]).then_inc(s_rowsum, 1)
                dve.wait_ge(s_base, 1)
                link(dve.tensor_copy(inside[:, 0:1], look[0][:, 0:1]))
                link(dve.tensor_scalar(scanned[:, :], scanned[:, :], inside[:, 0:1], None, ALU.add))
                dve.tensor_tensor(start_at[:, :], scanned[:, :], edges.count[:, :], ALU.subtract).then_inc(s_start, 1)
                link(dve.tensor_scalar(tmp[:, :], edges.count[:, :], 0.0, float(NO_ROW), ALU.is_equal, ALU.mult))
                link(dve.scalar_tensor_tensor(out=tmp[:, :], in0=scanned[:, :], scalar=-1.0, in1=tmp[:, :],
                                              op0=ALU.add, op1=ALU.add))
                link(dve.tensor_copy(edges.last[:, :], tmp[:, :]))

                def find(g, s, k):
                    n = T * g + k
                    dve.wait_ge(s_look, n + 1)
                    if k >= 2:
                        dve.wait_ge(s_cnt, 2 * n - 2)
                    dve.scalar_tensor_tensor(out=waste[k % 2][:, dm.AC:], in0=keyrow[s][:, k, :], scalar=keys[s][:, k:k + 1],
                                             in1=C.lower[:, :], op0=ALU.is_equal, op1=ALU.mult,
                                             accum_out=inside[:, k:k + 1]).then_inc(s_cnt, 1)
                    dve.scalar_tensor_tensor(out=waste[k % 2][:, 0:AC], in0=look[k % 2][:, 0:AC], scalar=1.0,
                                             in1=ohh[s][:, k, :], op0=ALU.mult, op1=ALU.mult,
                                             accum_out=before[:, k:k + 1]).then_inc(s_cnt, 1)

                def take_keys(g, s):
                    dve.tensor_copy(keys[s][:, :], edges.pay[:, bass.ds(T * g, T), 0]).then_inc(s_keys, 1)

                def step(g, s, u, is_tail):
                    more = not (isinstance(g, int) and g + 2 >= dm.EG)
                    for k in range(T):
                        find(g, s, k)
                        if more:
                            dve.wait_ge(s_cnt, 2 * (T * g + k) + 2)
                            one_hots(g + 2, s, k, s_oh)
                    dve.wait_ge(s_cnt, 2 * T * g + 2 * T)
                    if more:
                        take_keys(g + 2, s)
                    dve.wait_ge(s_scat[s], 64 * u)
                    dve.tensor_tensor(place[s][:, :], before[:, :], inside[:, :], ALU.add).then_inc(s_place, 1)
                    dve.wait_ge(s_place, g + 1)

                dve.wait_ge(s_hist1, dm.ET + 1)
                for g in range(2):
                    take_keys(g, g)
                    for k in range(T):
                        one_hots(g, g, k, s_oh)
                over_groups(dve, dm.EG, step, peeled=2)

            @block.tensor
            def _(pe):
                pe.wait_ge(s_zero, 2)
                pe.matmul(H, zero_h[:, 0:P], zero_h[:, 0:AC], start=True, stop=True, skip_group_check=True).then_inc(s_hist1, 1)
                def count(g, s, u, is_tail):
                    for k in range(T):
                        pe.wait_ge(s_oh1, 2 * (T * g + k + 1))
                        pe.matmul(H, ohl[s][:, k, :], ohh[s][:, k, :], start=False, stop=True,
                                  skip_group_check=True).then_inc(s_hist1, 1)
                over_groups(pe, dm.EG, count)
                pe.wait_ge(s_rowsum, 1)
                pe.matmul(look[0][:, 0:1], C.upper[:, :], before[:, 0:1], start=True, stop=True).then_inc(s_base, 1)
                pe.wait_ge(s_start, 1)
                pe.matmul(H, C.ident[:, :], start_at[:, :], start=True, stop=True, skip_group_check=True).then_inc(s_seed, 1)

                def turn(g, s):
                    pe.wait_ge(s_oh, 2 * T * (g + 1))
                    pe.wait_ge(s_keys, g + 1)
                    if not (isinstance(g, int) and g < 2):
                        pe.wait_ge(s_turned, g - 1)
                        pe.wait_ge(s_cnt, 2 * T * (g - 1))
                    for k in range(T):
                        pe.transpose(turned[s][:, k, :], ohl[s][:, k, :], C.ident_h[:, :])
                        ins = pe.matmul(keyrow[s][:, k, :], keys[s][:, k:k + 1].to_broadcast([P, P]), C.ident[:, :],
                                        start=True, stop=True)
                    ins.then_inc(s_turn, 1)

                turn(0, 0)
                def step(g, s, u, is_tail):
                    if not (isinstance(g, int) and g + 1 == dm.EG):
                        turn(g + 1, 1 - s)
                    pe.wait_ge(s_turned, g + 1)
                    for k in range(T):
                        n = T * g + k
                        pe.wait_ge(s_run, n + 1)
                        pe.matmul(H, ohl[s][:, k, :], ohh[s][:, k, :], start=False, stop=True,
                                  skip_group_check=True).then_inc(s_hist, 1)
                        if k >= 2 or not first_group(g):
                            pe.wait_ge(s_cnt, 2 * n - 2)
                        pe.matmul(look[k % 2][:, 0:AC], ohlT[s][:, k, :], run[k % 2][:, :], start=True, stop=True).then_inc(s_look, 1)
                over_groups(pe, dm.EG, step, peeled=2)

            @block.scalar
            def _(act):
                act.wait_ge(s_seed, 1)
                act.copy(run[0][:, :], H).then_inc(s_run, 1)

                def turned_out(g, s):
                    act.wait_ge(s_turn, g + 1)
                    if not (isinstance(g, int) and g < 2):
                        act.wait_ge(s_look, T * (g - 1))
                    act.copy(ohlT[s][:, :, :], turned[s][:, :, :]).then_inc(s_turned, 1)

                turned_out(0, 0)
                def step(g, s, u, is_tail):
                    for k in range(T):
                        n = T * g + k
                        act.wait_ge(s_hist, n + 1)
                        act.wait_ge(s_look, n)
                        act.copy(run[(k + 1) % 2][:, :], H).then_inc(s_run, 1)
                        if k == 0 and not (isinstance(g, int) and g + 1 == dm.EG):
                            turned_out(g + 1, 1 - s)
                over_groups(act, dm.EG, step, peeled=2)

            @block.gpsimd
            def _(pool):
                def tiles(g, s, u, is_tail):
                    wait_alone(pool, s_scat[s], 64 * u, s_held)
                    wait_alone(pool, s_place, g + 1, s_held)
                    pool.tensor_copy(pay[s][:, :, :], edges.pay[:, bass.ds(T * g, T), :]).then_inc(s_pay[s], 1)
                    wait_alone(pool, s_pay[s], u + 1, s_held)
                    for k in range(T):
                        pool.indirect_dma_start(edges.sorted, bass.IndirectOffsetOnAxis(ap=place[s][:, k:k + 1], axis=0),
                                                pay[s][:, k, :], None).then_inc(s_scat[s], 16)
                over_groups(pool, dm.EG, tiles)
                for s in range(2):
                    pool.wait_ge(s_scat[s], 64 * uses(dm.EG, s))


def sorted_phase(nc, dm, C, edges, tag):
    TH = dm.TH
    with ExitStack() as ctx:
        sp = Space(nc, ctx, tag)
        s_held = sp.sem("held")
        rows = sp.sb("rows", [TH, 2, P, 2])
        same = sp.sb("same", [TH, P])
        n_first = sp.sb("n_first", [TH, 2])
        firsts = sp.ps("firsts", [P, 2, P])
        cols = sp.ps("cols", [P, 2, 2, TH])
        s_load, s_turn, s_row, s_link, s_copy = sp.sem("load"), sp.sem("turn"), sp.sem("row"), sp.sem("link"), sp.sem("copy")
        with nc.Block() as block:
            @block.sync
            def _(sync):
                sync.dma_start(rows[:, :, :, :].rearrange("p h j c -> p h (j c)"),
                               edges.sorted.rearrange("(h p j) c -> p h (j c)", p=TH, j=P)).then_inc(s_load, 16)
                sync.wait_ge(s_load, 16)

            @block.tensor
            def _(pe):
                pe.wait_ge(s_load, 16)
                for c in range(2):
                    for h in range(2):
                        pe.transpose(cols[:, c, h, :], rows[:, h, :, c], C.ident[0:TH, 0:TH]).then_inc(s_turn, 1)
                for h in range(2):
                    pe.matmul(firsts[:, h, 0:TH], rows[:, h, 0:1, 0].to_broadcast([TH, P]), C.ident[0:TH, 0:TH],
                              start=True, stop=True).then_inc(s_row, 1)

            @block.vector
            def _(dve):
                link = Link(dve, s_link)
                dve.wait_ge(s_turn, 4)
                dve.tensor_copy(edges.keyT[:, :].rearrange("p (h t) -> p h t", h=2), cols[:, 0, :, :]).then_inc(s_copy, 1)
                dve.tensor_copy(edges.otherT[:, :].rearrange("p (h t) -> p h t", h=2), cols[:, 1, :, :]).then_inc(s_copy, 1)
                dve.wait_ge(s_row, 2)
                for h1 in range(2):
                    for h in range(h1, 2):
                        last_key = rows[:, h1, P - 1:P, 0]
                        if h == h1:
                            dve.scalar_tensor_tensor(out=edges.joins[0:TH, h1, h, :], in0=firsts[0:TH, h, 0:TH],
                                                     scalar=last_key, in1=C.upper[0:TH, 0:TH], op0=ALU.is_equal,
                                                     op1=ALU.mult).then_inc(s_copy, 1)
                        else:
                            dve.tensor_scalar(edges.joins[0:TH, h1, h, :], firsts[0:TH, h, 0:TH], last_key, None,
                                              ALU.is_equal).then_inc(s_copy, 1)
                for h in range(2):
                    link(dve.tensor_scalar(same[:, :], rows[:, h, :, 0], rows[:, h, 0:1, 0], 0.0, ALU.is_equal,
                                           ALU.add, accum_out=n_first[:, h:h + 1]))
                    link(dve.scalar_tensor_tensor(out=n_first[:, h:h + 1], in0=C.col[0:TH, :], scalar=float(P),
                                                  in1=n_first[:, h:h + 1], op0=ALU.mult, op1=ALU.add))
                    link(dve.tensor_scalar(edges.first_end[0:TH, h:h + 1], n_first[:, h:h + 1],
                                           float(h * TH * P - 1), None, ALU.add))
                dve.wait_ge(s_copy, 5)



def norm_stats(dve, link, x4, stats, mv, s_held):
    for dst, src, op in ((stats, x4, dve.bn_stats), (mv, stats, dve.bn_aggr)):
        for k in range(T):
            ins = op(dst[:, k, :], src[:, k, :])
            if k + 1 < T:
                ins.then_inc(link.sem, 1)
                link.n += 1
        ins.then_inc(link.sem, 1)
        link.n += 1
        wait_alone(dve, link.sem, link.base + link.n, s_held)


def norm_phase(nc, dm, C, x, w_align, h_out, a_out):
    with ExitStack() as ctx:
        sp = Space(nc, ctx, "nrm")
        s_held = sp.sem("held")
        x4 = [sp.sb(f"x{s}", [P, T, D]) for s in range(2)]
        h4 = [sp.sb(f"h{s}", [P, T, D]) for s in range(2)]
        stats = sp.sb("stats", [P, T, 6])
        mv = [sp.sb(f"mv{s}", [P, T, 2]) for s in range(2)]
        rstd = [sp.sb(f"rstd{s}", [P, T]) for s in range(2)]
        shift = [sp.sb(f"shift{s}", [P, T]) for s in range(2)]
        wide = sp.sb("wide", [P, 2, D])
        waste = [sp.sb(f"waste{j}", [P, D]) for j in range(4)]
        score = [sp.sb(f"score{j}", [P, dm.AC]) for j in range(2)]
        dots = [sp.sb(f"dots{s}", [P, T, 2]) for s in range(2)]
        s_x, s_st = sp.sems("x"), sp.sems("st")
        s_w, s_zero, s_link, s_mv, s_var, s_rstd, s_shift, s_h, s_dot = (sp.sem(n) for n in (
            "w", "zero", "link", "mv", "var", "rstd", "shift", "h", "dot"))
        s_table, s_a = sp.sem("table"), sp.sem("a")
        with nc.Block() as block:
            @block.sync
            def _(sync):
                sync.dma_start(wide[:, :, :].rearrange("p a c -> p (a c)"),
                               w_align.to_broadcast([P, 2 * D])).then_inc(s_w, 16)
                def load(g, s, u, is_tail):
                    if not first_group(g):
                        wait_alone(sync, s_h, g - 1, s_held)
                    rows_dma(sync, x, x4[s], g, dm, is_tail, s_x[s])
                over_groups(sync, dm.FULL, load, tail=True)
                sync.wait_ge(s_table, dm.NG)
                for j in range(2):
                    sync.dma_start(a_out[j].rearrange("(b a) o -> b (a o)", b=P), score[j][:, :]).then_inc(s_a, 16)
                sync.wait_ge(s_a, 32)

            @block.vector
            def _(dve):
                for j in range(2):
                    dve.memset(score[j][:, :], 0.0).then_inc(s_zero, 1)
                    dve.wait_ge(s_zero, j + 1)
                dve.wait_ge(s_w, 16)

                def dot(g, s, is_tail):
                    dve.wait_ge(s_h, g + 1)
                    for k, rows in enumerate(tile_rows(dm, is_tail)):
                        for j in range(2):
                            if k >= 2:
                                dve.wait_ge(s_dot, 8 * g + 2 * k + j - 3)
                            dve.scalar_tensor_tensor(out=waste[2 * (k % 2) + j][0:rows, :], in0=h4[s][0:rows, k, :], scalar=1.0,
                                                     in1=wide[0:rows, j, :], op0=ALU.mult, op1=ALU.mult,
                                                     accum_out=dots[s][0:rows, k, j:j + 1]).then_inc(s_dot, 1)
                            if j == 1 and k == len(tile_rows(dm, is_tail)) - 1:
                                dve.wait_ge(s_dot, 8 * g + 2 * k + 2)
                    for k, rows in enumerate(tile_rows(dm, is_tail)):
                        for j in range(2):
                            ins = dve.tensor_copy(score[j][0:rows, bass.ds(T * g + k, 1)], dots[s][0:rows, k, j:j + 1])
                    ins.then_inc(s_table, 1)

                def stats_of(g, s, u, is_tail):
                    dve.wait_ge(s_x[s], 32 * (u + 1))
                    link = Link(dve, s_link, 2 * T * g)
                    norm_stats(dve, link, x4[s], stats, mv[s], s_held)
                    dve.tensor_scalar(rstd[s][:, :], mv[s][:, :, 1], LN_EPS, None, ALU.add).then_inc(s_var, 1)
                    if not first_group(g):
                        dot(g - 1, 1 - s, False)
                    dve.wait_ge(s_rstd, g + 1)
                    dve.scalar_tensor_tensor(out=shift[s][:, :], in0=mv[s][:, :, 0], scalar=-1.0, in1=rstd[s][:, :],
                                             op0=ALU.mult, op1=ALU.mult).then_inc(s_shift, 1)
                over_groups(dve, dm.FULL, stats_of, tail=True)
                dot(dm.NG - 1, (dm.NG - 1) % 2, True)
                dve.wait_ge(s_table, dm.NG)

            @block.gpsimd
            def _(pool):
                def root(g, s, u, is_tail):
                    wait_alone(pool, s_var, g + 1, s_held)
                    pool.tensor_tensor(rstd[s][:, :], rstd[s][:, :], C.minus_half[:, :], ALU.pow).then_inc(s_rstd, 1)
                over_groups(pool, dm.FULL, root, tail=True)

            @block.scalar
            def _(act):
                def apply(g, s, u, is_tail):
                    act.wait_ge(s_shift, g + 1)
                    act.wait_ge(s_st[s], 32 * u)
                    if not first_group(g):
                        act.wait_ge(s_table, g - 1)
                    for k in range(T):
                        ins = act.activation(h4[s][:, k, :], x4[s][:, k, :], ACT.Relu,
                                             bias=shift[s][:, k:k + 1], scale=rstd[s][:, k:k + 1])
                    ins.then_inc(s_h, 1)
                    act.wait_ge(s_h, g + 1)
                    rows_dma(act, h_out, h4[s], g, dm, is_tail, s_st[s], store=True)
                over_groups(act, dm.FULL, apply, tail=True)
                for s in range(2):
                    act.wait_ge(s_st[s], 32 * uses(dm.NG, s))



def weights_phase(nc, dm, C, edges, a_nodes, params, e_dram):
    ET, AC = dm.ET, dm.AC
    b_align, g_a, b_a, m_a, v_a = params
    with ExitStack() as ctx:
        sp = Space(nc, ctx, "att")
        s_held = sp.sem("held")
        ends = sp.sb("ends", [P, ET, 2])
        whole = sp.sb("whole", [P, ET], I32)
        part = sp.sb("part", [P, ET], I32)
        hi, lo = sp.sb("hi", [P, ET]), sp.sb("lo", [P, ET])
        node = sp.sb("node", [P, ET, 2], I32)
        index = [sp.sb(f"index{s}", [P, T, 2], I32) for s in range(2)]
        got = [sp.sb(f"got{s}", [P, T, 2]) for s in range(2)]
        score = sp.sb("score", [P, ET])
        par = sp.sb("par", [P, 5])
        sc = sp.sb("sc", [P, 4])
        keyb = sp.sb("keyb", [P, ET + 1])
        brk = sp.sb("brk", [P, ET])
        brkn = sp.sb("brkn", [P, ET])
        run = sp.sb("run", [P, ET])
        top = sp.sb("top", [P, ET])
        edge = sp.sb("edge", [P, 4])
        row = sp.sb("row", [1, 8, P])
        lead = sp.sb("lead", [P, 2])
        e_tab = sp.sb("e_tab", [P, ET])
        rows = sp.sb("rows", [dm.TH, 2, P])
        pr = sp.ps("pr", [P, 4, P])
        pc = sp.ps("pc", [P, 2])
        pe_cols = sp.ps("pe_cols", [P, 2, dm.TH])
        s_load, s_link, s_node, s_pool, s_par = sp.sem("load"), sp.sem("link"), sp.sem("node"), sp.sem("pool"), sp.sem("par")
        s_ix, s_got = sp.sems("ix"), sp.sems("got")
        s_sum, s_edge, s_row, s_lead, s_col, s_top, s_e, s_est, s_erow, s_turn = (sp.sem(n) for n in (
            "sum", "edge", "row", "lead", "col", "top", "e", "est", "erow", "turn"))
        s_prev = sp.sem("prev")
        with nc.Block() as block:
            @block.sync
            def _(sync):
                srt = edges.sorted.rearrange("(p f) c -> p f c", p=P)
                sync.dma_start(ends[:, :, :], srt).then_inc(s_load, 16)
                for j, v in enumerate((b_align, g_a, b_a, m_a, v_a)):
                    sync.dma_start(par[:, j:j + 1], v.rearrange("(a b) -> a b", a=1).to_broadcast([P, 1])).then_inc(s_par, 16)
                sync.wait_ge(s_e, 1)
                sync.dma_start(e_dram.rearrange("(p f) -> p f", p=P), e_tab[:, :]).then_inc(s_est, 16)
                sync.wait_ge(s_est, 16)
                sync.dma_start(rows[:, :, :], e_dram.rearrange("(h p j) -> p h j", p=dm.TH, j=P)).then_inc(s_erow, 16)
                sync.wait_ge(s_erow, 16)

            @block.gpsimd
            def _(pool):
                pool.wait_ge(s_node, 2)
                def fetch(g, s, u, is_tail):
                    if not first_group(g):
                        wait_alone(pool, s_sum, g - 1, s_held)
                    pool.tensor_copy(index[s][:, :, :], node[:, bass.ds(T * g, T), :]).then_inc(s_ix[s], 1)
                    wait_alone(pool, s_ix[s], u + 1, s_held)
                    for k in range(T):
                        for j in range(2):
                            pool.indirect_dma_start(got[s][:, k, j:j + 1], None, a_nodes[j],
                                                    bass.IndirectOffsetOnAxis(ap=index[s][:, k, j:j + 1], axis=0)).then_inc(s_got[s], 16)
                over_groups(pool, dm.EG, fetch)
                pool.wait_ge(s_pool, 1)
                pool.tensor_tensor(sc[:, 1:2], sc[:, 0:1], C.minus_half[:, 0:1], ALU.pow).then_inc(s_pool, 1)

            @block.vector
            def _(dve):
                link = Link(dve, s_link)
                dve.wait_ge(s_load, 16)
                for j in range(2):
                    link(dve.tensor_copy(whole[:, :], ends[:, :, j]))
                    link(dve.tensor_scalar(part[:, :], whole[:, :], 7, None, ALU.arith_shift_right))
                    link(dve.tensor_copy(hi[:, :], part[:, :]))
                    link(dve.tensor_scalar(part[:, :], whole[:, :], P - 1, None, ALU.bitwise_and))
                    link(dve.tensor_copy(lo[:, :], part[:, :]))
                    dve.scalar_tensor_tensor(out=node[:, :, j], in0=lo[:, :], scalar=float(AC), in1=hi[:, :],
                                             op0=ALU.mult, op1=ALU.add).then_inc(s_node, 1)
                dve.wait_ge(s_par, 80)
                dve.tensor_scalar(sc[:, 0:1], par[:, 4:5], BN_A_EPS, None, ALU.add).then_inc(s_pool, 1)
                def add(g, s, u, is_tail):
                    dve.wait_ge(s_got[s], 16 * 2 * T * (u + 1))
                    dve.tensor_tensor(score[:, bass.ds(T * g, T)], got[s][:, :, 0], got[s][:, :, 1], ALU.add).then_inc(s_sum, 1)
                over_groups(dve, dm.EG, add)
                dve.wait_ge(s_sum, dm.EG)
                dve.wait_ge(s_pool, 2)
                link(dve.tensor_tensor(sc[:, 1:2], sc[:, 1:2], par[:, 1:2], ALU.mult))
                link(dve.tensor_tensor(sc[:, 2:3], par[:, 0:1], par[:, 3:4], ALU.subtract))
                link(dve.tensor_scalar(score[:, :], score[:, :], sc[:, 2:3], None, ALU.add))
                link(dve.tensor_scalar(score[:, :], score[:, :], sc[:, 1:2], par[:, 2:3], ALU.mult, ALU.add))
                link(dve.scalar_tensor_tensor(out=score[:, :], in0=score[:, :], scalar=0.01, in1=score[:, :],
                                              op0=ALU.mult, op1=ALU.max))
                link(dve.tensor_copy(keyb[:, 1:ET + 1], ends[:, :, 0]))
                link(dve.memset(edge[:, 0:4], -1.0))
                dve.tensor_copy(edge[:, 0:1], keyb[:, ET:ET + 1]).then_inc(s_edge, 1)
                dve.tensor_copy(edge[:, 1:2], keyb[:, 1:2]).then_inc(s_edge, 1)
                dve.wait_ge(s_row, 2)
                link(dve.memset(row[:, :, :], -1.0))
                link(dve.tensor_copy(row[0:1, 0, 1:P], pr[0:1, 0, 0:P - 1]))
                link(dve.tensor_copy(row[0:1, 1, 0:P - 1], pr[0:1, 1, 1:P]))
                dve.memset(row[0:1, 2, 0:1], 1.0).then_inc(s_lead, 1)
                dve.wait_ge(s_col, 2)
                link(dve.tensor_copy(keyb[:, 0:1], pc[:, 0:1]))
                link(dve.tensor_copy(lead[:, 0:1], pc[:, 1:2]))
                link(dve.tensor_tensor(brk[:, :], keyb[:, 0:ET], keyb[:, 1:ET + 1], ALU.not_equal))
                link(dve.tensor_copy(brkn[:, 0:ET - 1], brk[:, 1:ET]))
                link(dve.tensor_tensor(brkn[:, ET - 1:ET], keyb[:, ET:ET + 1], lead[:, 0:1], ALU.not_equal))
                for b in (brk, brkn):
                    link(dve.tensor_scalar(b[:, :], b[:, :], BELOW_ALL, None, ALU.mult))

                def carried(src_tab, brk_tab, out_tab, flip, edge_at, row_at, n):
                    view = (lambda a: a[:, ::-1]) if flip else (lambda a: a[:, :])
                    last = slice(0, 1) if flip else slice(ET - 1, ET)
                    link(dve.tensor_tensor_scan(view(out_tab), view(brk_tab), view(src_tab), BELOW_ALL, ALU.add, ALU.max))
                    dve.tensor_copy(edge[:, 2:3], out_tab[:, last]).then_inc(s_edge, 1)
                    link(dve.tensor_reduce(edge[:, 3:4], brk_tab[:, :], mybir.AxisListType.X, ALU.add))
                    dve.tensor_copy(edge[:, 1:2], edge[:, 3:4]).then_inc(s_edge, 1)
                    dve.wait_ge(s_row, 2 * n + 2)
                    link(dve.tensor_copy(row[0:1, 3, :], pr[0:1, 2, :]))
                    link(dve.tensor_copy(row[0:1, 4, :], pr[0:1, 3, :]))
                    rv = (lambda a: a[:, ::-1]) if flip else (lambda a: a)
                    link(dve.tensor_tensor_scan(rv(row[0:1, 5, :]), rv(row[0:1, 4, :]), rv(row[0:1, 3, :]), BELOW_ALL,
                                                ALU.add, ALU.max))
                    link(dve.memset(row[0:1, 6, :], BELOW_ALL))
                    if flip:
                        ins = dve.tensor_copy(row[0:1, 6, 0:P - 1], row[0:1, 5, 1:P])
                    else:
                        ins = dve.tensor_copy(row[0:1, 6, 1:P], row[0:1, 5, 0:P - 1])
                    ins.then_inc(s_lead, 1)
                    dve.wait_ge(s_col, 2 + n)
                    link(dve.tensor_copy(lead[:, 1:2], pc[:, 0:1]))
                    link(dve.tensor_tensor_scan(view(out_tab), view(brk_tab), view(src_tab), lead[:, 1:2], ALU.add, ALU.max))

                carried(score, brk, run, False, 2, 3, 1)
                carried(run, brkn, top, True, 2, 3, 2)
                dve.tensor_tensor(score[:, :], score[:, :], top[:, :], ALU.subtract).then_inc(s_top, 1)
                dve.wait_ge(s_turn, 2)
                link(dve.tensor_copy(edges.weightT[:, :].rearrange("p (h t) -> p h t", h=2), pe_cols[:, :, :]))

            @block.tensor
            def _(pe):
                pe.wait_ge(s_edge, 2)
                for j in range(2):
                    pe.matmul(pr[0:1, j, :], edge[:, j:j + 1], C.ident[:, :], start=True, stop=True).then_inc(s_row, 1)
                pe.wait_ge(s_lead, 1)
                for j in range(2):
                    pe.matmul(pc[:, j:j + 1], row[0:1, j, :], row[0:1, 2, 0:1], start=True, stop=True).then_inc(s_col, 1)
                for n in (1, 2):
                    pe.wait_ge(s_edge, 2 * n + 2)
                    pe.matmul(pr[0:1, 2, :], edge[:, 2:3], C.ident[:, :], start=True, stop=True).then_inc(s_row, 1)
                    pe.matmul(pr[0:1, 3, :], edge[:, 1:2], C.ident[:, :], start=True, stop=True).then_inc(s_row, 1)
                    pe.wait_ge(s_lead, n + 1)
                    pe.matmul(pc[:, 0:1], row[0:1, 6, :], row[0:1, 2, 0:1], start=True, stop=True).then_inc(s_col, 1)
                pe.wait_ge(s_erow, 16)
                for h in range(2):
                    pe.transpose(pe_cols[:, h, :], rows[:, h, :], C.ident[0:dm.TH, 0:dm.TH]).then_inc(s_turn, 1)

            @block.scalar
            def _(act):
                act.wait_ge(s_top, 1)
                act.activation(e_tab[:, :], score[:, :], ACT.Exp).then_inc(s_e, 1)



def segment_phase(nc, dm, C, edges, rows_in, raw, tag, weighted):
    W = D + 1 if weighted else D
    TH = dm.TH
    with ExitStack() as ctx:
        sp = Space(nc, ctx, tag)
        s_held = sp.sem("held")
        index = [sp.sb(f"index{s}", [P, T], I32) for s in range(2)]
        keys = [sp.sb(f"keys{s}", [P, T]) for s in range(2)]
        wts = [sp.sb(f"wts{s}", [P, T]) for s in range(2)]
        msg = [sp.sb(f"msg{s}", [P, T, W]) for s in range(2)]
        same = [sp.sb(f"same{s}", [P, T, P]) for s in range(2)]
        out = [sp.sb(f"out{s}", [P, T, W]) for s in range(2)]
        tails = sp.sb("tails", [TH, 2, W])
        heads = sp.sb("heads", [TH, 2, W])
        keyrow = [sp.ps(f"keyrow{s}", [P, T, P]) for s in range(2)]
        total = [sp.ps(f"total{k}", [P, 512]) for k in range(T)]
        s_free = sp.sem("free")
        s_ix, s_msg, s_st = sp.sems("ix"), sp.sems("msg"), sp.sems("st")
        s_one, s_row, s_same, s_tot, s_out = sp.sem("one"), sp.sem("row"), sp.sem("same"), sp.sem("tot"), sp.sem("out")
        s_tail, s_head, s_carry, s_add, s_back = sp.sem("tail"), sp.sem("head"), sp.sem("carry"), sp.sem("add"), sp.sem("back")
        with nc.Block() as block:
            @block.gpsimd
            def _(pool):
                if weighted:
                    for s in range(2):
                        for k in range(T):
                            pool.memset(msg[s][:, k, D:W], 1.0).then_inc(s_one, 1)
                def fetch(g, s, u, is_tail):
                    if not first_group(g):
                        wait_alone(pool, s_out, T * (g - 1), s_held)
                    pool.tensor_copy(index[s][:, :], edges.otherT[:, bass.ds(T * g, T)]).then_inc(s_ix[s], 1)
                    pool.tensor_copy(keys[s][:, :], edges.keyT[:, bass.ds(T * g, T)]).then_inc(s_ix[s], 1)
                    n = 2
                    if weighted:
                        pool.tensor_copy(wts[s][:, :], edges.weightT[:, bass.ds(T * g, T)]).then_inc(s_ix[s], 1)
                        n = 3
                    wait_alone(pool, s_ix[s], n * u + n, s_held)
                    for k in range(T):
                        pool.indirect_dma_start(msg[s][:, k, 0:D], None, rows_in,
                                                bass.IndirectOffsetOnAxis(ap=index[s][:, k:k + 1], axis=0)
                                                ).then_inc(s_msg[s], 16)
                over_groups(pool, dm.EG, fetch)
                for s in range(2):
                    pool.wait_ge(s_st[s], 16 * uses(dm.EG, s))
                for h in range(2):
                    pool.indirect_dma_start(heads[:, h, :], None, raw,
                                            bass.IndirectOffsetOnAxis(ap=edges.first_end[0:TH, h:h + 1], axis=0)
                                            ).then_inc(s_head, 16)
                pool.wait_ge(s_tail, 16)
                pool.wait_ge(s_add, 2)
                for h in range(2):
                    pool.indirect_dma_start(raw, bass.IndirectOffsetOnAxis(ap=edges.first_end[0:TH, h:h + 1], axis=0),
                                            heads[:, h, :], None).then_inc(s_back, 16)
                pool.wait_ge(s_back, 32)

            @block.tensor
            def _(pe):
                n_ix = 3 if weighted else 2
                if weighted:
                    pe.wait_ge(s_one, 2 * T)
                def sums(g, s, u, is_tail):
                    pe.wait_ge(s_ix[s], n_ix * (u + 1))
                    if not first_group(g):
                        pe.wait_ge(s_same, T * (g - 1))
                    for k in range(T):
                        ins = pe.matmul(keyrow[s][:, k, :], keys[s][:, k:k + 1].to_broadcast([P, P]), C.ident[:, :],
                                        start=True, stop=True)
                    ins.then_inc(s_row, 1)
                    pe.wait_ge(s_msg[s], 16 * T * (u + 1))
                    for k in range(T):
                        pe.wait_ge(s_same, T * g + k + 1)
                        if not first_group(g):
                            pe.wait_ge(s_out, T * g + k - T + 1)
                        pe.matmul(total[k][:, 0:W], same[s][:, k, :], msg[s][:, k, :], start=True, stop=True).then_inc(s_tot, 1)
                over_groups(pe, dm.EG, sums)
                pe.wait_ge(s_tail, 16)
                pe.wait_ge(s_out, dm.ET)
                for h in range(2):
                    for h1 in range(h + 1):
                        ins = pe.matmul(total[h][0:TH, 0:W], edges.joins[0:TH, h1, h, :], tails[:, h1, :],
                                        start=h1 == 0, stop=h1 == h)
                    ins.then_inc(s_carry, 1)

            @block.vector
            def _(dve):
                def masks(g, s, u, is_tail):
                    dve.wait_ge(s_row, g + 1)
                    if not first_group(g):
                        dve.wait_ge(s_tot, T * (g - 1))
                    for k in range(T):
                        dve.tensor_scalar(same[s][:, k, :], keyrow[s][:, k, :], keys[s][:, k:k + 1],
                                          wts[s][:, k:k + 1] if weighted else None, ALU.is_equal,
                                          *([ALU.mult] if weighted else [])).then_inc(s_same, 1)
                over_groups(dve, dm.EG, masks)
                dve.wait_ge(s_head, 32)
                dve.wait_ge(s_carry, 2)
                for h in range(2):
                    dve.tensor_tensor(heads[:, h, :], heads[:, h, :], total[h][0:TH, 0:W], ALU.add).then_inc(s_add, 1)

            @block.scalar
            def _(act):
                def evacuate(g, s, u, is_tail):
                    act.wait_ge(s_st[s], 16 * u)
                    for k in range(T):
                        act.wait_ge(s_tot, T * g + k + 1)
                        act.copy(out[s][:, k, :], total[k][:, 0:W]).then_inc(s_out, 1)
                over_groups(act, dm.EG, evacuate)

            @block.sync
            def _(sync):
                def store(g, s, u, is_tail):
                    wait_alone(sync, s_out, T * g + T, s_held)
                    sync.dma_start(raw[bass.ds(g * ROWS, ROWS), :].rearrange("(k p) c -> p k c", p=P),
                                   out[s][:, :, :]).then_inc(s_st[s], 16)
                over_groups(sync, dm.EG, store)
                for s in range(2):
                    sync.wait_ge(s_st[s], 16 * uses(dm.EG, s))
                sync.dma_start(tails[:, :, :], raw.rearrange("(h p j) c -> p h j c", p=TH, j=P)[:, :, P - 1, :]).then_inc(s_tail, 16)
                sync.wait_ge(s_tail, 16)


def flipped_weights(nc, dm, C, jobs, tag):
    with ExitStack() as ctx:
        sp = Space(nc, ctx, tag)
        s_held = sp.sem("held")
        raw = [sp.sb(f"raw{j}", [P, w.shape[0] // P, D]) for j, (w, _, _) in enumerate(jobs)]
        ps = [sp.ps(f"ps{j}", [P, P]) for j in range(2)]
        s_load, s_turn, s_out = sp.sem("load"), sp.sem("turn"), sp.sem("out")
        blocks = [(j, o, c) for j, (w, _, _) in enumerate(jobs) for o in range(w.shape[0] // P) for c in range(KC)]
        with nc.Block() as block:
            @block.sync
            def _(sync):
                for j, (w, _, _) in enumerate(jobs):
                    sync.dma_start(raw[j][:, :, :], w.rearrange("(o p) c -> p o c", p=P)).then_inc(s_load, 16)
                sync.wait_ge(s_load, 16 * len(jobs))

            @block.tensor
            def _(pe):
                pe.wait_ge(s_load, 16 * len(jobs))
                for n, (j, o, c) in enumerate(blocks):
                    if n >= 2:
                        pe.wait_ge(s_out, n - 1)
                    pe.transpose(ps[n % 2][:, :], raw[j][:, o, c * P:(c + 1) * P], C.ident[:, :]).then_inc(s_turn, 1)

            @block.vector
            def _(dve):
                for n, (j, o, c) in enumerate(blocks):
                    target, factors = jobs[j][1][:, c, o * P:(o + 1) * P], jobs[j][2]
                    dve.wait_ge(s_turn, n + 1)
                    if factors is None:
                        dve.tensor_copy(target, ps[n % 2][:, :]).then_inc(s_out, 1)
                    else:
                        dve.tensor_tensor(target, ps[n % 2][:, :], factors[:, o * P:(o + 1) * P], ALU.mult).then_inc(s_out, 1)
                dve.wait_ge(s_out, len(blocks))


def attention_norm_phase(nc, dm, C, b_att, g, b, m, v, factor, offset):
    with ExitStack() as ctx:
        sp = Space(nc, ctx, "atn")
        s_held = sp.sem("held")
        par = sp.sb("par", [P, 5, D])
        s_par, s_var, s_root, s_link = sp.sem("par"), sp.sem("var"), sp.sem("root"), sp.sem("link")
        with nc.Block() as block:
            @block.sync
            def _(sync):
                for j, t in enumerate((b_att, g, b, m, v)):
                    sync.dma_start(par[:, j, :], t.rearrange("(a c) -> a c", a=1).to_broadcast([P, D])).then_inc(s_par, 16)
                sync.wait_ge(s_par, 80)

            @block.gpsimd
            def _(pool):
                pool.wait_ge(s_var, 1)
                pool.tensor_tensor(par[:, 4, :], par[:, 4, :], C.minus_half[:, 0:1].to_broadcast([P, D]), ALU.pow).then_inc(s_root, 1)

            @block.vector
            def _(dve):
                link = Link(dve, s_link)
                dve.wait_ge(s_par, 80)
                dve.tensor_scalar(par[:, 4, :], par[:, 4, :], BN_A_EPS, None, ALU.add).then_inc(s_var, 1)
                dve.wait_ge(s_root, 1)
                link(dve.tensor_tensor(factor[:, :], par[:, 4, :], par[:, 1, :], ALU.mult))
                link(dve.tensor_tensor(par[:, 0, :], par[:, 0, :], par[:, 3, :], ALU.subtract))
                link(dve.tensor_tensor(par[:, 0, :], par[:, 0, :], factor[:, :], ALU.mult))
                link(dve.tensor_tensor(offset[:, :], par[:, 0, :], par[:, 2, :], ALU.add))


def turn_rows(pe, C, src, c, bank, done):
    for k in range(T):
        ins = pe.transpose(bank[:, k * P:(k + 1) * P], src[:, k, c * P:(c + 1) * P], C.ident[:, :])
    ins.then_inc(done, 1)


def context_phase(nc, dm, C, raw, w_att, offset, ctx_dram):
    with ExitStack() as ctx:
        sp = Space(nc, ctx, "ctx")
        s_held = sp.sem("held")
        raw4 = [sp.sb(f"raw{s}", [P, T, D + 1]) for s in range(2)]
        inv = sp.sb("inv", [P, T])
        share = [sp.sb(f"share{s}", [P, T]) for s in range(2)]
        mean = [sp.sb(f"mean{s}", [P, T, D]) for s in range(2)]
        meanT = [sp.sb(f"meanT{s}", [P, KC, ROWS]) for s in range(2)]
        lin = [sp.sb(f"lin{s}", [P, T, D]) for s in range(2)]
        low = [sp.sb(f"low{s}", [P, T, D]) for s in range(2)]
        out = [sp.sb(f"out{s}", [P, T, D]) for s in range(2)]
        turn = [sp.ps(f"turn{c}", [P, ROWS]) for c in range(KC)]
        prod = [sp.ps(f"prod{j}", [P, 2, D]) for j in range(T // 2)]
        s_raw, s_st = sp.sems("raw"), sp.sems("st")
        s_share, s_link, s_mean, s_turn, s_meanT, s_prod, s_lin, s_low, s_exp, s_out = (sp.sem(n) for n in (
            "share", "link", "mean", "turn", "meanT", "prod", "lin", "low", "exp", "out"))
        with nc.Block() as block:
            @block.sync
            def _(sync):
                def load(g, s, u, is_tail):
                    if not first_group(g):
                        wait_alone(sync, s_mean, T * (g - 1), s_held)
                        wait_alone(sync, s_share, g - 1, s_held)
                    sync.dma_start(raw4[s][:, :, :], raw[bass.ds(g * ROWS, ROWS), :]
                                   .rearrange("(k p) c -> p k c", p=P)).then_inc(s_raw[s], 16)
                over_groups(sync, dm.EG, load)

            @block.vector
            def _(dve):
                def finish(g, s, u):
                    dve.wait_ge(s_exp, g + 1)
                    dve.wait_ge(s_st[s], 16 * u)
                    dve.scalar_tensor_tensor(out=out[s][:, :, :], in0=low[s][:, :, :], scalar=-1.0, in1=lin[s][:, :, :],
                                             op0=ALU.add, op1=ALU.max).then_inc(s_out, 1)

                def average(g, s, u):
                    link = Link(dve, s_link, 2 * g)
                    dve.wait_ge(s_raw[s], 16 * (u + 1))
                    link(dve.tensor_scalar(inv[:, :], raw4[s][:, :, D], 1e-8, None, ALU.add))
                    link(dve.reciprocal(inv[:, :], inv[:, :]))
                    if not first_group(g):
                        dve.wait_ge(s_turn, KC * (g - 1))
                    for k in range(T):
                        dve.tensor_scalar(mean[s][:, k, :], raw4[s][:, k, 0:D], inv[:, k:k + 1], None,
                                          ALU.mult).then_inc(s_mean, 1)
                    dve.tensor_tensor(share[s][:, :], raw4[s][:, :, D], inv[:, :], ALU.mult).then_inc(s_share, 1)
                    dve.wait_ge(s_share, g + 1)

                def linear(g, s):
                    for j in range(T // 2):
                        dve.wait_ge(s_prod, T // 2 * g + j + 1)
                        for k in (2 * j, 2 * j + 1):
                            dve.scalar_tensor_tensor(out=lin[s][:, k, :], in0=offset[:, :], scalar=share[s][:, k:k + 1],
                                                     in1=prod[j][:, k - 2 * j, :], op0=ALU.mult, op1=ALU.add).then_inc(s_lin, 1)
                    dve.wait_ge(s_lin, T * g + T)
                    dve.tensor_scalar(low[s][:, :, :], lin[s][:, :, :], 0.0, None, ALU.min).then_inc(s_low, 1)

                def step(g, s, u, is_tail):
                    average(g, s, u)
                    if not (isinstance(g, int) and g < 2):
                        finish(g - 2, s, u - 1)
                        dve.wait_ge(s_out, g - 1)
                    if not first_group(g):
                        linear(g - 1, 1 - s)
                over_groups(dve, dm.EG, step)
                last = dm.EG - 1
                finish(last - 1, (last - 1) % 2, (last - 1) // 2)
                linear(last, last % 2)
                finish(last, last % 2, last // 2)

            @block.tensor
            def _(pe):
                def products(g, s):
                    pe.wait_ge(s_meanT, KC * g + KC)
                    for j in range(T // 2):
                        if not first_group(g):
                            pe.wait_ge(s_lin, T * (g - 1) + 2 * j + 2)
                        for k in (2 * j, 2 * j + 1):
                            for c in range(KC):
                                ins = pe.matmul(prod[j][:, k - 2 * j, :], meanT[s][:, c, k * P:(k + 1) * P],
                                                w_att[:, c, :], start=c == 0, stop=c == KC - 1)
                        ins.then_inc(s_prod, 1)

                def step(g, s, u, is_tail):
                    pe.wait_ge(s_mean, T * g + T)
                    for c in range(KC):
                        if not first_group(g):
                            pe.wait_ge(s_meanT, KC * (g - 1) + c + 1)
                        turn_rows(pe, C, mean[s], c, turn[c], s_turn)
                    if not first_group(g):
                        products(g - 1, 1 - s)
                over_groups(pe, dm.EG, step)
                products(dm.EG - 1, (dm.EG - 1) % 2)

            @block.scalar
            def _(act):
                def exps(g, s):
                    act.wait_ge(s_low, g + 1)
                    act.activation(low[s][:, :, :], low[s][:, :, :], ACT.Exp).then_inc(s_exp, 1)

                def step(g, s, u, is_tail):
                    for c in range(KC):
                        act.wait_ge(s_turn, KC * g + c + 1)
                        if not (isinstance(g, int) and g < 2):
                            act.wait_ge(s_prod, T // 2 * (g - 1))
                        act.copy(meanT[s][:, c, :], turn[c][:, :]).then_inc(s_meanT, 1)
                    if not first_group(g):
                        exps(g - 1, 1 - s)
                over_groups(act, dm.EG, step)
                exps(dm.EG - 1, (dm.EG - 1) % 2)

            @block.gpsimd
            def _(pool):
                def store(g, s, u, is_tail):
                    wait_alone(pool, s_out, g + 1, s_held)
                    pool.dma_start(ctx_dram[bass.ds(g * ROWS, ROWS), :].rearrange("(k p) c -> p k c", p=P),
                                   out[s][:, :, :]).then_inc(s_st[s], 16)
                over_groups(pool, dm.EG, store)
                for s in range(2):
                    pool.wait_ge(s_st[s], 16 * uses(dm.EG, s))



def gather_rows(pool, dm, edges, rows_in, node4, at, g, s, u, s_zero, s_copy, s_rows, s_held):
    pool.memset(node4[s][:, :, :], 0.0).then_inc(s_zero[s], 1)
    pool.tensor_copy(at[s][:, :], edges.last[:, bass.ds(T * g, T)]).then_inc(s_copy[s], 1)
    wait_alone(pool, s_zero[s], u + 1, s_held)
    wait_alone(pool, s_copy[s], u + 1, s_held)
    for k in range(T):
        pool.indirect_dma_start(node4[s][:, k, :], None, rows_in,
                                bass.IndirectOffsetOnAxis(ap=at[s][:, k:k + 1], axis=0),
                                bounds_check=dm.EPAD - 1, oob_is_err=False).then_inc(s_rows[s], 16)



def gru_phase(nc, dm, C, edges, x, h, ctx_dram, w_ih, w_hh, b_ih, b_hh, x1, h1, sums):
    NG = dm.NG
    with ExitStack() as ctx:
        sp = Space(nc, ctx, "gru")
        s_held = sp.sem("held")
        h4, x4, c4, y4, g4 = ([sp.sb(f"{n}{s}", [P, T, D]) for s in range(2)] for n in ("h", "x", "c", "y", "g"))
        at = [sp.sb(f"at{s}", [P, T], I32) for s in range(2)]
        hT, cT, upd = ([sp.sb(f"{n}{s}", [P, KC, ROWS]) for s in range(2)] for n in ("hT", "cT", "upd"))
        tr, tz, hn, pre, new = ([sp.sb(f"{n}{c}", [P, ROWS]) for c in range(KC)] for n in ("tr", "tz", "hn", "pre", "new"))
        sq = sp.sb("sq", [P, T, D])
        acc = sp.sb("acc", [P, 2, T, D])
        stats, mv = sp.sb("stats", [P, T, 6]), sp.sb("mv", [P, T, 2])
        rstd = [sp.sb(f"rstd{s}", [P, T]) for s in range(2)]
        shift = [sp.sb(f"shift{s}", [P, T]) for s in range(2)]
        bias = sp.sb("bias", [P, 2, 6])
        half = sp.sb("half", [P, 6])
        p_r, p_z, p_hn, p_in = (sp.ps(n, [P, ROWS]) for n in ("r", "z", "hn", "in"))
        ring = [sp.ps(f"ring{j}", [P, ROWS]) for j in range(3)]
        sum_ps = sp.ps("sum", [P, 4])
        s_h, s_x, s_zero, s_c, s_at, s_x1, s_h1 = (sp.sems(n) for n in ("h", "x", "zero", "c", "at", "x1", "h1"))
        (s_par, s_bias, s_turn, s_turned, s_back, s_r, s_z, s_hn, s_in, s_tr, s_tz, s_hnb, s_pre, s_new, s_dif,
         s_upd, s_y, s_link, s_var, s_rstd, s_shift, s_g, s_acc, s_sum, s_zeroed) = (sp.sem(n) for n in (
             "par", "bias", "turn", "turned", "back", "r", "z", "hn", "in", "tr", "tz", "hnb", "pre", "new", "dif",
             "upd", "y", "link", "var", "rstd", "shift", "g", "acc", "sum", "zeroed"))
        with nc.Block() as block:
            @block.sync
            def _(sync):
                with nc.allow_non_contiguous_dma(reason="bias vectors by feature"):
                    for j, b in enumerate((b_ih, b_hh)):
                        sync.dma_start(bias[:, j, :], b.rearrange("(j p) -> p j", p=P)).then_inc(s_par, 16)

                def load_x(g, s, is_tail):
                    if not first_group(g):
                        wait_alone(sync, s_y, 2 * (g - 1), s_held)
                    rows_dma(sync, x, x4[s], g, dm, is_tail, s_x[s])

                def load(g, s, u, is_tail):
                    if not first_group(g):
                        wait_alone(sync, s_turn, 4 * (g - 1), s_held)
                    rows_dma(sync, h, h4[s], g, dm, is_tail, s_h[s])
                    if not first_group(g):
                        load_x(g - 1, 1 - s, False)
                over_groups(sync, dm.FULL, load, tail=True)
                load_x(NG - 1, (NG - 1) % 2, True)

            @block.gpsimd
            def _(pool):
                for j in range(2):
                    pool.memset(acc[:, j, :, :], 0.0).then_inc(s_zeroed, 1)
                pool.wait_ge(s_zeroed, 2)

                def fetch(g, s, u):
                    if not first_group(g):
                        wait_alone(pool, s_turn, 4 * (g - 1), s_held)
                    gather_rows(pool, dm, edges, ctx_dram, c4, at, g, s, u, s_zero, s_at, s_c, s_held)

                def after(g, s, is_tail):
                    wait_alone(pool, s_var, g + 1, s_held)
                    pool.tensor_tensor(rstd[s][:, :], rstd[s][:, :], C.minus_half[:, :], ALU.pow).then_inc(s_rstd, 1)
                    wait_alone(pool, s_g, g + 1, s_held)
                    parts = parts_of(dm, is_tail)
                    for a, b, rows in parts:
                        src = g4[s][0:rows, a:b, :]
                        pool.tensor_tensor(sq[0:rows, a:b, :], src, src, ALU.mult).then_inc(s_acc, 1)
                        pool.tensor_tensor(acc[0:rows, 0, a:b, :], acc[0:rows, 0, a:b, :], src, ALU.add).then_inc(s_acc, 1)
                    wait_alone(pool, s_acc, 3 * g + 2 * len(parts), s_held)
                    for a, b, rows in parts:
                        pool.tensor_tensor(acc[0:rows, 1, a:b, :], acc[0:rows, 1, a:b, :], sq[0:rows, a:b, :],
                                           ALU.add).then_inc(s_acc, 1)
                    wait_alone(pool, s_acc, 3 * g + 3 * len(parts), s_held)

                fetch(0, 0, 0)
                def step(g, s, u, is_tail):
                    if not is_tail:
                        fetch(g + 1, 1 - s, u + s)
                    if not first_group(g):
                        after(g - 1, 1 - s, False)
                over_groups(pool, dm.FULL, step, tail=True)
                after(NG - 1, (NG - 1) % 2, True)

            @block.tensor
            def _(pe):
                def gates(g, s, c):
                    def product(bank, j, pairs, free, done):
                        if c or not first_group(g):
                            pe.wait_ge(free, KC * g + c)
                        n = len(pairs) * KC
                        for a, (w, v) in enumerate(pairs):
                            for k in range(KC):
                                ins = pe.matmul(bank[:, :], w[:, k, j * P:(j + 1) * P], v[s][:, k, :],
                                                start=a * KC + k == 0, stop=a * KC + k == n - 1)
                        ins.then_inc(done, 1)
                    product(p_r, c, [(w_hh, hT), (w_ih, cT)], s_tr, s_r)
                    product(p_z, KC + c, [(w_hh, hT), (w_ih, cT)], s_tz, s_z)
                    product(p_hn, 2 * KC + c, [(w_hh, hT)], s_hnb, s_hn)
                    product(p_in, 2 * KC + c, [(w_ih, cT)], s_pre, s_in)

                def turn(g, s, u):
                    early = isinstance(g, int) and g < 2
                    pe.wait_ge(s_h[s], 32 * (u + 1))
                    if not first_group(g):
                        pe.wait_ge(s_turned, 4 * g)
                    turn_rows(pe, C, h4[s], 0, ring[0], s_turn)
                    if not early:
                        pe.wait_ge(s_y, 2 * g - 3)
                    turn_rows(pe, C, h4[s], 1, ring[1], s_turn)
                    pe.wait_ge(s_c[s], 16 * T * (u + 1))
                    if not early:
                        pe.wait_ge(s_y, 2 * g - 2)
                    turn_rows(pe, C, c4[s], 0, ring[2], s_turn)
                    pe.wait_ge(s_turned, 4 * g + 1)
                    turn_rows(pe, C, c4[s], 1, ring[0], s_turn)

                def back(g, s, later):
                    pe.wait_ge(s_upd, KC * g + KC)
                    for j in range(2):
                        if later is not None:
                            pe.wait_ge(s_turned, later + j)
                        else:
                            pe.wait_ge(s_y, 2 * g - 1 + j)
                        for k in (0, 1):
                            for c in range(KC):
                                ins = pe.transpose(ring[1 + j][:, k * D + c * P:k * D + (c + 1) * P],
                                                   upd[s][:, c, (2 * j + k) * P:(2 * j + k + 1) * P], C.ident[:, :])
                        ins.then_inc(s_back, 1)

                turn(0, 0, 0)
                def step(g, s, u, is_tail):
                    pe.wait_ge(s_turned, 4 * g + 4)
                    gates(g, s, 0)
                    if not first_group(g):
                        back(g - 1, 1 - s, 4 * g + 2)
                    if not is_tail:
                        turn(g + 1, 1 - s, u + s)
                    gates(g, s, 1)
                over_groups(pe, dm.FULL, step, tail=True)
                back(NG - 1, (NG - 1) % 2, None)
                pe.wait_ge(s_acc, 3 * NG + 3)
                for j in range(2):
                    for c in range(KC):
                        for t in range(T):
                            ins = pe.matmul(sum_ps[:, 2 * j + c:2 * j + c + 1], acc[:, j, t, c * P:(c + 1) * P],
                                            C.ones[:, 0:1], start=t == 0, stop=t == T - 1)
                        ins.then_inc(s_sum, 1)

            @block.scalar
            def _(act):
                def turned(g, s):
                    if not first_group(g):
                        act.wait_ge(s_in, KC * (g - 1))
                        act.wait_ge(s_dif, KC * (g - 1))
                    for j, (dst, c) in enumerate(((hT, 0), (hT, 1), (cT, 0), (cT, 1))):
                        act.wait_ge(s_turn, 4 * g + j + 1)
                        act.copy(dst[s][:, c, :], ring[j % 3][:, :]).then_inc(s_turned, 1)

                def gates(g, s, c):
                    again = not first_group(g)
                    act.wait_ge(s_r, KC * g + c + 1)
                    if again:
                        act.wait_ge(s_pre, KC * (g - 1) + c + 1)
                    act.activation(tr[c][:, :], p_r[:, :], ACT.Tanh, bias=half[:, c:c + 1], scale=0.5).then_inc(s_tr, 1)
                    act.wait_ge(s_z, KC * g + c + 1)
                    if again:
                        act.wait_ge(s_upd, KC * (g - 1) + c + 1)
                    act.activation(tz[c][:, :], p_z[:, :], ACT.Tanh, bias=half[:, KC + c:KC + c + 1], scale=0.5).then_inc(s_tz, 1)
                    act.wait_ge(s_hn, KC * g + c + 1)
                    act.activation(hn[c][:, :], p_hn[:, :], ACT.Identity, bias=half[:, 2 * KC + c:2 * KC + c + 1],
                                   scale=0.5).then_inc(s_hnb, 1)

                def candidate(g, s, c):
                    act.wait_ge(s_pre, KC * g + c + 1)
                    act.activation(new[c][:, :], pre[c][:, :], ACT.Tanh, bias=bias[:, 0, 2 * KC + c:2 * KC + c + 1]).then_inc(s_new, 1)

                def norm(g, s, u, is_tail):
                    act.wait_ge(s_y, 2 * g + 2)
                    rows_dma(act, x1, y4[s], g, dm, is_tail, s_x1[s], store=True)
                    act.wait_ge(s_shift, g + 1)
                    act.wait_ge(s_h1[s], 32 * u)
                    if not first_group(g):
                        act.wait_ge(s_acc, 3 * (g - 1))
                    for k in range(T):
                        ins = act.activation(g4[s][:, k, :], y4[s][:, k, :], ACT.Relu,
                                             bias=shift[s][:, k:k + 1], scale=rstd[s][:, k:k + 1])
                    ins.then_inc(s_g, 1)
                    act.wait_ge(s_g, g + 1)
                    rows_dma(act, h1, g4[s], g, dm, is_tail, s_h1[s], store=True)

                act.wait_ge(s_bias, 2)
                turned(0, 0)
                def step(g, s, u, is_tail):
                    gates(g, s, 0)
                    if not is_tail:
                        turned(g + 1, 1 - s)
                    candidate(g, s, 0)
                    if not first_group(g):
                        norm(g - 1, 1 - s, u - 1 + s, False)
                    gates(g, s, 1)
                    candidate(g, s, 1)
                over_groups(act, dm.FULL, step, tail=True)
                norm(NG - 1, (NG - 1) % 2, (NG - 1) // 2, True)
                for s in range(2):
                    act.wait_ge(s_x1[s], 32 * uses(NG, s))
                    act.wait_ge(s_h1[s], 32 * uses(NG, s))

            @block.vector
            def _(dve):
                LINKS = 2 * KC + 2 * T
                def prepare(g, c, link):
                    dve.wait_ge(s_hnb, KC * g + c + 1)
                    dve.wait_ge(s_tr, KC * g + c + 1)
                    if not first_group(g):
                        dve.wait_ge(s_new, KC * (g - 1) + c + 1)
                    link(dve.scalar_tensor_tensor(out=pre[c][:, :], in0=tr[c][:, :], scalar=1.0, in1=hn[c][:, :],
                                                  op0=ALU.add, op1=ALU.mult))
                    dve.wait_ge(s_in, KC * g + c + 1)
                    dve.tensor_tensor(pre[c][:, :], pre[c][:, :], p_in[:, :], ALU.add).then_inc(s_pre, 1)

                def update(g, s, c, link):
                    dve.wait_ge(s_new, KC * g + c + 1)
                    dve.tensor_tensor(hn[c][:, :], hT[s][:, c, :], new[c][:, :], ALU.subtract).then_inc(s_dif, 1)
                    dve.wait_ge(s_dif, KC * g + c + 1)
                    dve.wait_ge(s_tz, KC * g + c + 1)
                    link(dve.scalar_tensor_tensor(out=hn[c][:, :], in0=tz[c][:, :], scalar=1.0, in1=hn[c][:, :],
                                                  op0=ALU.add, op1=ALU.mult))
                    if not first_group(g):
                        dve.wait_ge(s_back, 2 * (g - 1))
                    dve.scalar_tensor_tensor(out=upd[s][:, c, :], in0=hn[c][:, :], scalar=0.5, in1=new[c][:, :],
                                             op0=ALU.mult, op1=ALU.add).then_inc(s_upd, 1)

                def finish(g, s, u, link):
                    dve.wait_ge(s_x[s], 32 * (u + 1))
                    dve.wait_ge(s_x1[s], 32 * u)
                    if not first_group(g):
                        dve.wait_ge(s_g, g - 1)
                    for j in range(2):
                        dve.wait_ge(s_back, 2 * g + j + 1)
                        dve.tensor_tensor(y4[s][:, 2 * j:2 * j + 2, :], x4[s][:, 2 * j:2 * j + 2, :],
                                          ring[1 + j][:, :].rearrange("p (k c) -> p k c", k=2), ALU.add).then_inc(s_y, 1)
                    dve.wait_ge(s_y, 2 * g + 2)
                    norm_stats(dve, link, y4[s], stats, mv, s_held)
                    dve.tensor_scalar(rstd[s][:, :], mv[:, :, 1], LN_EPS, None, ALU.add).then_inc(s_var, 1)
                    dve.wait_ge(s_rstd, g + 1)
                    dve.scalar_tensor_tensor(out=shift[s][:, :], in0=mv[:, :, 0], scalar=-1.0, in1=rstd[s][:, :],
                                             op0=ALU.mult, op1=ALU.mult).then_inc(s_shift, 1)
                    dve.wait_ge(s_shift, g + 1)

                dve.wait_ge(s_par, 32)
                dve.tensor_tensor(half[:, :], bias[:, 0, :], bias[:, 1, :], ALU.add).then_inc(s_bias, 1)
                dve.wait_ge(s_bias, 1)
                dve.tensor_copy(half[:, 2 * KC:3 * KC], bias[:, 1, 2 * KC:3 * KC]).then_inc(s_link, 1)
                dve.wait_ge(s_link, 1)
                dve.tensor_scalar(half[:, :], half[:, :], 0.5, None, ALU.mult).then_inc(s_bias, 1)

                def step(g, s, u, is_tail):
                    link = Link(dve, s_link, 1 if first_group(g) else 1 + 2 * KC + LINKS * (g - 1))
                    prepare(g, 0, link)
                    if not first_group(g):
                        finish(g - 1, 1 - s, u - 1 + s, link)
                    update(g, s, 0, link)
                    prepare(g, 1, link)
                    update(g, s, 1, link)
                over_groups(dve, dm.FULL, step, tail=True)
                finish(NG - 1, (NG - 1) % 2, (NG - 1) // 2, Link(dve, s_link, 1 + 2 * KC + LINKS * (NG - 1)))
                dve.wait_ge(s_sum, 2 * KC)
                dve.tensor_copy(sums[:, :], sum_ps[:, :])



def first_norm_phase(nc, dm, C, sums, gamma, beta, w, count, coef, lift, deg_dram):
    with ExitStack() as ctx:
        sp = Space(nc, ctx, "bn0")
        s_held = sp.sem("held")
        par = sp.sb("par", [P, 2, KC])
        tmp = sp.sb("tmp", [P, 3, KC])
        TQ = dm.AC // T
        deg = sp.sb("deg", [P, dm.AC])
        degT = sp.sb("degT", [TQ, T, P])
        ps = sp.ps("ps", [P, KC])
        turned = sp.ps("turned", [P, T, P])
        s_par, s_link, s_var, s_root, s_coef, s_lift, s_deg, s_turn, s_degT, s_st = (sp.sem(n) for n in (
            "par", "link", "var", "root", "coef", "lift", "deg", "turn", "degT", "st"))
        with nc.Block() as block:
            @block.sync
            def _(sync):
                with nc.allow_non_contiguous_dma(reason="vectors by feature"):
                    for j, v in enumerate((gamma, beta)):
                        sync.dma_start(par[:, j, :], v.rearrange("(c p) -> p c", p=P)).then_inc(s_par, 16)
                sync.wait_ge(s_par, 32)
                sync.wait_ge(s_degT, 1)
                sync.dma_start(deg_dram.rearrange("(t q p) -> q t p", q=TQ, p=P), degT[:, :, :]).then_inc(s_st, 16)
                sync.wait_ge(s_st, 16)

            @block.vector
            def _(dve):
                link = Link(dve, s_link)
                dve.tensor_scalar(deg[:, :], count[:, :], 1.0, None, ALU.add).then_inc(s_deg, 1)
                dve.wait_ge(s_par, 32)
                link(dve.tensor_scalar(tmp[:, 0:2, :].rearrange("p a c -> p (a c)"), sums[:, :], 1.0 / dm.N, None, ALU.mult))
                link(dve.tensor_tensor(tmp[:, 2, :], tmp[:, 0, :], tmp[:, 0, :], ALU.mult))
                link(dve.tensor_tensor(tmp[:, 1, :], tmp[:, 1, :], tmp[:, 2, :], ALU.subtract))
                dve.tensor_scalar(tmp[:, 1, :], tmp[:, 1, :], 0.0, BN_B_EPS, ALU.max, ALU.add).then_inc(s_var, 1)
                dve.wait_ge(s_root, 1)
                scale_shift(dve, link, tmp[:, 1, :], tmp[:, 0, :], tmp[:, 2, :], par, coef, s_coef)
                dve.wait_ge(s_lift, 1)
                link(dve.tensor_copy(lift[:, :], ps[:, :]))
                dve.wait_ge(s_turn, T)
                dve.tensor_copy(degT[:, :, :], turned[0:TQ, :, :]).then_inc(s_degT, 1)

            @block.gpsimd
            def _(pool):
                pool.wait_ge(s_var, 1)
                pool.tensor_tensor(tmp[:, 1, :], tmp[:, 1, :], C.minus_half[:, 0:KC], ALU.pow).then_inc(s_root, 1)

            @block.tensor
            def _(pe):
                pe.wait_ge(s_deg, 1)
                for t in range(T):
                    pe.transpose(turned[0:TQ, t, :], deg[:, t * TQ:(t + 1) * TQ], C.ident[:, :]).then_inc(s_turn, 1)
                pe.wait_ge(s_coef, 1)
                for o in range(KC):
                    for k in range(KC):
                        ins = pe.matmul(ps[:, o:o + 1], w[:, k, o * P:(o + 1) * P], coef[:, 1, k:k + 1],
                                        start=k == 0, stop=k == KC - 1)
                ins.then_inc(s_lift, 1)


def scale_shift(dve, link, rstd, mean, spare, par, coef, done):
    link(dve.tensor_tensor(coef[:, 0, :], rstd, par[:, 0, :], ALU.mult))
    link(dve.tensor_tensor(spare, mean, coef[:, 0, :], ALU.mult))
    dve.tensor_tensor(coef[:, 1, :], par[:, 1, :], spare, ALU.subtract).then_inc(done, 1)


def gin_in_phase(nc, dm, C, edges, rows_in, raw, w, bias, scale, lift, deg_dram, yT, gamma, beta, coef, tag):
    NG = dm.NG
    with ExitStack() as ctx:
        sp = Space(nc, ctx, tag)
        s_held = sp.sem("held")
        r4, a4, sum4 = ([sp.sb(f"{n}{s}", [P, T, D]) for s in range(2)] for n in ("r", "a", "sum"))
        at = [sp.sb(f"at{s}", [P, T], I32) for s in range(2)]
        deg = [sp.sb(f"deg{s}", [P, ROWS]) for s in range(2)]
        sumT = [sp.sb(f"sumT{s}", [P, KC, ROWS]) for s in range(2)]
        lin = [sp.sb(f"lin{s}", [P, KC, ROWS]) for s in range(2)]
        y = [sp.sb(f"y{s}", [P, KC, ROWS]) for s in range(2)] if lift is not None else lin
        stats = sp.sb("stats", [P, KC, NG, 6])
        stats_now = sp.sb("stats_now", [P, 6])
        mv = sp.sb("mv", [P, KC, 2])
        par = sp.sb("par", [P, 3, KC])
        root = sp.sb("root", [P, 2, KC])
        turn = [sp.ps(f"turn{c}", [P, ROWS]) for c in range(KC)]
        prod = [[sp.ps(f"prod{s}{c}", [P, ROWS]) for c in range(KC)] for s in range(2)]
        s_r, s_zero, s_a, s_at, s_deg, s_y = (sp.sems(n) for n in ("r", "zero", "a", "at", "deg", "y"))
        s_par, s_sum, s_turn, s_turned, s_prod, s_lin, s_lift, s_st, s_mv, s_var, s_root, s_coef, s_link, s_mean = (
            sp.sem(n) for n in ("par", "sum", "turn", "turned", "prod", "lin", "lift", "st", "mv", "var", "root",
                                "coef", "link", "mean"))
        done = s_lift if lift is not None else s_lin
        with nc.Block() as block:
            @block.sync
            def _(sync):
                with nc.allow_non_contiguous_dma(reason="vectors by feature"):
                    for j, v in enumerate((gamma, beta, bias)):
                        sync.dma_start(par[:, j, :], v.rearrange("(c p) -> p c", p=P)).then_inc(s_par, 16)
                sync.wait_ge(s_par, 48)

                def move(g, s, u, is_tail):
                    if not first_group(g):
                        wait_alone(sync, s_sum, g - 1, s_held)
                    rows_dma(sync, rows_in, r4[s], g, dm, is_tail, s_r[s])
                    if lift is not None:
                        if not first_group(g):
                            wait_alone(sync, s_lift, KC * (g - 1), s_held)
                        sync.dma_start(deg[s][:, :], deg_dram[bass.ds(g * ROWS, ROWS)].rearrange("(a n) -> a n", a=1)
                                       .to_broadcast([P, ROWS])).then_inc(s_deg[s], 16)
                over_groups(sync, dm.FULL, move, tail=True)

            @block.gpsimd
            def _(pool):
                def fetch(g, s, u, is_tail):
                    if not first_group(g):
                        wait_alone(pool, s_sum, g - 1, s_held)
                    gather_rows(pool, dm, edges, raw, a4, at, g, s, u, s_zero, s_at, s_a, s_held)
                over_groups(pool, dm.FULL, fetch, tail=True)
                pool.wait_ge(s_var, 1)
                pool.tensor_tensor(root[:, 0, :], root[:, 0, :], C.minus_half[:, 0:KC], ALU.pow).then_inc(s_root, 1)

            @block.tensor
            def _(pe):
                def products(g, s):
                    pe.wait_ge(s_turned, KC * g + KC)
                    for o in range(KC):
                        if not first_group(g):
                            pe.wait_ge(s_lin, KC * (g - 1))
                        for k in range(KC):
                            ins = pe.matmul(prod[s][o][:, :], w[:, k, o * P:(o + 1) * P], sumT[s][:, k, :],
                                            start=k == 0, stop=k == KC - 1)
                        ins.then_inc(s_prod, 1)

                def step(g, s, u, is_tail):
                    pe.wait_ge(s_sum, g + 1)
                    for c in range(KC):
                        if not first_group(g):
                            pe.wait_ge(s_turned, KC * (g - 1) + c + 1)
                        turn_rows(pe, C, sum4[s], c, turn[c], s_turn)
                    if not first_group(g):
                        products(g - 1, 1 - s)
                over_groups(pe, dm.FULL, step, tail=True)
                products(NG - 1, (NG - 1) % 2)

            @block.scalar
            def _(act):
                act.wait_ge(s_par, 48)
                def store(g, s, is_tail):
                    n = dm.N - dm.FULL * ROWS if is_tail else ROWS
                    act.wait_ge(done, KC * g + KC)
                    act.dma_start(yT[:, bass.ds(g * ROWS, n)].rearrange("(c p) n -> p c n", p=P),
                                  y[s][:, :, 0:n]).then_inc(s_y[s], 16)

                def linear(g, s, u):
                    act.wait_ge(s_y[s], 16 * u)
                    for o in range(KC):
                        act.wait_ge(s_prod, KC * g + o + 1)
                        if not first_group(g):
                            act.wait_ge(s_mean, KC * (g - 1))
                        act.activation(lin[s][:, o, :], prod[s][o][:, :], ACT.Identity, bias=par[:, 2, o:o + 1]).then_inc(s_lin, 1)

                def step(g, s, u, is_tail):
                    for c in range(KC):
                        act.wait_ge(s_turn, KC * g + c + 1)
                        if not first_group(g):
                            act.wait_ge(s_prod, KC * (g - 1))
                        if scale is None:
                            act.copy(sumT[s][:, c, :], turn[c][:, :]).then_inc(s_turned, 1)
                        else:
                            act.activation(sumT[s][:, c, :], turn[c][:, :], ACT.Copy, scale=scale[:, 0, c:c + 1]).then_inc(s_turned, 1)
                    if not first_group(g):
                        linear(g - 1, 1 - s, u - 1 + s)
                    if not (isinstance(g, int) and g < 2):
                        store(g - 2, s, False)
                over_groups(act, dm.FULL, step, tail=True)
                linear(NG - 1, (NG - 1) % 2, (NG - 1) // 2)
                store(NG - 2, (NG - 2) % 2, False)
                store(NG - 1, (NG - 1) % 2, True)
                for s in range(2):
                    act.wait_ge(s_y[s], 16 * uses(NG, s))

            @block.vector
            def _(dve):
                def finish(g, s, u, is_tail):
                    n = dm.N - dm.FULL * ROWS if is_tail else ROWS
                    for o in range(KC):
                        dve.wait_ge(s_lin, KC * g + o + 1)
                        if lift is not None:
                            if o == 0:
                                dve.wait_ge(s_deg[s], 16 * (u + 1))
                                dve.wait_ge(s_y[s], 16 * u)
                            dve.scalar_tensor_tensor(out=y[s][:, o, :], in0=deg[s][:, :], scalar=lift[:, o:o + 1],
                                                     in1=lin[s][:, o, :], op0=ALU.mult, op1=ALU.add).then_inc(s_lift, 1)
                            dve.wait_ge(s_lift, KC * g + o + 1)
                        dve.bn_stats(stats_now[:, :], y[s][:, o, 0:n]).then_inc(s_mean, 1)
                        dve.wait_ge(s_mean, KC * g + o + 1)
                        dve.tensor_copy(stats[:, o, bass.ds(g, 1), :].rearrange("p g c -> p (g c)"), stats_now[:, :]).then_inc(s_mv, 1)
                        dve.wait_ge(s_mv, KC * g + o + 1)

                def step(g, s, u, is_tail):
                    dve.wait_ge(s_r[s], 32 * (u + 1))
                    dve.wait_ge(s_a[s], 16 * T * (u + 1))
                    if not first_group(g):
                        dve.wait_ge(s_turn, KC * (g - 1))
                    dve.tensor_tensor(sum4[s][:, :, :], r4[s][:, :, :], a4[s][:, :, :], ALU.add).then_inc(s_sum, 1)
                    if not first_group(g):
                        finish(g - 1, 1 - s, u - 1 + s, False)
                over_groups(dve, dm.FULL, step, tail=True)
                finish(NG - 1, (NG - 1) % 2, (NG - 1) // 2, True)
                link = Link(dve, s_link)
                for o in range(KC):
                    link(dve.bn_aggr(mv[:, o, :], stats[:, o, :, :].rearrange("p g c -> p (g c)")))
                dve.tensor_scalar(root[:, 0, :], mv[:, :, 1], BN_B_EPS, None, ALU.add).then_inc(s_var, 1)
                dve.wait_ge(s_root, 1)
                scale_shift(dve, link, root[:, 0, :], mv[:, :, 0], root[:, 1, :], par, coef, s_coef)
                dve.wait_ge(s_coef, 1)


def gin_out_phase(nc, dm, C, yT, coef, w, bias, x1, out, tag):
    NG = dm.NG
    with ExitStack() as ctx:
        sp = Space(nc, ctx, tag)
        s_held = sp.sem("held")
        yt, aT = ([sp.sb(f"{n}{s}", [P, KC, ROWS]) for s in range(2)] for n in ("yt", "aT"))
        lin, o4 = ([sp.sb(f"{n}{s}", [P, T, D]) for s in range(2)] for n in ("lin", "o"))
        x4 = [sp.sb(f"x{s}", [P, T, D]) for s in range(2)] if x1 is not None else None
        wide = sp.sb("wide", [P, 2, D])
        prod = [[sp.ps(f"prod{s}{j}", [P, 2, D]) for j in range(2)] for s in range(2)]
        s_yt, s_x, s_st = sp.sems("yt"), sp.sems("x"), sp.sems("st")
        s_w, s_aT, s_prod, s_lin, s_o = (sp.sem(n) for n in ("w", "aT", "prod", "lin", "o"))
        with nc.Block() as block:
            @block.sync
            def _(sync):
                for j in range(2):
                    sync.dma_start(wide[:, j, :], bias.rearrange("(a c) -> a c", a=1).to_broadcast([P, D])).then_inc(s_w, 16)

                def move(g, s, u, is_tail):
                    n = dm.N - dm.FULL * ROWS if is_tail else ROWS
                    if not first_group(g):
                        wait_alone(sync, s_aT, KC * (g - 1), s_held)
                    sync.dma_start(yt[s][:, :, 0:n], yT[:, bass.ds(g * ROWS, n)]
                                   .rearrange("(c p) n -> p c n", p=P)).then_inc(s_yt[s], 16)
                    if x1 is not None:
                        if not first_group(g):
                            wait_alone(sync, s_o, g - 1, s_held)
                        rows_dma(sync, x1, x4[s], g, dm, is_tail, s_x[s])
                over_groups(sync, dm.FULL, move, tail=True)

            @block.gpsimd
            def _(pool):
                def store(g, s, u, is_tail):
                    wait_alone(pool, s_o, g + 1, s_held)
                    rows_dma(pool, out, o4[s], g, dm, is_tail, s_st[s], store=True)
                over_groups(pool, dm.FULL, store, tail=True)
                for s in range(2):
                    pool.wait_ge(s_st[s], 32 * uses(NG, s))

            @block.scalar
            def _(act):
                def relu(g, s, u):
                    act.wait_ge(s_lin, 2 * g + 2)
                    act.wait_ge(s_st[s], 32 * u)
                    act.activation(o4[s][:, :, :], lin[s][:, :, :], ACT.Relu).then_inc(s_o, 1)

                def step(g, s, u, is_tail):
                    act.wait_ge(s_yt[s], 16 * (u + 1))
                    if not first_group(g):
                        act.wait_ge(s_prod, 2 * (g - 1))
                    for c in range(KC):
                        act.activation(aT[s][:, c, :], yt[s][:, c, :], ACT.Relu, bias=coef[:, 1, c:c + 1],
                                       scale=coef[:, 0, c:c + 1]).then_inc(s_aT, 1)
                    if x1 is None and not first_group(g):
                        relu(g - 1, 1 - s, u - 1 + s)
                over_groups(act, dm.FULL, step, tail=True)
                if x1 is None:
                    relu(NG - 1, (NG - 1) % 2, (NG - 1) // 2)

            @block.tensor
            def _(pe):
                def step(g, s, u, is_tail):
                    pe.wait_ge(s_aT, KC * g + KC)
                    for j in range(2):
                        if not first_group(g):
                            pe.wait_ge(s_lin, 2 * (g - 1))
                        for k in range(2):
                            for c in range(KC):
                                ins = pe.matmul(prod[s][j][:, k, :], aT[s][:, c, (2 * j + k) * P:(2 * j + k + 1) * P],
                                                w[:, c, :], start=c == 0, stop=c == KC - 1)
                        ins.then_inc(s_prod, 1)
                over_groups(pe, dm.FULL, step, tail=True)

            @block.vector
            def _(dve):
                dve.wait_ge(s_w, 32)
                def step(g, s, u, is_tail):
                    if x1 is None and not first_group(g):
                        dve.wait_ge(s_o, g - 1)
                    for j in range(2):
                        dve.wait_ge(s_prod, 2 * g + j + 1)
                        dve.tensor_tensor(lin[s][:, 2 * j:2 * j + 2, :], prod[s][j][:, :, :], wide[:, :, :],
                                          ALU.add).then_inc(s_lin, 1)
                    if x1 is not None:
                        dve.wait_ge(s_lin, 2 * g + 2)
                        dve.wait_ge(s_x[s], 32 * (u + 1))
                        dve.wait_ge(s_st[s], 32 * u)
                        dve.scalar_tensor_tensor(out=o4[s][:, :, :], in0=lin[s][:, :, :], scalar=0.0,
                                                 in1=x4[s][:, :, :], op0=ALU.max, op1=ALU.add).then_inc(s_o, 1)
                over_groups(dve, dm.FULL, step, tail=True)



class Edges:

    def __init__(self, sp, nc, dm, name):
        self.hi = sp.sb(f"{name}_hi", [P, dm.ET])
        self.lo = sp.sb(f"{name}_lo", [P, dm.ET])
        self.pay = sp.sb(f"{name}_pay", [P, dm.ET, 2])
        self.sorted = nc.dram_tensor(f"{name}_sorted", (dm.EPAD, 2), F32, kind="Internal").ap()
        self.count = sp.sb(f"{name}_count", [P, dm.AC])
        self.last = sp.sb(f"{name}_last", [P, dm.AC], I32)
        self.keyT = sp.sb(f"{name}_keyT", [P, dm.ET])
        self.otherT = sp.sb(f"{name}_otherT", [P, dm.ET], I32)
        self.joins = sp.sb(f"{name}_joins", [P, 2, 2, dm.TH])
        self.first_end = sp.sb(f"{name}_first_end", [P, 2], I32)


class Constants:
    def __init__(self, sp, dm):
        self.ident, self.ident_h = sp.sb("ident", [P, P]), sp.sb("ident_h", [P, P], BF16)
        self.lower, self.upper = sp.sb("lower", [P, P]), sp.sb("upper", [P, P])
        self.iota, self.col = sp.sb("iota", [P, dm.WIDE], F16), sp.sb("col", [P, 1])
        self.minus_half, self.ones = sp.sb("minus_half", [P, T]), sp.sb("ones", [P, T])


def load_weights(nc, jobs, tag):
    with ExitStack() as ctx:
        s_load = Space(nc, ctx, tag).sem("load")
        with nc.Block() as block:
            @block.sync
            def _(sync):
                for w, t in jobs:
                    sync.dma_start(t[:, :, :], w.rearrange("(c p) o -> p c o", p=P)).then_inc(s_load, 16)
                sync.wait_ge(s_load, 16 * len(jobs))


def build(nc, a, out, nodes, edges_n):
    dm = Dims(nodes, edges_n)

    def dram(name, shape):
        return nc.dram_tensor(name, shape, F32, kind="Internal").ap()

    l0 = {k[len("L0_gnn_"):]: v for k, v in a.items() if k.startswith("L0_gnn_")}
    l1 = {k[len("L1_gnn_"):]: v for k, v in a.items() if k.startswith("L1_gnn_")}
    h = dram("h", (dm.N, D))
    x1, h1, z = dram("x1", (dm.N, D)), dram("h1", (dm.N, D)), dram("z", (dm.N, D))
    a_nodes = [dram(f"score{j}", (dm.NPAD, 1)) for j in range(2)]
    e_dram = dram("weights", (dm.EPAD,))
    raw0, raw1 = dram("raw0", (dm.EPAD, D + 1)), dram("raw1", (dm.EPAD, D))
    ctx_dram = dram("context", (dm.EPAD, D))
    deg_dram = dram("degrees", (dm.NPAD,))
    yT = dram("yT", (D, dm.NPAD))

    with ExitStack() as ctx:
        sp = Space(nc, ctx, "all")
        s_held = sp.sem("held")
        C = Constants(sp, dm)
        by_src, by_dst = Edges(sp, nc, dm, "src"), Edges(sp, nc, dm, "dst")
        by_src.weightT = sp.sb("weightT", [P, dm.ET])
        w_att, w_hh, w_ih = sp.sb("w_att", [P, KC, D]), sp.sb("w_hh", [P, KC, 3 * D]), sp.sb("w_ih", [P, KC, 3 * D])
        w1a, w1b, w2a, w2b = (sp.sb(n, [P, KC, D]) for n in ("w1a", "w1b", "w2a", "w2b"))
        factor, offset = sp.sb("factor", [P, D]), sp.sb("offset", [P, D])
        sums, lift = sp.sb("sums", [P, 4]), sp.sb("lift", [P, KC])
        coef = [sp.sb(f"coef{j}", [P, 2, KC]) for j in range(3)]

        constants_phase(nc, dm, C)
        edges_phase(nc, dm, C, a["src"], a["dst"], by_src, by_dst)
        for e, name in ((by_src, "srt0"), (by_dst, "srt1")):
            sort_phase(nc, dm, C, e, name)
            sorted_phase(nc, dm, C, e, name + "t")
        load_weights(nc, [(l1["W1a"], w1a), (l1["W1b"], w1b), (l1["W2a"], w2a), (l1["W2b"], w2b)], "lw")
        attention_norm_phase(nc, dm, C, l0["b_att"], l0["bn_t_g"], l0["bn_t_b"], l0["bn_t_m"], l0["bn_t_v"], factor, offset)
        flipped_weights(nc, dm, C, [(l0["W_att"], w_att, factor), (l0["W_hh"], w_hh, None), (l0["W_ih"], w_ih, None)], "fw")
        norm_phase(nc, dm, C, a["x"], l0["W_align"], h, a_nodes)
        weights_phase(nc, dm, C, by_src, a_nodes,
                      (l0["b_align"], l0["bn_a_g"], l0["bn_a_b"], l0["bn_a_m"], l0["bn_a_v"]), e_dram)
        segment_phase(nc, dm, C, by_src, h, raw0, "sg0", weighted=True)
        context_phase(nc, dm, C, raw0, w_att, offset, ctx_dram)
        gru_phase(nc, dm, C, by_src, a["x"], h, ctx_dram, w_ih, w_hh, l0["b_ih"], l0["b_hh"], x1, h1, sums)
        segment_phase(nc, dm, C, by_dst, h1, raw1, "sg1", weighted=False)
        first_norm_phase(nc, dm, C, sums, l1["g0"], l1["b0"], w1a, by_dst.count, coef[0], lift, deg_dram)
        gin_in_phase(nc, dm, C, by_dst, h1, raw1, w1a, l1["b1a"], coef[0], lift, deg_dram, yT, l1["g1"], l1["bt1"], coef[1], "gi1")
        gin_out_phase(nc, dm, C, yT, coef[1], w1b, l1["b1b"], None, z, "go1")
        segment_phase(nc, dm, C, by_dst, z, raw1, "sg2", weighted=False)
        gin_in_phase(nc, dm, C, by_dst, z, raw1, w2a, l1["b2a"], None, None, None, yT, l1["g2"], l1["bt2"], coef[2], "gi2")
        gin_out_phase(nc, dm, C, yT, coef[2], w2b, l1["b2b"], x1, out, "go2")


NAMES = ["x", "src", "dst"] + ["L0_gnn_" + n for n in (
    "W_align", "b_align", "bn_a_g", "bn_a_b", "bn_a_m", "bn_a_v", "W_att", "b_att", "bn_t_g", "bn_t_b", "bn_t_m",
    "bn_t_v", "W_ih", "W_hh", "b_ih", "b_hh")] + ["L1_gnn_" + n for n in (
        "g0", "b0", "W1a", "b1a", "g1", "bt1", "W1b", "b1b", "W2a", "b2a", "g2", "bt2", "W2b", "b2b")]


def kernel(**inputs):
    import concourse.bacc as bacc
    from concourse.bass_utils import run_bass_kernel_spmd as run

    nc = bacc.Bacc("TRN2", target_bir_lowering=False, num_devices=1)
    arrays, args = {}, {}
    for name in NAMES:
        v = np.ascontiguousarray(inputs[name])
        arrays[f"in_{name}"] = v
        args[name] = nc.dram_tensor(f"in_{name}", v.shape, mybir.dt.from_np(v.dtype), kind="ExternalInput").ap()
    nodes, edges_n = inputs["x"].shape[0], inputs["src"].shape[0]
    out = nc.dram_tensor("out_x", (nodes, D), F32, kind="ExternalOutput").ap()
    build(nc, args, out, nodes, edges_n)
    return run(nc, [arrays], core_ids=[0]).results[0]["out_x"]
```

```python
from contextlib import ExitStack

import concourse.bass as bass
import numpy as np
from concourse import mybir

F32, I32, BF16, F16 = mybir.dt.float32, mybir.dt.int32, mybir.dt.bfloat16, mybir.dt.float16
ALU = mybir.AluOpType
ACT = mybir.ActivationFunctionType
ONE_PASS = mybir.dt.float32r

P = 128
D = 256
KC = D // P
T = 4
ROWS = P * T
LN_EPS = 1e-5
BN_A_EPS = 1e-6
BN_B_EPS = 1e-5
NO_ROW = 1 << 20
BELOW_ALL = -1e30


class Dims:

    def __init__(self, nodes, edges):
        self.N, self.E = nodes, edges
        self.NG = -(-nodes // ROWS)
        self.AC = self.NG * T
        self.NPAD = self.AC * P
        self.WIDE = max(self.AC, P)
        self.FULL = nodes // ROWS
        self.TAIL = [min(P, nodes - r) for r in range(self.FULL * ROWS, nodes, P)]
        self.ET = -(-edges // P)
        self.EG = self.ET // T
        self.EPAD = self.ET * P
        self.TH = self.ET // 2
        assert self.FULL == self.NG - 1 and self.FULL % 2 == 1 and self.TAIL
        assert self.ET % T == 0 and self.EG % 2 == 1 and self.TH <= P and self.AC <= 512


class Scores:

    def __init__(self, sp, nc, dm):
        self.terms = nc.dram_tensor("terms", (2 * dm.NPAD, 1), F32, kind="Internal").ap()
        self.ends = sp.sb("ends", [P, dm.ET, 2])
        self.at = sp.sb("ends_at", [P, dm.ET, 2], I32)
        self.total = sp.sb("score", [P, dm.ET])


class Link:

    def __init__(self, eng, sem, base=0):
        self.eng, self.sem, self.base, self.n = eng, sem, base, 0

    def __call__(self, ins):
        ins.then_inc(self.sem, 1)
        self.n += 1
        self.eng.wait_ge(self.sem, self.base + self.n)


def split_upper(eng, upper, x):
    return eng.tensor_copy(upper, x)


def split_lower(eng, lower, x, upper):
    return eng.tensor_tensor(lower, x, upper.bitcast(F32), ALU.subtract)


def split_products(pe, bank, weights, moving, first, last):
    (wu, wl), (mu, ml) = weights, moving
    for n, (w, m) in enumerate(((wu, mu), (wl, mu), (wu, ml))):
        ins = pe.matmul(bank, w, m, start=first and n == 0, stop=last and n == 2)
    return ins


class Space:

    def __init__(self, nc, ctx, tag):
        self.nc, self.ctx, self.tag, self.own = nc, ctx, tag, []

    def sb(self, name, shape, dt=F32):
        return self.ctx.enter_context(self.nc.sbuf_tensor(f"{self.tag}_{name}", shape, dt))

    def ps(self, name, shape, dt=F32):
        bank = self.ctx.enter_context(self.nc.psum_tensor(f"{self.tag}_{name}", [P, 512 if dt == F32 else 1024], dt))
        view = bank[0:shape[0], 0:int(np.prod(shape[1:]))]
        names = "abc"[:len(shape) - 1]
        return view if len(shape) == 2 else view.rearrange(
            f"p ({' '.join(names)}) -> p {' '.join(names)}", **dict(zip(names, shape[1:])))

    def sem(self, name):
        sem = self.nc.alloc_semaphore(f"{self.tag}_{name}")
        if not self.own:
            self.ctx.callback(self.clear)
        self.own.append(sem)
        return sem

    def clear(self):
        self.nc.clear_and_free_semaphores(self.own)
        self.nc.all_engine_barrier()

    def sems(self, name, n=2):
        return [self.sem(f"{name}{k}") for k in range(n)]


def over_groups(eng, full, body, tail=False, peeled=0):
    for g in range(3):
        body(g, g % 2, g // 2, False)
    if full - peeled > 3:
        with eng.Fori(1, (full - peeled - 1) // 2) as i:
            body(2 * i + 1, 1, i, False)
            body(2 * i + 2, 0, i + 1, False)
    for g in range(full - peeled, full):
        body(g, g % 2, g // 2, False)
    if tail:
        body(full, full % 2, full // 2, True)


def uses(groups, slot):
    return (groups + 1 - slot) // 2


def first_group(g):
    return isinstance(g, int) and g == 0


def wait_alone(eng, sem, value, held):
    eng.wait_ge(sem, value)
    if not isinstance(value, int):
        eng.sem_inc(held, 1)


def rows_dma(eng, dram, sbuf, g, dm, is_tail, sem, store=False):
    def move(d, s, inc):
        eng.dma_start(*((d, s) if store else (s, d))).then_inc(sem, inc)
    if not is_tail:
        move(dram[bass.ds(g * ROWS, ROWS), :].rearrange("(k p) c -> p k c", p=P), sbuf[:, :, :], 32)
        return
    n = len(dm.TAIL) - 1
    assert n >= 1
    move(dram[g * ROWS:g * ROWS + n * P, :].rearrange("(k p) c -> p k c", p=P), sbuf[:, 0:n, :], 16)
    move(dram[g * ROWS + n * P:dm.N, :], sbuf[0:dm.TAIL[-1], n, :], 16)


def parts_of(dm, is_tail):
    n = len(dm.TAIL) - 1
    return [(0, n, P), (n, n + 1, dm.TAIL[-1])] if is_tail else [(0, T, P)]



def constants_phase(nc, dm, C):
    with ExitStack() as ctx:
        sp = Space(nc, ctx, "cst")
        iota_i = sp.sb("iota_i", [P, dm.WIDE], I32)
        col_i = sp.sb("col_i", [P, 1], I32)
        s_mem, s_sel, s_iota = sp.sem("mem"), sp.sem("sel"), sp.sem("iota")
        s_conv = sp.sem("conv")
        with nc.Block() as block:
            @block.gpsimd
            def _(pool):
                pool.iota(iota_i[:, :], pattern=[[1, dm.WIDE]], base=0, channel_multiplier=0).then_inc(s_iota, 1)
                pool.iota(col_i[:, :], pattern=[[0, 1]], base=0, channel_multiplier=1).then_inc(s_iota, 1)
                pool.memset(C.ident[:, :], 0.0).then_inc(s_mem, 1)
                pool.memset(C.lower[:, :], 1.0).then_inc(s_mem, 1)
                pool.memset(C.upper[:, :], 1.0).then_inc(s_mem, 1)
                pool.memset(C.minus_half[:, :], -0.5).then_inc(s_mem, 1)
                pool.memset(C.ones[:, :], 1.0).then_inc(s_mem, 1)
                pool.wait_ge(s_mem, 5)
                pool.affine_select(out=C.ident[:, :], in_=C.ident[:, :], compare_op=ALU.not_equal, fill=1.0,
                                   base=0, pattern=[[-1, P]], channel_multiplier=1).then_inc(s_sel, 1)
                pool.affine_select(out=C.lower[:, :], in_=C.lower[:, :], compare_op=ALU.is_gt, fill=0.0,
                                   base=0, pattern=[[-1, P]], channel_multiplier=1).then_inc(s_sel, 1)
                pool.affine_select(out=C.upper[:, :], in_=C.upper[:, :], compare_op=ALU.is_gt, fill=0.0,
                                   base=0, pattern=[[1, P]], channel_multiplier=-1).then_inc(s_sel, 1)
                pool.wait_ge(s_sel, 3)

            @block.vector
            def _(dve):
                dve.wait_ge(s_iota, 2)
                dve.tensor_copy(C.iota[:, :], iota_i[:, :]).then_inc(s_conv, 1)
                dve.tensor_copy(C.col[:, :], col_i[:, :]).then_inc(s_conv, 1)
                dve.wait_ge(s_sel, 3)
                dve.tensor_copy(C.ident_h[:, :], C.ident[:, :]).then_inc(s_conv, 1)
                dve.wait_ge(s_conv, 3)



def edges_phase(nc, dm, C, src, dst, src_edges, dst_edges):
    with ExitStack() as ctx:
        sp = Space(nc, ctx, "edg")
        raw = [sp.sb(f"raw{k}", [P, dm.ET], I32) for k in range(2)]
        part = [sp.sb(f"part{k}", [P, dm.ET], I32) for k in range(2)]
        key = [sp.sb(f"key{k}", [P, dm.ET]) for k in range(2)]
        s_fill, s_load, s_link = sp.sem("fill"), sp.sem("load"), sp.sem("link")
        whole = dm.E // dm.ET
        rest = dm.E - whole * dm.ET
        with nc.Block() as block:
            @block.vector
            def _(dve):
                link = Link(dve, s_link)
                for k in range(2):
                    dve.memset(raw[k][:, :], dm.NPAD - 1).then_inc(s_fill, 1)
                dve.wait_ge(s_load, 16 * (4 if rest else 2))
                for k in range(2):
                    link(dve.tensor_copy(key[k][:, :], raw[k][:, :]))
                for k, edges in enumerate((src_edges, dst_edges)):
                    link(dve.tensor_scalar(part[0][:, :], raw[k][:, :], 7, None, ALU.arith_shift_right))
                    link(dve.tensor_scalar(part[1][:, :], raw[k][:, :], P - 1, None, ALU.bitwise_and))
                    link(dve.tensor_copy(edges.hi[:, :], part[0][:, :]))
                    link(dve.tensor_copy(edges.lo[:, :], part[1][:, :]))
                    link(dve.tensor_copy(edges.pay[:, :, 0], key[k][:, :]))
                    other = key[1 - k]
                    link(dve.scalar_tensor_tensor(out=edges.pay[:, :, 1], in0=other[:, :], scalar=float(dm.N),
                                                  in1=other[:, :], op0=ALU.is_lt, op1=ALU.mult))

            @block.sync
            def _(sync):
                sync.wait_ge(s_fill, 2)
                for k, e in enumerate((src, dst)):
                    sync.dma_start(raw[k][0:whole, :],
                                   e[0:whole * dm.ET].rearrange("(p f) -> p f", f=dm.ET)).then_inc(s_load, 16)
                    if rest:
                        sync.dma_start(raw[k][whole:whole + 1, 0:rest],
                                       e[whole * dm.ET:dm.E].rearrange("(p f) -> p f", p=1)).then_inc(s_load, 16)
                sync.wait_ge(s_load, 16 * (4 if rest else 2))



def sort_phase(nc, dm, C, edges, tag, scores=None):
    AC = dm.AC
    with ExitStack() as ctx:
        sp = Space(nc, ctx, tag)
        s_held = sp.sem("held")
        ohl = [sp.sb(f"ohl{s}", [P, T, P], BF16) for s in range(2)]
        ohh = [sp.sb(f"ohh{s}", [P, T, AC], BF16) for s in range(2)]
        ohlT = [sp.sb(f"ohlT{s}", [P, T, P]) for s in range(2)]
        keys = [sp.sb(f"keys{s}", [P, T]) for s in range(2)]
        start_at = sp.sb("start_at", [P, AC])
        scanned = sp.sb("scanned", [P, AC])
        zeros = sp.sb("zeros", [P, AC])
        run = [sp.sb(f"run{k}", [P, AC]) for k in range(2)]
        waste = [sp.sb(f"waste{k}", [P, AC + P]) for k in range(2)]
        tmp = sp.sb("tmp", [P, AC])
        before = sp.sb("before", [P, T])
        inside = sp.sb("inside", [P, T])
        place = [sp.sb(f"place{s}", [P, T], I32) for s in range(2)]
        pay = [sp.sb(f"pay{s}", [P, T, 2]) for s in range(2)]
        zero_h = sp.sb("zero_h", [P, dm.WIDE], BF16)
        hist = sp.ps("hist", [P, 512])
        look = [sp.ps(f"look{k}", [P, 512]) for k in range(T)]
        keyrow = [sp.ps(f"keyrow{s}", [P, T, P]) for s in range(2)]
        turned = sp.ps("turned", [P, T, P], BF16)
        H = hist[:, 0:AC]

        s_zero, s_oh1, s_hist1, s_link = sp.sem("zero"), sp.sem("oh1"), sp.sem("hist1"), sp.sem("link")
        s_rowsum, s_base, s_start, s_seed = sp.sem("rowsum"), sp.sem("base"), sp.sem("start"), sp.sem("seed")
        s_oh, s_keys, s_turn, s_turned, s_look = sp.sem("oh"), sp.sem("keys"), sp.sem("turn"), sp.sem("turned"), sp.sem("look")
        s_hist, s_run, s_cnt, s_place = sp.sem("hist"), sp.sem("run"), sp.sem("cnt"), sp.sem("place")
        s_pay, s_scat = sp.sems("pay"), sp.sems("scat")
        if scores:
            index = [sp.sb(f"index{s}", [P, T, 2], I32) for s in range(2)]
            got = [sp.sb(f"got{s}", [P, T, 2]) for s in range(2)]
            s_ix, s_got, s_sum = sp.sems("ix"), sp.sems("got"), sp.sem("sum")

        with nc.Block() as block:
            @block.vector
            def _(dve):
                def one_hots(g, s, k, ready):
                    dve.tensor_scalar(ohl[s][:, k, :], C.iota[:, 0:P], edges.lo[:, bass.ds(T * g + k, 1)], None,
                                      ALU.is_equal).then_inc(ready, 1)
                    dve.tensor_scalar(ohh[s][:, k, :], C.iota[:, 0:AC], edges.hi[:, bass.ds(T * g + k, 1)], None,
                                      ALU.is_equal).then_inc(ready, 1)

                dve.memset(zero_h[:, :], 0.0).then_inc(s_zero, 1)
                dve.memset(zeros[:, :], 0.0).then_inc(s_zero, 1)
                def count(g, s, u, is_tail):
                    if not first_group(g):
                        dve.wait_ge(s_hist1, T * (g - 1) + 1)
                    for k in range(T):
                        one_hots(g, s, k, s_oh1)
                over_groups(dve, dm.EG, count)
                link = Link(dve, s_link)
                dve.wait_ge(s_hist1, dm.ET + 1)
                link(dve.tensor_copy(edges.count[:, :], H))
                link(dve.tensor_tensor_scan(scanned[:, :], edges.count[:, :], zeros[:, :], 0.0, ALU.add, ALU.add))
                dve.tensor_copy(before[:, 0:1], scanned[:, AC - 1:AC]).then_inc(s_rowsum, 1)
                dve.wait_ge(s_base, 1)
                link(dve.tensor_copy(inside[:, 0:1], look[0][:, 0:1]))
                link(dve.tensor_scalar(scanned[:, :], scanned[:, :], inside[:, 0:1], None, ALU.add))
                dve.tensor_tensor(start_at[:, :], scanned[:, :], edges.count[:, :], ALU.subtract).then_inc(s_start, 1)
                link(dve.tensor_scalar(tmp[:, :], edges.count[:, :], 0.0, float(NO_ROW), ALU.is_equal, ALU.mult))
                link(dve.scalar_tensor_tensor(out=tmp[:, :], in0=scanned[:, :], scalar=-1.0, in1=tmp[:, :],
                                              op0=ALU.add, op1=ALU.add))
                link(dve.tensor_copy(edges.last[:, :], tmp[:, :]))

                def find(g, s, k):
                    n = T * g + k
                    dve.wait_ge(s_look, n + 1)
                    if k >= 2:
                        dve.wait_ge(s_cnt, 2 * n - 2)
                    dve.scalar_tensor_tensor(out=waste[k % 2][:, dm.AC:], in0=keyrow[s][:, k, :], scalar=keys[s][:, k:k + 1],
                                             in1=C.lower[:, :], op0=ALU.is_equal, op1=ALU.mult,
                                             accum_out=inside[:, k:k + 1]).then_inc(s_cnt, 1)
                    dve.scalar_tensor_tensor(out=waste[k % 2][:, 0:AC], in0=look[k][:, 0:AC], scalar=1.0,
                                             in1=ohh[s][:, k, :], op0=ALU.mult, op1=ALU.mult,
                                             accum_out=before[:, k:k + 1]).then_inc(s_cnt, 1)

                def take_keys(g, s):
                    dve.tensor_copy(keys[s][:, :], edges.pay[:, bass.ds(T * g, T), 0]).then_inc(s_keys, 1)

                def step(g, s, u, is_tail):
                    more = not (isinstance(g, int) and g + 2 >= dm.EG)
                    for k in range(T + 1):
                        if k < T:
                            find(g, s, k)
                        if more and k > 0:
                            dve.wait_ge(s_cnt, 2 * (T * g + k))
                            one_hots(g + 2, s, k - 1, s_oh)
                    dve.wait_ge(s_cnt, 2 * T * g + 2 * T)
                    if more:
                        take_keys(g + 2, s)
                    dve.wait_ge(s_scat[s], 64 * u)
                    dve.tensor_tensor(place[s][:, :], before[:, :], inside[:, :], ALU.add).then_inc(s_place, 1)
                    dve.wait_ge(s_place, g + 1)
                    if scores and not first_group(g):
                        add(g - 1, 1 - s, u - 1 + s)

                def add(g, s, u):
                    dve.wait_ge(s_got[s], 16 * 2 * T * (u + 1))
                    dve.tensor_tensor(scores.total[:, bass.ds(T * g, T)], got[s][:, :, 0], got[s][:, :, 1],
                                      ALU.add).then_inc(s_sum, 1)

                dve.wait_ge(s_hist1, dm.ET + 1)
                for g in range(2):
                    take_keys(g, g)
                    for k in range(T):
                        one_hots(g, g, k, s_oh)
                over_groups(dve, dm.EG, step, peeled=2)
                if scores:
                    add(dm.EG - 1, (dm.EG - 1) % 2, (dm.EG - 1) // 2)
                    dve.wait_ge(s_sum, dm.EG)

            @block.tensor
            def _(pe):
                pe.wait_ge(s_zero, 2)
                pe.matmul(H, zero_h[:, 0:P], zero_h[:, 0:AC], start=True, stop=True, skip_group_check=True).then_inc(s_hist1, 1)
                def count(g, s, u, is_tail):
                    for k in range(T):
                        pe.wait_ge(s_oh1, 2 * (T * g + k + 1))
                        pe.matmul(H, ohl[s][:, k, :], ohh[s][:, k, :], start=False, stop=True,
                                  skip_group_check=True).then_inc(s_hist1, 1)
                over_groups(pe, dm.EG, count)
                pe.wait_ge(s_rowsum, 1)
                pe.matmul(look[0][:, 0:1], C.upper[:, :], before[:, 0:1], start=True, stop=True).then_inc(s_base, 1)
                pe.wait_ge(s_start, 1)
                pe.matmul(H, C.ident[:, :], start_at[:, :], start=True, stop=True, skip_group_check=True).then_inc(s_seed, 1)

                def turn(g, s):
                    pe.wait_ge(s_oh, 2 * T * (g + 1))
                    pe.wait_ge(s_keys, g + 1)
                    pe.wait_ge(s_turned, g)
                    if not (isinstance(g, int) and g < 2):
                        pe.wait_ge(s_cnt, 2 * T * (g - 1))
                    for k in range(T):
                        pe.transpose(turned[:, k, :], ohl[s][:, k, :], C.ident_h[:, :])
                        ins = pe.matmul(keyrow[s][:, k, :], keys[s][:, k:k + 1].to_broadcast([P, P]), C.ident[:, :],
                                        start=True, stop=True)
                    ins.then_inc(s_turn, 1)

                turn(0, 0)
                def step(g, s, u, is_tail):
                    pe.wait_ge(s_turned, g + 1)
                    for k in range(T):
                        n = T * g + k
                        pe.wait_ge(s_run, n + 1)
                        pe.matmul(H, ohl[s][:, k, :], ohh[s][:, k, :], start=False, stop=True,
                                  skip_group_check=True).then_inc(s_hist, 1)
                        if not first_group(g):
                            pe.wait_ge(s_cnt, 2 * (n - T) + 2)
                        pe.matmul(look[k][:, 0:AC], ohlT[s][:, k, :], run[k % 2][:, :], start=True, stop=True).then_inc(s_look, 1)
                        if k == 1 and not (isinstance(g, int) and g + 1 == dm.EG):
                            turn(g + 1, 1 - s)
                over_groups(pe, dm.EG, step, peeled=2)

            @block.scalar
            def _(act):
                act.wait_ge(s_seed, 1)
                act.copy(run[0][:, :], H).then_inc(s_run, 1)

                def turned_out(g, s):
                    act.wait_ge(s_turn, g + 1)
                    if not (isinstance(g, int) and g < 2):
                        act.wait_ge(s_look, T * (g - 1))
                    act.copy(ohlT[s][:, :, :], turned[:, :, :]).then_inc(s_turned, 1)

                turned_out(0, 0)
                def step(g, s, u, is_tail):
                    for k in range(T):
                        n = T * g + k
                        act.wait_ge(s_hist, n + 1)
                        act.wait_ge(s_look, n)
                        act.copy(run[(k + 1) % 2][:, :], H).then_inc(s_run, 1)
                        if k == 1 and not (isinstance(g, int) and g + 1 == dm.EG):
                            turned_out(g + 1, 1 - s)
                over_groups(act, dm.EG, step, peeled=2)

            @block.gpsimd
            def _(pool):
                def tiles(g, s, u, is_tail):
                    wait_alone(pool, s_scat[s], 64 * u, s_held)
                    wait_alone(pool, s_place, g + 1, s_held)
                    pool.tensor_copy(pay[s][:, :, :], edges.pay[:, bass.ds(T * g, T), :]).then_inc(s_pay[s], 1)
                    wait_alone(pool, s_pay[s], u + 1, s_held)
                    for k in range(T):
                        pool.indirect_dma_start(edges.sorted, bass.IndirectOffsetOnAxis(ap=place[s][:, k:k + 1], axis=0),
                                                pay[s][:, k, :], None).then_inc(s_scat[s], 16)
                    if scores:
                        fetch_scores(g, s, u)

                def fetch_scores(g, s, u):
                    if not first_group(g):
                        wait_alone(pool, s_sum, g - 1, s_held)
                    pool.tensor_copy(index[s][:, :, :], scores.at[:, bass.ds(T * g, T), :]).then_inc(s_ix[s], 1)
                    wait_alone(pool, s_ix[s], u + 1, s_held)
                    for k in range(T):
                        for j in range(2):
                            pool.indirect_dma_start(got[s][:, k, j:j + 1], None, scores.terms,
                                                    bass.IndirectOffsetOnAxis(ap=index[s][:, k, j:j + 1], axis=0)
                                                    ).then_inc(s_got[s], 16)
                over_groups(pool, dm.EG, tiles)
                for s in range(2):
                    pool.wait_ge(s_scat[s], 64 * uses(dm.EG, s))


def sorted_phase(nc, dm, C, edges, tag, scores=None):
    TH = dm.TH
    with ExitStack() as ctx:
        sp = Space(nc, ctx, tag)
        rows = sp.sb("rows", [TH, 2, P, 2])
        same = sp.sb("same", [TH, P])
        n_first = sp.sb("n_first", [TH, 2])
        firsts = sp.ps("firsts", [P, 2, P])
        cols = sp.ps("cols", [P, 2, 2, TH])
        s_load, s_turn, s_row, s_link, s_copy = sp.sem("load"), sp.sem("turn"), sp.sem("row"), sp.sem("link"), sp.sem("copy")
        s_ends = sp.sem("ends")
        with nc.Block() as block:
            @block.sync
            def _(sync):
                sync.dma_start(rows[:, :, :, :].rearrange("p h j c -> p h (j c)"),
                               edges.sorted.rearrange("(h p j) c -> p h (j c)", p=TH, j=P)).then_inc(s_load, 16)
                if scores:
                    sync.dma_start(scores.ends[:, :, :], edges.sorted.rearrange("(p f) c -> p f c", p=P)).then_inc(s_ends, 16)
                    sync.wait_ge(s_ends, 16)
                sync.wait_ge(s_load, 16)

            @block.tensor
            def _(pe):
                pe.wait_ge(s_load, 16)
                for c in range(2):
                    for h in range(2):
                        pe.transpose(cols[:, c, h, :], rows[:, h, :, c], C.ident[0:TH, 0:TH]).then_inc(s_turn, 1)
                for h in range(2):
                    pe.matmul(firsts[:, h, 0:TH], rows[:, h, 0:1, 0].to_broadcast([TH, P]), C.ident[0:TH, 0:TH],
                              start=True, stop=True).then_inc(s_row, 1)

            @block.vector
            def _(dve):
                link = Link(dve, s_link)
                dve.wait_ge(s_turn, 4)
                dve.tensor_copy(edges.keyT[:, :].rearrange("p (h t) -> p h t", h=2), cols[:, 0, :, :]).then_inc(s_copy, 1)
                dve.tensor_copy(edges.otherT[:, :].rearrange("p (h t) -> p h t", h=2), cols[:, 1, :, :]).then_inc(s_copy, 1)
                dve.wait_ge(s_row, 2)
                for h1 in range(2):
                    for h in range(h1, 2):
                        last_key = rows[:, h1, P - 1:P, 0]
                        if h == h1:
                            dve.scalar_tensor_tensor(out=edges.joins[0:TH, h1, h, :], in0=firsts[0:TH, h, 0:TH],
                                                     scalar=last_key, in1=C.upper[0:TH, 0:TH], op0=ALU.is_equal,
                                                     op1=ALU.mult).then_inc(s_copy, 1)
                        else:
                            dve.tensor_scalar(edges.joins[0:TH, h1, h, :], firsts[0:TH, h, 0:TH], last_key, None,
                                              ALU.is_equal).then_inc(s_copy, 1)
                for h in range(2):
                    link(dve.tensor_scalar(same[:, :], rows[:, h, :, 0], rows[:, h, 0:1, 0], 0.0, ALU.is_equal,
                                           ALU.add, accum_out=n_first[:, h:h + 1]))
                    link(dve.scalar_tensor_tensor(out=n_first[:, h:h + 1], in0=C.col[0:TH, :], scalar=float(P),
                                                  in1=n_first[:, h:h + 1], op0=ALU.mult, op1=ALU.add))
                    link(dve.tensor_scalar(edges.first_end[0:TH, h:h + 1], n_first[:, h:h + 1],
                                           float(h * TH * P - 1), None, ALU.add))
                dve.wait_ge(s_copy, 5)
                if scores:
                    dve.wait_ge(s_ends, 16)
                    link(dve.tensor_copy(scores.at[:, :, 0], scores.ends[:, :, 0]))
                    link(dve.tensor_scalar(scores.at[:, :, 1], scores.ends[:, :, 1], float(dm.NPAD), None, ALU.add))



def norm_stats(dve, link, x4, stats, mv, s_held):
    for dst, src, op in ((stats, x4, dve.bn_stats), (mv, stats, dve.bn_aggr)):
        for k in range(T):
            ins = op(dst[:, k, :], src[:, k, :])
            if k + 1 < T:
                ins.then_inc(link.sem, 1)
                link.n += 1
        ins.then_inc(link.sem, 1)
        link.n += 1
        wait_alone(dve, link.sem, link.base + link.n, s_held)


def norm_phase(nc, dm, C, x, w_align, h_out, scores):
    NG = dm.NG
    with ExitStack() as ctx:
        sp = Space(nc, ctx, "nrm")
        s_held = sp.sem("held")
        x4 = [sp.sb(f"x{s}", [P, T, D]) for s in range(2)]
        h4 = [sp.sb(f"h{s}", [P, T, D]) for s in range(2)]
        hT = [sp.sb(f"hT{s}", [P, KC, ROWS]) for s in range(2)]
        stats, mv = sp.sb("stats", [P, T, 6]), sp.sb("mv", [P, T, 2])
        rstd = [sp.sb(f"rstd{s}", [P, T]) for s in range(2)]
        shift = [sp.sb(f"shift{s}", [P, T]) for s in range(2)]
        halves = sp.sb("halves", [P, KC, 2])
        dots = [sp.sb(f"dots{s}", [2, ROWS]) for s in range(2)]
        turn = [[sp.ps(f"turn{s}{c}", [P, ROWS]) for c in range(KC)] for s in range(2)]
        dots_ps = sp.ps("dots", [2, ROWS])
        s_x, s_st, s_sc = sp.sems("x"), sp.sems("st"), sp.sems("sc")
        s_turned = sp.sems("turned", KC)
        s_w, s_stats, s_mv, s_var, s_rstd, s_shift, s_h, s_turn, s_prod, s_dot = (sp.sem(n) for n in (
            "w", "stats", "mv", "var", "rstd", "shift", "h", "turn", "prod", "dot"))
        with nc.Block() as block:
            @block.sync
            def _(sync):
                with nc.allow_non_contiguous_dma(reason="score weights by feature"):
                    for j in range(2):
                        sync.dma_start(halves[:, :, j], w_align[0, j * D:(j + 1) * D].rearrange("(c p) -> p c", p=P)).then_inc(s_w, 16)

                def load(g, s, u, is_tail):
                    if not first_group(g):
                        wait_alone(sync, s_h, g - 1, s_held)
                    rows_dma(sync, x, x4[s], g, dm, is_tail, s_x[s])
                over_groups(sync, dm.FULL, load, tail=True)

            @block.vector
            def _(dve):
                def turned(g, s):
                    dve.wait_ge(s_turn, KC * g + KC)
                    if not (isinstance(g, int) and g < 2):
                        dve.wait_ge(s_prod, g - 1)
                    dve.tensor_copy(hT[s][:, 1, :], turn[s][1][:, :]).then_inc(s_turned[1], 1)

                def dot(g, s, u):
                    dve.wait_ge(s_prod, g + 1)
                    dve.wait_ge(s_sc[s], 16 * u)
                    dve.tensor_copy(dots[s][:, :], dots_ps[:, :]).then_inc(s_dot, 1)

                def step(g, s, u, is_tail):
                    dve.wait_ge(s_x[s], 32 * (u + 1))
                    for k in range(T):
                        dve.bn_stats(stats[:, k, :], x4[s][:, k, :]).then_inc(s_stats, 1)
                    wait_alone(dve, s_stats, T * g + T, s_held)
                    for k in range(T):
                        dve.bn_aggr(mv[:, k, :], stats[:, k, :]).then_inc(s_mv, 1)
                    if not first_group(g):
                        dve.wait_ge(s_h, g - 1)
                    dve.wait_ge(s_mv, T * g + T)
                    dve.tensor_scalar(rstd[s][:, :], mv[:, :, 1], LN_EPS, None, ALU.add).then_inc(s_var, 1)
                    dve.tensor_scalar(shift[s][:, :], mv[:, :, 0], -1.0, None, ALU.mult).then_inc(s_var, 1)
                    if not (isinstance(g, int) and g < 2):
                        turned(g - 2, s)
                    if not (isinstance(g, int) and g < 3):
                        dot(g - 3, 1 - s, u - 2 + s)
                    wait_alone(dve, s_var, 2 * g + 2, s_held)
                over_groups(dve, dm.FULL, step, tail=True)
                turned(NG - 2, (NG - 2) % 2)
                turned(NG - 1, (NG - 1) % 2)
                dot(NG - 3, (NG - 3) % 2, (NG - 3) // 2)
                dot(NG - 2, (NG - 2) % 2, (NG - 2) // 2)
                dot(NG - 1, (NG - 1) % 2, (NG - 1) // 2)

            @block.gpsimd
            def _(pool):
                def store(g, s):
                    wait_alone(pool, s_dot, g + 1, s_held)
                    pool.dma_start(scores.rearrange("(j n) o -> j (n o)", j=2)[:, bass.ds(g * ROWS, ROWS)],
                                   dots[s][:, :]).then_inc(s_sc[s], 16)

                def root(g, s, u, is_tail):
                    wait_alone(pool, s_var, 2 * g + 2, s_held)
                    pool.tensor_tensor(rstd[s][:, :], rstd[s][:, :], C.minus_half[:, :], ALU.pow).then_inc(s_rstd, 1)
                    wait_alone(pool, s_rstd, g + 1, s_held)
                    pool.tensor_tensor(shift[s][:, :], shift[s][:, :], rstd[s][:, :], ALU.mult).then_inc(s_shift, 1)
                    if not (isinstance(g, int) and g < 3):
                        store(g - 3, 1 - s)
                over_groups(pool, dm.FULL, root, tail=True)
                for g in range(NG - 3, NG):
                    store(g, g % 2)
                for s in range(2):
                    pool.wait_ge(s_sc[s], 16 * uses(NG, s))

            @block.tensor
            def _(pe):
                pe.wait_ge(s_w, 32)
                def products(g, s):
                    for c in range(KC):
                        pe.wait_ge(s_turned[c], g + 1)
                    pe.wait_ge(s_dot, g)
                    for c in range(KC):
                        ins = pe.matmul(dots_ps[:, :], halves[:, c, :], hT[s][:, c, :], start=c == 0, stop=c == KC - 1)
                    ins.then_inc(s_prod, 1)

                def step(g, s, u, is_tail):
                    pe.wait_ge(s_h, g + 1)
                    for c in range(KC):
                        if not first_group(g):
                            pe.wait_ge(s_turned[c], g - 1)
                        turn_rows(pe, C, h4[s], c, turn[s][c], s_turn)
                    if not first_group(g):
                        products(g - 1, 1 - s)
                over_groups(pe, dm.FULL, step, tail=True)
                products(NG - 1, (NG - 1) % 2)

            @block.scalar
            def _(act):
                def turned(g, s):
                    act.wait_ge(s_turn, KC * g + 1)
                    if not (isinstance(g, int) and g < 2):
                        act.wait_ge(s_prod, g - 1)
                    act.copy(hT[s][:, 0, :], turn[s][0][:, :]).then_inc(s_turned[0], 1)

                def step(g, s, u, is_tail):
                    act.wait_ge(s_shift, g + 1)
                    act.wait_ge(s_st[s], 32 * u)
                    if not first_group(g):
                        act.wait_ge(s_turn, KC * (g - 1))
                    for k in range(T):
                        ins = act.activation(h4[s][:, k, :], x4[s][:, k, :], ACT.Relu,
                                             bias=shift[s][:, k:k + 1], scale=rstd[s][:, k:k + 1])
                    ins.then_inc(s_h, 1)
                    if not first_group(g):
                        turned(g - 1, 1 - s)
                    act.wait_ge(s_h, g + 1)
                    rows_dma(act, h_out, h4[s], g, dm, is_tail, s_st[s], store=True)
                over_groups(act, dm.FULL, step, tail=True)
                turned(NG - 1, (NG - 1) % 2)
                for s in range(2):
                    act.wait_ge(s_st[s], 32 * uses(NG, s))



def weights_phase(nc, dm, C, edges, scores, params, e_dram):
    ET = dm.ET
    b_align, g_a, b_a, m_a, v_a = params
    with ExitStack() as ctx:
        sp = Space(nc, ctx, "att")
        score, ends = scores.total, scores.ends
        par = sp.sb("par", [P, 5])
        sc = sp.sb("sc", [P, 4])
        keyb = sp.sb("keyb", [P, ET + 1])
        brk = sp.sb("brk", [P, ET])
        brkn = sp.sb("brkn", [P, ET])
        run = sp.sb("run", [P, ET])
        top = sp.sb("top", [P, ET])
        edge = sp.sb("edge", [P, 4])
        row = sp.sb("row", [1, 8, P])
        lead = sp.sb("lead", [P, 2])
        e_tab = sp.sb("e_tab", [P, ET])
        rows = sp.sb("rows", [dm.TH, 2, P])
        pr = sp.ps("pr", [P, 4, P])
        pc = sp.ps("pc", [P, 2])
        pe_cols = sp.ps("pe_cols", [P, 2, dm.TH])
        s_link, s_pool, s_par = sp.sem("link"), sp.sem("pool"), sp.sem("par")
        s_edge, s_row, s_lead, s_col, s_top, s_e, s_est, s_erow, s_turn = (sp.sem(n) for n in (
            "edge", "row", "lead", "col", "top", "e", "est", "erow", "turn"))
        with nc.Block() as block:
            @block.sync
            def _(sync):
                for j, v in enumerate((b_align, g_a, b_a, m_a, v_a)):
                    sync.dma_start(par[:, j:j + 1], v.rearrange("(a b) -> a b", a=1).to_broadcast([P, 1])).then_inc(s_par, 16)
                sync.wait_ge(s_e, 1)
                sync.dma_start(e_dram.rearrange("(p f) -> p f", p=P), e_tab[:, :]).then_inc(s_est, 16)
                sync.wait_ge(s_est, 16)
                sync.dma_start(rows[:, :, :], e_dram.rearrange("(h p j) -> p h j", p=dm.TH, j=P)).then_inc(s_erow, 16)
                sync.wait_ge(s_erow, 16)

            @block.gpsimd
            def _(pool):
                pool.wait_ge(s_pool, 1)
                pool.tensor_tensor(sc[:, 1:2], sc[:, 0:1], C.minus_half[:, 0:1], ALU.pow).then_inc(s_pool, 1)

            @block.vector
            def _(dve):
                link = Link(dve, s_link)
                dve.wait_ge(s_par, 80)
                dve.tensor_scalar(sc[:, 0:1], par[:, 4:5], BN_A_EPS, None, ALU.add).then_inc(s_pool, 1)
                dve.wait_ge(s_pool, 2)
                link(dve.tensor_tensor(sc[:, 1:2], sc[:, 1:2], par[:, 1:2], ALU.mult))
                link(dve.tensor_tensor(sc[:, 2:3], par[:, 0:1], par[:, 3:4], ALU.subtract))
                link(dve.tensor_scalar(score[:, :], score[:, :], sc[:, 2:3], None, ALU.add))
                link(dve.tensor_scalar(score[:, :], score[:, :], sc[:, 1:2], par[:, 2:3], ALU.mult, ALU.add))
                link(dve.scalar_tensor_tensor(out=score[:, :], in0=score[:, :], scalar=0.01, in1=score[:, :],
                                              op0=ALU.mult, op1=ALU.max))
                link(dve.tensor_copy(keyb[:, 1:ET + 1], ends[:, :, 0]))
                link(dve.memset(edge[:, 0:4], -1.0))
                dve.tensor_copy(edge[:, 0:1], keyb[:, ET:ET + 1]).then_inc(s_edge, 1)
                dve.tensor_copy(edge[:, 1:2], keyb[:, 1:2]).then_inc(s_edge, 1)
                dve.wait_ge(s_row, 2)
                link(dve.memset(row[:, :, :], -1.0))
                link(dve.tensor_copy(row[0:1, 0, 1:P], pr[0:1, 0, 0:P - 1]))
                link(dve.tensor_copy(row[0:1, 1, 0:P - 1], pr[0:1, 1, 1:P]))
                dve.memset(row[0:1, 2, 0:1], 1.0).then_inc(s_lead, 1)
                dve.wait_ge(s_col, 2)
                link(dve.tensor_copy(keyb[:, 0:1], pc[:, 0:1]))
                link(dve.tensor_copy(lead[:, 0:1], pc[:, 1:2]))
                link(dve.tensor_tensor(brk[:, :], keyb[:, 0:ET], keyb[:, 1:ET + 1], ALU.not_equal))
                link(dve.tensor_copy(brkn[:, 0:ET - 1], brk[:, 1:ET]))
                link(dve.tensor_tensor(brkn[:, ET - 1:ET], keyb[:, ET:ET + 1], lead[:, 0:1], ALU.not_equal))
                for b in (brk, brkn):
                    link(dve.tensor_scalar(b[:, :], b[:, :], BELOW_ALL, None, ALU.mult))

                def carried(src_tab, brk_tab, out_tab, flip, edge_at, row_at, n):
                    view = (lambda a: a[:, ::-1]) if flip else (lambda a: a[:, :])
                    last = slice(0, 1) if flip else slice(ET - 1, ET)
                    link(dve.tensor_tensor_scan(view(out_tab), view(brk_tab), view(src_tab), BELOW_ALL, ALU.add, ALU.max))
                    dve.tensor_copy(edge[:, 2:3], out_tab[:, last]).then_inc(s_edge, 1)
                    link(dve.tensor_reduce(edge[:, 3:4], brk_tab[:, :], mybir.AxisListType.X, ALU.add))
                    dve.tensor_copy(edge[:, 1:2], edge[:, 3:4]).then_inc(s_edge, 1)
                    dve.wait_ge(s_row, 2 * n + 2)
                    link(dve.tensor_copy(row[0:1, 3, :], pr[0:1, 2, :]))
                    link(dve.tensor_copy(row[0:1, 4, :], pr[0:1, 3, :]))
                    rv = (lambda a: a[:, ::-1]) if flip else (lambda a: a)
                    link(dve.tensor_tensor_scan(rv(row[0:1, 5, :]), rv(row[0:1, 4, :]), rv(row[0:1, 3, :]), BELOW_ALL,
                                                ALU.add, ALU.max))
                    link(dve.memset(row[0:1, 6, :], BELOW_ALL))
                    if flip:
                        ins = dve.tensor_copy(row[0:1, 6, 0:P - 1], row[0:1, 5, 1:P])
                    else:
                        ins = dve.tensor_copy(row[0:1, 6, 1:P], row[0:1, 5, 0:P - 1])
                    ins.then_inc(s_lead, 1)
                    dve.wait_ge(s_col, 2 + n)
                    link(dve.tensor_copy(lead[:, 1:2], pc[:, 0:1]))
                    link(dve.tensor_tensor_scan(view(out_tab), view(brk_tab), view(src_tab), lead[:, 1:2], ALU.add, ALU.max))

                carried(score, brk, run, False, 2, 3, 1)
                carried(run, brkn, top, True, 2, 3, 2)
                dve.tensor_tensor(score[:, :], score[:, :], top[:, :], ALU.subtract).then_inc(s_top, 1)
                dve.wait_ge(s_turn, 2)
                link(dve.tensor_copy(edges.weightT[:, :].rearrange("p (h t) -> p h t", h=2), pe_cols[:, :, :]))

            @block.tensor
            def _(pe):
                pe.wait_ge(s_edge, 2)
                for j in range(2):
                    pe.matmul(pr[0:1, j, :], edge[:, j:j + 1], C.ident[:, :], start=True, stop=True).then_inc(s_row, 1)
                pe.wait_ge(s_lead, 1)
                for j in range(2):
                    pe.matmul(pc[:, j:j + 1], row[0:1, j, :], row[0:1, 2, 0:1], start=True, stop=True).then_inc(s_col, 1)
                for n in (1, 2):
                    pe.wait_ge(s_edge, 2 * n + 2)
                    pe.matmul(pr[0:1, 2, :], edge[:, 2:3], C.ident[:, :], start=True, stop=True).then_inc(s_row, 1)
                    pe.matmul(pr[0:1, 3, :], edge[:, 1:2], C.ident[:, :], start=True, stop=True).then_inc(s_row, 1)
                    pe.wait_ge(s_lead, n + 1)
                    pe.matmul(pc[:, 0:1], row[0:1, 6, :], row[0:1, 2, 0:1], start=True, stop=True).then_inc(s_col, 1)
                pe.wait_ge(s_erow, 16)
                for h in range(2):
                    pe.transpose(pe_cols[:, h, :], rows[:, h, :], C.ident[0:dm.TH, 0:dm.TH]).then_inc(s_turn, 1)

            @block.scalar
            def _(act):
                act.wait_ge(s_top, 1)
                act.activation(e_tab[:, :], score[:, :], ACT.Exp).then_inc(s_e, 1)



def segment_phase(nc, dm, C, edges, rows_in, raw, tag, weighted):
    W = D + 1 if weighted else D
    TH = dm.TH
    with ExitStack() as ctx:
        sp = Space(nc, ctx, tag)
        s_held = sp.sem("held")
        index = [sp.sb(f"index{s}", [P, T], I32) for s in range(2)]
        keys = [sp.sb(f"keys{s}", [P, T]) for s in range(2)]
        wts = [sp.sb(f"wts{s}", [P, T]) for s in range(2)]
        msg = [sp.sb(f"msg{s}", [P, T, W]) for s in range(2)]
        same = [sp.sb(f"same{s}", [P, T, P]) for s in range(2)]
        out = [sp.sb(f"out{s}", [P, T, W]) for s in range(2)]
        tails = sp.sb("tails", [TH, 2, W])
        heads = sp.sb("heads", [TH, 2, W])
        keyrow = [sp.ps(f"keyrow{s}", [P, T, P]) for s in range(2)]
        total = [sp.ps(f"total{k}", [P, 512]) for k in range(T)]
        s_ix, s_msg, s_st = sp.sems("ix"), sp.sems("msg"), sp.sems("st")
        s_one, s_row, s_same, s_tot, s_out = sp.sem("one"), sp.sem("row"), sp.sem("same"), sp.sem("tot"), sp.sem("out")
        s_tail, s_head, s_carry, s_add, s_back = sp.sem("tail"), sp.sem("head"), sp.sem("carry"), sp.sem("add"), sp.sem("back")
        with nc.Block() as block:
            @block.gpsimd
            def _(pool):
                if weighted:
                    for s in range(2):
                        for k in range(T):
                            pool.memset(msg[s][:, k, D:W], 1.0).then_inc(s_one, 1)
                def fetch(g, s, u, is_tail):
                    if not first_group(g):
                        wait_alone(pool, s_out, T * (g - 1), s_held)
                    pool.tensor_copy(index[s][:, :], edges.otherT[:, bass.ds(T * g, T)]).then_inc(s_ix[s], 1)
                    pool.tensor_copy(keys[s][:, :], edges.keyT[:, bass.ds(T * g, T)]).then_inc(s_ix[s], 1)
                    n = 2
                    if weighted:
                        pool.tensor_copy(wts[s][:, :], edges.weightT[:, bass.ds(T * g, T)]).then_inc(s_ix[s], 1)
                        n = 3
                    wait_alone(pool, s_ix[s], n * u + n, s_held)
                    for k in range(T):
                        pool.indirect_dma_start(msg[s][:, k, 0:D], None, rows_in,
                                                bass.IndirectOffsetOnAxis(ap=index[s][:, k:k + 1], axis=0)
                                                ).then_inc(s_msg[s], 16)
                over_groups(pool, dm.EG, fetch)
                for s in range(2):
                    pool.wait_ge(s_st[s], 16 * uses(dm.EG, s))
                for h in range(2):
                    pool.indirect_dma_start(heads[:, h, :], None, raw,
                                            bass.IndirectOffsetOnAxis(ap=edges.first_end[0:TH, h:h + 1], axis=0)
                                            ).then_inc(s_head, 16)
                pool.wait_ge(s_tail, 16)
                pool.wait_ge(s_add, 2)
                for h in range(2):
                    pool.indirect_dma_start(raw, bass.IndirectOffsetOnAxis(ap=edges.first_end[0:TH, h:h + 1], axis=0),
                                            heads[:, h, :], None).then_inc(s_back, 16)
                pool.wait_ge(s_back, 32)

            @block.tensor
            def _(pe):
                n_ix = 3 if weighted else 2
                if weighted:
                    pe.wait_ge(s_one, 2 * T)
                def sums(g, s, u, is_tail):
                    pe.wait_ge(s_ix[s], n_ix * (u + 1))
                    if not first_group(g):
                        pe.wait_ge(s_same, T * (g - 1))
                    for k in range(T):
                        ins = pe.matmul(keyrow[s][:, k, :], keys[s][:, k:k + 1].to_broadcast([P, P]), C.ident[:, :],
                                        start=True, stop=True)
                    ins.then_inc(s_row, 1)
                    pe.wait_ge(s_msg[s], 16 * T * (u + 1))
                    for k in range(T):
                        pe.wait_ge(s_same, T * g + k + 1)
                        if not first_group(g):
                            pe.wait_ge(s_out, T * g + k - T + 1)
                        pe.matmul(total[k][:, 0:W], same[s][:, k, :], msg[s][:, k, :], start=True, stop=True).then_inc(s_tot, 1)
                over_groups(pe, dm.EG, sums)
                pe.wait_ge(s_tail, 16)
                pe.wait_ge(s_out, dm.ET)
                for h in range(2):
                    for h1 in range(h + 1):
                        ins = pe.matmul(total[h][0:TH, 0:W], edges.joins[0:TH, h1, h, :], tails[:, h1, :],
                                        start=h1 == 0, stop=h1 == h)
                    ins.then_inc(s_carry, 1)

            @block.vector
            def _(dve):
                def masks(g, s, u, is_tail):
                    dve.wait_ge(s_row, g + 1)
                    if not first_group(g):
                        dve.wait_ge(s_tot, T * (g - 1))
                    for k in range(T):
                        dve.tensor_scalar(same[s][:, k, :], keyrow[s][:, k, :], keys[s][:, k:k + 1],
                                          wts[s][:, k:k + 1] if weighted else None, ALU.is_equal,
                                          *([ALU.mult] if weighted else [])).then_inc(s_same, 1)
                over_groups(dve, dm.EG, masks)
                dve.wait_ge(s_head, 32)
                dve.wait_ge(s_carry, 2)
                for h in range(2):
                    dve.tensor_tensor(heads[:, h, :], heads[:, h, :], total[h][0:TH, 0:W], ALU.add).then_inc(s_add, 1)

            @block.scalar
            def _(act):
                def evacuate(g, s, u, is_tail):
                    act.wait_ge(s_st[s], 16 * u)
                    for k in range(T):
                        act.wait_ge(s_tot, T * g + k + 1)
                        act.copy(out[s][:, k, :], total[k][:, 0:W]).then_inc(s_out, 1)
                over_groups(act, dm.EG, evacuate)

            @block.sync
            def _(sync):
                def store(g, s, u, is_tail):
                    wait_alone(sync, s_out, T * g + T, s_held)
                    sync.dma_start(raw[bass.ds(g * ROWS, ROWS), :].rearrange("(k p) c -> p k c", p=P),
                                   out[s][:, :, :]).then_inc(s_st[s], 16)
                over_groups(sync, dm.EG, store)
                for s in range(2):
                    sync.wait_ge(s_st[s], 16 * uses(dm.EG, s))
                sync.dma_start(tails[:, :, :], raw.rearrange("(h p j) c -> p h j c", p=TH, j=P)[:, :, P - 1, :]).then_inc(s_tail, 16)
                sync.wait_ge(s_tail, 16)


def flipped_weights(nc, dm, C, jobs, tag):
    with ExitStack() as ctx:
        sp = Space(nc, ctx, tag)
        raw = [sp.sb(f"raw{j}", [P, w.shape[0] // P, D]) for j, (w, _, _) in enumerate(jobs)]
        ps = [sp.ps(f"ps{j}", [P, P]) for j in range(2)]
        s_load, s_turn, s_out = sp.sem("load"), sp.sem("turn"), sp.sem("out")
        blocks = [(j, o, c) for j, (w, _, _) in enumerate(jobs) for o in range(w.shape[0] // P) for c in range(KC)]
        with nc.Block() as block:
            @block.sync
            def _(sync):
                for j, (w, _, _) in enumerate(jobs):
                    sync.dma_start(raw[j][:, :, :], w.rearrange("(o p) c -> p o c", p=P)).then_inc(s_load, 16)
                sync.wait_ge(s_load, 16 * len(jobs))

            @block.tensor
            def _(pe):
                pe.wait_ge(s_load, 16 * len(jobs))
                for n, (j, o, c) in enumerate(blocks):
                    if n >= 2:
                        pe.wait_ge(s_out, n - 1)
                    pe.transpose(ps[n % 2][:, :], raw[j][:, o, c * P:(c + 1) * P], C.ident[:, :]).then_inc(s_turn, 1)

            @block.vector
            def _(dve):
                for n, (j, o, c) in enumerate(blocks):
                    target, factors = jobs[j][1][:, c, o * P:(o + 1) * P], jobs[j][2]
                    dve.wait_ge(s_turn, n + 1)
                    if factors is None:
                        dve.tensor_copy(target, ps[n % 2][:, :]).then_inc(s_out, 1)
                    else:
                        dve.tensor_tensor(target, ps[n % 2][:, :], factors[:, o * P:(o + 1) * P], ALU.mult).then_inc(s_out, 1)
                dve.wait_ge(s_out, len(blocks))


def attention_norm_phase(nc, dm, C, b_att, g, b, m, v, factor, offset):
    with ExitStack() as ctx:
        sp = Space(nc, ctx, "atn")
        par = sp.sb("par", [P, 5, D])
        s_par, s_var, s_root, s_link = sp.sem("par"), sp.sem("var"), sp.sem("root"), sp.sem("link")
        with nc.Block() as block:
            @block.sync
            def _(sync):
                for j, t in enumerate((b_att, g, b, m, v)):
                    sync.dma_start(par[:, j, :], t.rearrange("(a c) -> a c", a=1).to_broadcast([P, D])).then_inc(s_par, 16)
                sync.wait_ge(s_par, 80)

            @block.gpsimd
            def _(pool):
                pool.wait_ge(s_var, 1)
                pool.tensor_tensor(par[:, 4, :], par[:, 4, :], C.minus_half[:, 0:1].to_broadcast([P, D]), ALU.pow).then_inc(s_root, 1)

            @block.vector
            def _(dve):
                link = Link(dve, s_link)
                dve.wait_ge(s_par, 80)
                dve.tensor_scalar(par[:, 4, :], par[:, 4, :], BN_A_EPS, None, ALU.add).then_inc(s_var, 1)
                dve.wait_ge(s_root, 1)
                link(dve.tensor_tensor(factor[:, :], par[:, 4, :], par[:, 1, :], ALU.mult))
                link(dve.tensor_tensor(par[:, 0, :], par[:, 0, :], par[:, 3, :], ALU.subtract))
                link(dve.tensor_tensor(par[:, 0, :], par[:, 0, :], factor[:, :], ALU.mult))
                link(dve.tensor_tensor(offset[:, :], par[:, 0, :], par[:, 2, :], ALU.add))


def turn_rows(pe, C, src, c, bank, done):
    for k in range(T):
        ins = pe.transpose(bank[:, k * P:(k + 1) * P], src[:, k, c * P:(c + 1) * P], C.ident[:, :])
    ins.then_inc(done, 1)


def context_phase(nc, dm, C, raw, w_att, offset, ctx_dram):
    with ExitStack() as ctx:
        sp = Space(nc, ctx, "ctx")
        s_held = sp.sem("held")
        raw4 = [sp.sb(f"raw{s}", [P, T, D + 1]) for s in range(2)]
        inv = sp.sb("inv", [P, T])
        share = [sp.sb(f"share{s}", [P, T]) for s in range(2)]
        mean = [sp.sb(f"mean{s}", [P, T, D]) for s in range(2)]
        meanT = [sp.sb(f"meanT{s}", [P, KC, ROWS]) for s in range(2)]
        lin = [sp.sb(f"lin{s}", [P, T, D]) for s in range(2)]
        low = [sp.sb(f"low{s}", [P, T, D]) for s in range(2)]
        out = [sp.sb(f"out{s}", [P, T, D]) for s in range(2)]
        turn = [sp.ps(f"turn{c}", [P, ROWS]) for c in range(KC)]
        prod = [[sp.ps(f"prod{s}{j}", [P, 2, D]) for j in range(T // 2)] for s in range(2)]
        s_raw, s_st = sp.sems("raw"), sp.sems("st")
        s_share, s_link, s_mean, s_turn, s_meanT, s_prod, s_lin, s_low, s_exp, s_out = (sp.sem(n) for n in (
            "share", "link", "mean", "turn", "meanT", "prod", "lin", "low", "exp", "out"))
        with nc.Block() as block:
            @block.sync
            def _(sync):
                def load(g, s, u, is_tail):
                    if not first_group(g):
                        wait_alone(sync, s_mean, T * (g - 1), s_held)
                        wait_alone(sync, s_share, g - 1, s_held)
                    sync.dma_start(raw4[s][:, :, :], raw[bass.ds(g * ROWS, ROWS), :]
                                   .rearrange("(k p) c -> p k c", p=P)).then_inc(s_raw[s], 16)
                over_groups(sync, dm.EG, load)

            @block.vector
            def _(dve):
                def finish(g, s, u):
                    dve.wait_ge(s_exp, g + 1)
                    dve.wait_ge(s_st[s], 16 * u)
                    dve.scalar_tensor_tensor(out=out[s][:, :, :], in0=low[s][:, :, :], scalar=-1.0, in1=lin[s][:, :, :],
                                             op0=ALU.add, op1=ALU.max).then_inc(s_out, 1)

                def average(g, s, u):
                    link = Link(dve, s_link, 2 * g)
                    dve.wait_ge(s_raw[s], 16 * (u + 1))
                    link(dve.tensor_scalar(inv[:, :], raw4[s][:, :, D], 1e-8, None, ALU.add))
                    link(dve.reciprocal(inv[:, :], inv[:, :]))
                    if not first_group(g):
                        dve.wait_ge(s_turn, KC * (g - 1))
                    for k in range(T):
                        dve.tensor_scalar(mean[s][:, k, :], raw4[s][:, k, 0:D], inv[:, k:k + 1], None,
                                          ALU.mult).then_inc(s_mean, 1)
                    dve.tensor_tensor(share[s][:, :], raw4[s][:, :, D], inv[:, :], ALU.mult).then_inc(s_share, 1)
                    dve.wait_ge(s_share, g + 1)

                def linear(g, s):
                    if not (isinstance(g, int) and g < 2):
                        dve.wait_ge(s_out, g - 1)
                    for j in range(T // 2):
                        dve.wait_ge(s_prod, T // 2 * g + j + 1)
                        for k in (2 * j, 2 * j + 1):
                            dve.scalar_tensor_tensor(out=lin[s][:, k, :], in0=offset[:, :], scalar=share[s][:, k:k + 1],
                                                     in1=prod[s][j][:, k - 2 * j, :], op0=ALU.mult, op1=ALU.add).then_inc(s_lin, 1)
                    dve.wait_ge(s_lin, T * g + T)
                    dve.tensor_scalar(low[s][:, :, :], lin[s][:, :, :], 0.0, None, ALU.min).then_inc(s_low, 1)

                def step(g, s, u, is_tail):
                    average(g, s, u)
                    if not (isinstance(g, int) and g < 2):
                        linear(g - 2, s)
                    if not (isinstance(g, int) and g < 3):
                        finish(g - 3, 1 - s, u - 2 + s)
                over_groups(dve, dm.EG, step)
                last = dm.EG - 1
                linear(last - 1, (last - 1) % 2)
                finish(last - 2, last % 2, (last - 2) // 2)
                linear(last, last % 2)
                finish(last - 1, (last - 1) % 2, (last - 1) // 2)
                finish(last, last % 2, last // 2)

            @block.tensor
            def _(pe):
                def products(g, s):
                    pe.wait_ge(s_meanT, KC * g + KC)
                    if not first_group(g):
                        pe.wait_ge(s_lin, T * (g - 1))
                    for j in range(T // 2):
                        for k in (2 * j, 2 * j + 1):
                            for c in range(KC):
                                ins = pe.matmul(prod[s][j][:, k - 2 * j, :], meanT[s][:, c, k * P:(k + 1) * P],
                                                w_att[:, c, :], start=c == 0, stop=c == KC - 1)
                        ins.then_inc(s_prod, 1)

                def step(g, s, u, is_tail):
                    pe.wait_ge(s_mean, T * g + T)
                    for c in range(KC):
                        if not first_group(g):
                            pe.wait_ge(s_meanT, KC * (g - 1) + c + 1)
                        turn_rows(pe, C, mean[s], c, turn[c], s_turn)
                    if not first_group(g):
                        products(g - 1, 1 - s)
                over_groups(pe, dm.EG, step)
                products(dm.EG - 1, (dm.EG - 1) % 2)

            @block.scalar
            def _(act):
                def exps(g, s):
                    act.wait_ge(s_low, g + 1)
                    act.activation(low[s][:, :, :], low[s][:, :, :], ACT.Exp).then_inc(s_exp, 1)

                def step(g, s, u, is_tail):
                    for c in range(KC):
                        act.wait_ge(s_turn, KC * g + c + 1)
                        if not (isinstance(g, int) and g < 2):
                            act.wait_ge(s_prod, T // 2 * (g - 1))
                        act.copy(meanT[s][:, c, :], turn[c][:, :]).then_inc(s_meanT, 1)
                    if not (isinstance(g, int) and g < 2):
                        exps(g - 2, s)
                over_groups(act, dm.EG, step)
                exps(dm.EG - 2, (dm.EG - 2) % 2)
                exps(dm.EG - 1, (dm.EG - 1) % 2)

            @block.gpsimd
            def _(pool):
                def store(g, s, u, is_tail):
                    wait_alone(pool, s_out, g + 1, s_held)
                    pool.dma_start(ctx_dram[bass.ds(g * ROWS, ROWS), :].rearrange("(k p) c -> p k c", p=P),
                                   out[s][:, :, :]).then_inc(s_st[s], 16)
                over_groups(pool, dm.EG, store)
                for s in range(2):
                    pool.wait_ge(s_st[s], 16 * uses(dm.EG, s))



def gather_rows(pool, dm, edges, rows_in, node4, at, g, s, u, s_zero, s_copy, s_rows, s_held):
    pool.memset(node4[s][:, :, :], 0.0).then_inc(s_zero[s], 1)
    pool.tensor_copy(at[s][:, :], edges.last[:, bass.ds(T * g, T)]).then_inc(s_copy[s], 1)
    wait_alone(pool, s_zero[s], u + 1, s_held)
    wait_alone(pool, s_copy[s], u + 1, s_held)
    for k in range(T):
        pool.indirect_dma_start(node4[s][:, k, :], None, rows_in,
                                bass.IndirectOffsetOnAxis(ap=at[s][:, k:k + 1], axis=0),
                                bounds_check=dm.EPAD - 1, oob_is_err=False).then_inc(s_rows[s], 16)



def gru_phase(nc, dm, C, edges, x, h, ctx_dram, w_ih, w_hh, b_ih, b_hh, x1, h1, sums):
    NG = dm.NG
    with ExitStack() as ctx:
        sp = Space(nc, ctx, "gru")
        s_held = sp.sem("held")
        h4, x4, c4, y4, g4 = ([sp.sb(f"{n}{s}", [P, T, D]) for s in range(2)] for n in ("h", "x", "c", "y", "g"))
        at = [sp.sb(f"at{s}", [P, T], I32) for s in range(2)]
        hT, cT, upd = ([sp.sb(f"{n}{s}", [P, KC, ROWS]) for s in range(2)] for n in ("hT", "cT", "upd"))
        h_up, h_low, c_up, c_low = ([sp.sb(f"{n}{s}", [P, KC, ROWS], ONE_PASS) for s in range(2)]
                                    for n in ("h_up", "h_low", "c_up", "c_low"))
        tr, tz, hn, pre, new = ([sp.sb(f"{n}{c}", [P, ROWS]) for c in range(KC)] for n in ("tr", "tz", "hn", "pre", "new"))
        sq = sp.sb("sq", [P, T, D])
        acc = sp.sb("acc", [P, 2, T, D])
        stats, mv = sp.sb("stats", [P, T, 6]), sp.sb("mv", [P, T, 2])
        rstd = [sp.sb(f"rstd{s}", [P, T]) for s in range(2)]
        shift = [sp.sb(f"shift{s}", [P, T]) for s in range(2)]
        bias = sp.sb("bias", [P, 2, 6])
        half = sp.sb("half", [P, 6])
        p_r, p_z, p_hn, p_in = (sp.ps(n, [P, ROWS]) for n in ("r", "z", "hn", "in"))
        ring = [sp.ps(f"ring{j}", [P, ROWS]) for j in range(3)]
        sum_ps = sp.ps("sum", [P, 4])
        s_h, s_x, s_zero, s_c, s_at, s_x1, s_h1 = (sp.sems(n) for n in ("h", "x", "zero", "c", "at", "x1", "h1"))
        (s_par, s_bias, s_turn, s_turned, s_back, s_r, s_z, s_hn, s_in, s_tr, s_tz, s_hnb, s_pre, s_new, s_dif,
         s_upd, s_y, s_link, s_var, s_rstd, s_shift, s_g, s_acc, s_sum, s_zeroed, s_split) = (sp.sem(n) for n in (
             "par", "bias", "turn", "turned", "back", "r", "z", "hn", "in", "tr", "tz", "hnb", "pre", "new", "dif",
             "upd", "y", "link", "var", "rstd", "shift", "g", "acc", "sum", "zeroed", "split"))
        with nc.Block() as block:
            @block.sync
            def _(sync):
                with nc.allow_non_contiguous_dma(reason="bias vectors by feature"):
                    for j, b in enumerate((b_ih, b_hh)):
                        sync.dma_start(bias[:, j, :], b.rearrange("(j p) -> p j", p=P)).then_inc(s_par, 16)

                def load_x(g, s, is_tail):
                    if not first_group(g):
                        wait_alone(sync, s_y, 2 * (g - 1), s_held)
                    rows_dma(sync, x, x4[s], g, dm, is_tail, s_x[s])

                def load(g, s, u, is_tail):
                    if not first_group(g):
                        wait_alone(sync, s_turn, 4 * (g - 1), s_held)
                    rows_dma(sync, h, h4[s], g, dm, is_tail, s_h[s])
                    if not first_group(g):
                        load_x(g - 1, 1 - s, False)
                over_groups(sync, dm.FULL, load, tail=True)
                load_x(NG - 1, (NG - 1) % 2, True)

            @block.gpsimd
            def _(pool):
                for j in range(2):
                    pool.memset(acc[:, j, :, :], 0.0).then_inc(s_zeroed, 1)
                pool.wait_ge(s_zeroed, 2)

                def fetch(g, s, u):
                    if not first_group(g):
                        wait_alone(pool, s_turn, 4 * (g - 1), s_held)
                    gather_rows(pool, dm, edges, ctx_dram, c4, at, g, s, u, s_zero, s_at, s_c, s_held)

                def after(g, s, is_tail):
                    wait_alone(pool, s_var, g + 1, s_held)
                    pool.tensor_tensor(rstd[s][:, :], rstd[s][:, :], C.minus_half[:, :], ALU.pow).then_inc(s_rstd, 1)
                    wait_alone(pool, s_g, g + 1, s_held)
                    parts = parts_of(dm, is_tail)
                    for a, b, rows in parts:
                        src = g4[s][0:rows, a:b, :]
                        pool.tensor_tensor(sq[0:rows, a:b, :], src, src, ALU.mult).then_inc(s_acc, 1)
                        pool.tensor_tensor(acc[0:rows, 0, a:b, :], acc[0:rows, 0, a:b, :], src, ALU.add).then_inc(s_acc, 1)
                    wait_alone(pool, s_acc, 3 * g + 2 * len(parts), s_held)
                    for a, b, rows in parts:
                        pool.tensor_tensor(acc[0:rows, 1, a:b, :], acc[0:rows, 1, a:b, :], sq[0:rows, a:b, :],
                                           ALU.add).then_inc(s_acc, 1)
                    wait_alone(pool, s_acc, 3 * g + 3 * len(parts), s_held)

                fetch(0, 0, 0)
                def step(g, s, u, is_tail):
                    if not is_tail:
                        fetch(g + 1, 1 - s, u + s)
                    if not first_group(g):
                        after(g - 1, 1 - s, False)
                over_groups(pool, dm.FULL, step, tail=True)
                after(NG - 1, (NG - 1) % 2, True)

            @block.tensor
            def _(pe):
                def gates(g, s, c):
                    def product(bank, j, pairs, free, done):
                        if c or not first_group(g):
                            pe.wait_ge(free, KC * g + c)
                        n = len(pairs) * KC
                        for a, (w, v) in enumerate(pairs):
                            for k in range(KC):
                                ins = split_products(pe, bank[:, :], [part[:, k, j * P:(j + 1) * P] for part in w],
                                                     [part[s][:, k, :] for part in v], a * KC + k == 0,
                                                     a * KC + k == n - 1)
                        ins.then_inc(done, 1)
                    of_h, of_c = (w_hh, (h_up, h_low)), (w_ih, (c_up, c_low))
                    product(p_r, c, [of_h, of_c], s_tr, s_r)
                    product(p_z, KC + c, [of_h, of_c], s_tz, s_z)
                    product(p_hn, 2 * KC + c, [of_h], s_hnb, s_hn)
                    product(p_in, 2 * KC + c, [of_c], s_pre, s_in)

                def turn(g, s, u):
                    early = isinstance(g, int) and g < 2
                    pe.wait_ge(s_h[s], 32 * (u + 1))
                    if not first_group(g):
                        pe.wait_ge(s_turned, 4 * g)
                    turn_rows(pe, C, h4[s], 0, ring[0], s_turn)
                    if not early:
                        pe.wait_ge(s_y, 2 * g - 3)
                    turn_rows(pe, C, h4[s], 1, ring[1], s_turn)
                    pe.wait_ge(s_c[s], 16 * T * (u + 1))
                    if not early:
                        pe.wait_ge(s_y, 2 * g - 2)
                    turn_rows(pe, C, c4[s], 0, ring[2], s_turn)
                    pe.wait_ge(s_turned, 4 * g + 1)
                    turn_rows(pe, C, c4[s], 1, ring[0], s_turn)

                def back(g, s, later):
                    pe.wait_ge(s_upd, KC * g + KC)
                    for j in range(2):
                        if later is not None:
                            pe.wait_ge(s_turned, later + j)
                        else:
                            pe.wait_ge(s_y, 2 * g - 1 + j)
                        for k in (0, 1):
                            for c in range(KC):
                                ins = pe.transpose(ring[1 + j][:, k * D + c * P:k * D + (c + 1) * P],
                                                   upd[s][:, c, (2 * j + k) * P:(2 * j + k + 1) * P], C.ident[:, :])
                        ins.then_inc(s_back, 1)

                turn(0, 0, 0)
                def step(g, s, u, is_tail):
                    pe.wait_ge(s_split, 4 * g + 4)
                    gates(g, s, 0)
                    if not first_group(g):
                        back(g - 1, 1 - s, 4 * g + 2)
                    if not is_tail:
                        turn(g + 1, 1 - s, u + s)
                    gates(g, s, 1)
                over_groups(pe, dm.FULL, step, tail=True)
                back(NG - 1, (NG - 1) % 2, None)
                pe.wait_ge(s_acc, 3 * NG + 3)
                for j in range(2):
                    for c in range(KC):
                        for t in range(T):
                            ins = pe.matmul(sum_ps[:, 2 * j + c:2 * j + c + 1], acc[:, j, t, c * P:(c + 1) * P],
                                            C.ones[:, 0:1], start=t == 0, stop=t == T - 1)
                        ins.then_inc(s_sum, 1)

            @block.scalar
            def _(act):
                def turned(g, s):
                    if not first_group(g):
                        act.wait_ge(s_split, 4 * (g - 1))
                        act.wait_ge(s_dif, KC * (g - 1))
                    for j, (dst, c) in enumerate(((hT, 0), (hT, 1), (cT, 0), (cT, 1))):
                        act.wait_ge(s_turn, 4 * g + j + 1)
                        act.copy(dst[s][:, c, :], ring[j % 3][:, :]).then_inc(s_turned, 1)

                def gates(g, s, c):
                    again = not first_group(g)
                    act.wait_ge(s_r, KC * g + c + 1)
                    if again:
                        act.wait_ge(s_pre, KC * (g - 1) + c + 1)
                    act.activation(tr[c][:, :], p_r[:, :], ACT.Tanh, bias=half[:, c:c + 1], scale=0.5).then_inc(s_tr, 1)
                    act.wait_ge(s_z, KC * g + c + 1)
                    if again:
                        act.wait_ge(s_upd, KC * (g - 1) + c + 1)
                    act.activation(tz[c][:, :], p_z[:, :], ACT.Tanh, bias=half[:, KC + c:KC + c + 1], scale=0.5).then_inc(s_tz, 1)
                    act.wait_ge(s_hn, KC * g + c + 1)
                    act.activation(hn[c][:, :], p_hn[:, :], ACT.Identity, bias=half[:, 2 * KC + c:2 * KC + c + 1],
                                   scale=0.5).then_inc(s_hnb, 1)

                def candidate(g, s, c):
                    act.wait_ge(s_pre, KC * g + c + 1)
                    act.activation(new[c][:, :], pre[c][:, :], ACT.Tanh, bias=bias[:, 0, 2 * KC + c:2 * KC + c + 1]).then_inc(s_new, 1)

                def norm(g, s, u, is_tail):
                    act.wait_ge(s_y, 2 * g + 2)
                    rows_dma(act, x1, y4[s], g, dm, is_tail, s_x1[s], store=True)
                    act.wait_ge(s_shift, g + 1)
                    act.wait_ge(s_h1[s], 32 * u)
                    if not first_group(g):
                        act.wait_ge(s_acc, 3 * (g - 1))
                    for k in range(T):
                        ins = act.activation(g4[s][:, k, :], y4[s][:, k, :], ACT.Relu,
                                             bias=shift[s][:, k:k + 1], scale=rstd[s][:, k:k + 1])
                    ins.then_inc(s_g, 1)
                    act.wait_ge(s_g, g + 1)
                    rows_dma(act, h1, g4[s], g, dm, is_tail, s_h1[s], store=True)

                act.wait_ge(s_bias, 2)
                turned(0, 0)
                def step(g, s, u, is_tail):
                    gates(g, s, 0)
                    if not is_tail:
                        turned(g + 1, 1 - s)
                    candidate(g, s, 0)
                    if not first_group(g):
                        norm(g - 1, 1 - s, u - 1 + s, False)
                    gates(g, s, 1)
                    candidate(g, s, 1)
                over_groups(act, dm.FULL, step, tail=True)
                norm(NG - 1, (NG - 1) % 2, (NG - 1) // 2, True)
                for s in range(2):
                    act.wait_ge(s_x1[s], 32 * uses(NG, s))
                    act.wait_ge(s_h1[s], 32 * uses(NG, s))

            @block.vector
            def _(dve):
                LINKS = 2 * KC + 2 * T
                def prepare(g, c, link):
                    dve.wait_ge(s_hnb, KC * g + c + 1)
                    dve.wait_ge(s_tr, KC * g + c + 1)
                    if not first_group(g):
                        dve.wait_ge(s_new, KC * (g - 1) + c + 1)
                    link(dve.scalar_tensor_tensor(out=pre[c][:, :], in0=tr[c][:, :], scalar=1.0, in1=hn[c][:, :],
                                                  op0=ALU.add, op1=ALU.mult))
                    dve.wait_ge(s_in, KC * g + c + 1)
                    dve.tensor_tensor(pre[c][:, :], pre[c][:, :], p_in[:, :], ALU.add).then_inc(s_pre, 1)

                def split(g, s):
                    if not first_group(g):
                        dve.wait_ge(s_in, KC * (g - 1))
                    dve.wait_ge(s_turned, 4 * g + 2)
                    split_upper(dve, h_up[s][:, :, :], hT[s][:, :, :]).then_inc(s_split, 1)
                    dve.wait_ge(s_turned, 4 * g + 4)
                    split_upper(dve, c_up[s][:, :, :], cT[s][:, :, :]).then_inc(s_split, 1)
                    dve.wait_ge(s_split, 4 * g + 1)
                    split_lower(dve, h_low[s][:, :, :], hT[s][:, :, :], h_up[s][:, :, :]).then_inc(s_split, 1)
                    dve.wait_ge(s_split, 4 * g + 2)
                    split_lower(dve, c_low[s][:, :, :], cT[s][:, :, :], c_up[s][:, :, :]).then_inc(s_split, 1)

                def update(g, s, c, link):
                    dve.wait_ge(s_new, KC * g + c + 1)
                    dve.tensor_tensor(hn[c][:, :], hT[s][:, c, :], new[c][:, :], ALU.subtract).then_inc(s_dif, 1)
                    dve.wait_ge(s_dif, KC * g + c + 1)
                    dve.wait_ge(s_tz, KC * g + c + 1)
                    link(dve.scalar_tensor_tensor(out=hn[c][:, :], in0=tz[c][:, :], scalar=1.0, in1=hn[c][:, :],
                                                  op0=ALU.add, op1=ALU.mult))
                    if not first_group(g):
                        dve.wait_ge(s_back, 2 * (g - 1))
                    dve.scalar_tensor_tensor(out=upd[s][:, c, :], in0=hn[c][:, :], scalar=0.5, in1=new[c][:, :],
                                             op0=ALU.mult, op1=ALU.add).then_inc(s_upd, 1)

                def finish(g, s, u, link):
                    dve.wait_ge(s_x[s], 32 * (u + 1))
                    dve.wait_ge(s_x1[s], 32 * u)
                    if not first_group(g):
                        dve.wait_ge(s_g, g - 1)
                    for j in range(2):
                        dve.wait_ge(s_back, 2 * g + j + 1)
                        dve.tensor_tensor(y4[s][:, 2 * j:2 * j + 2, :], x4[s][:, 2 * j:2 * j + 2, :],
                                          ring[1 + j][:, :].rearrange("p (k c) -> p k c", k=2), ALU.add).then_inc(s_y, 1)
                    dve.wait_ge(s_y, 2 * g + 2)
                    norm_stats(dve, link, y4[s], stats, mv, s_held)
                    dve.tensor_scalar(rstd[s][:, :], mv[:, :, 1], LN_EPS, None, ALU.add).then_inc(s_var, 1)
                    dve.wait_ge(s_rstd, g + 1)
                    dve.scalar_tensor_tensor(out=shift[s][:, :], in0=mv[:, :, 0], scalar=-1.0, in1=rstd[s][:, :],
                                             op0=ALU.mult, op1=ALU.mult).then_inc(s_shift, 1)
                    dve.wait_ge(s_shift, g + 1)

                dve.wait_ge(s_par, 32)
                dve.tensor_tensor(half[:, :], bias[:, 0, :], bias[:, 1, :], ALU.add).then_inc(s_bias, 1)
                dve.wait_ge(s_bias, 1)
                dve.tensor_copy(half[:, 2 * KC:3 * KC], bias[:, 1, 2 * KC:3 * KC]).then_inc(s_link, 1)
                dve.wait_ge(s_link, 1)
                dve.tensor_scalar(half[:, :], half[:, :], 0.5, None, ALU.mult).then_inc(s_bias, 1)

                split(0, 0)
                def step(g, s, u, is_tail):
                    link = Link(dve, s_link, 1 if first_group(g) else 1 + 2 * KC + LINKS * (g - 1))
                    prepare(g, 0, link)
                    if not first_group(g):
                        finish(g - 1, 1 - s, u - 1 + s, link)
                    update(g, s, 0, link)
                    if not is_tail:
                        split(g + 1, 1 - s)
                    prepare(g, 1, link)
                    update(g, s, 1, link)
                over_groups(dve, dm.FULL, step, tail=True)
                finish(NG - 1, (NG - 1) % 2, (NG - 1) // 2, Link(dve, s_link, 1 + 2 * KC + LINKS * (NG - 1)))
                dve.wait_ge(s_sum, 2 * KC)
                dve.tensor_copy(sums[:, :], sum_ps[:, :])



def first_norm_phase(nc, dm, C, sums, gamma, beta, w, count, coef, lift, deg_dram):
    with ExitStack() as ctx:
        sp = Space(nc, ctx, "bn0")
        par = sp.sb("par", [P, 2, KC])
        tmp = sp.sb("tmp", [P, 3, KC])
        TQ = dm.AC // T
        deg = sp.sb("deg", [P, dm.AC])
        degT = sp.sb("degT", [TQ, T, P])
        ps = sp.ps("ps", [P, KC])
        turned = sp.ps("turned", [P, T, P])
        s_par, s_link, s_var, s_root, s_coef, s_lift, s_deg, s_turn, s_degT, s_st = (sp.sem(n) for n in (
            "par", "link", "var", "root", "coef", "lift", "deg", "turn", "degT", "st"))
        with nc.Block() as block:
            @block.sync
            def _(sync):
                with nc.allow_non_contiguous_dma(reason="vectors by feature"):
                    for j, v in enumerate((gamma, beta)):
                        sync.dma_start(par[:, j, :], v.rearrange("(c p) -> p c", p=P)).then_inc(s_par, 16)
                sync.wait_ge(s_par, 32)
                sync.wait_ge(s_degT, 1)
                sync.dma_start(deg_dram.rearrange("(t q p) -> q t p", q=TQ, p=P), degT[:, :, :]).then_inc(s_st, 16)
                sync.wait_ge(s_st, 16)

            @block.vector
            def _(dve):
                link = Link(dve, s_link)
                dve.tensor_scalar(deg[:, :], count[:, :], 1.0, None, ALU.add).then_inc(s_deg, 1)
                dve.wait_ge(s_par, 32)
                link(dve.tensor_scalar(tmp[:, 0:2, :].rearrange("p a c -> p (a c)"), sums[:, :], 1.0 / dm.N, None, ALU.mult))
                link(dve.tensor_tensor(tmp[:, 2, :], tmp[:, 0, :], tmp[:, 0, :], ALU.mult))
                link(dve.tensor_tensor(tmp[:, 1, :], tmp[:, 1, :], tmp[:, 2, :], ALU.subtract))
                dve.tensor_scalar(tmp[:, 1, :], tmp[:, 1, :], 0.0, BN_B_EPS, ALU.max, ALU.add).then_inc(s_var, 1)
                dve.wait_ge(s_root, 1)
                scale_shift(dve, link, tmp[:, 1, :], tmp[:, 0, :], tmp[:, 2, :], par, coef, s_coef)
                dve.wait_ge(s_lift, 1)
                link(dve.tensor_copy(lift[:, :], ps[:, :]))
                dve.wait_ge(s_turn, T)
                dve.tensor_copy(degT[:, :, :], turned[0:TQ, :, :]).then_inc(s_degT, 1)

            @block.gpsimd
            def _(pool):
                pool.wait_ge(s_var, 1)
                pool.tensor_tensor(tmp[:, 1, :], tmp[:, 1, :], C.minus_half[:, 0:KC], ALU.pow).then_inc(s_root, 1)

            @block.tensor
            def _(pe):
                pe.wait_ge(s_deg, 1)
                for t in range(T):
                    pe.transpose(turned[0:TQ, t, :], deg[:, t * TQ:(t + 1) * TQ], C.ident[:, :]).then_inc(s_turn, 1)
                pe.wait_ge(s_coef, 1)
                for o in range(KC):
                    for k in range(KC):
                        ins = pe.matmul(ps[:, o:o + 1], w[:, k, o * P:(o + 1) * P], coef[:, 1, k:k + 1],
                                        start=k == 0, stop=k == KC - 1)
                ins.then_inc(s_lift, 1)


def scale_shift(dve, link, rstd, mean, spare, par, coef, done):
    link(dve.tensor_tensor(coef[:, 0, :], rstd, par[:, 0, :], ALU.mult))
    link(dve.tensor_tensor(spare, mean, coef[:, 0, :], ALU.mult))
    dve.tensor_tensor(coef[:, 1, :], par[:, 1, :], spare, ALU.subtract).then_inc(done, 1)


def gin_in_phase(nc, dm, C, edges, rows_in, raw, w, bias, scale, lift, deg_dram, yT, gamma, beta, coef, tag):
    NG = dm.NG
    with ExitStack() as ctx:
        sp = Space(nc, ctx, tag)
        s_held = sp.sem("held")
        r4, a4, sum4 = ([sp.sb(f"{n}{s}", [P, T, D]) for s in range(2)] for n in ("r", "a", "sum"))
        at = [sp.sb(f"at{s}", [P, T], I32) for s in range(2)]
        deg = [sp.sb(f"deg{s}", [P, ROWS]) for s in range(2)]
        sumT = [sp.sb(f"sumT{s}", [P, KC, ROWS]) for s in range(2)]
        lin = [sp.sb(f"lin{s}", [P, KC, ROWS]) for s in range(2)]
        y = [sp.sb(f"y{s}", [P, KC, ROWS]) for s in range(2)] if lift is not None else lin
        stats = sp.sb("stats", [P, KC, NG, 6])
        stats_now = [sp.sb(f"stats_now{s}", [P, KC, 6]) for s in range(2)]
        mv = sp.sb("mv", [P, KC, 2])
        par = sp.sb("par", [P, 3, KC])
        root = sp.sb("root", [P, 2, KC])
        turn = [sp.ps(f"turn{c}", [P, ROWS]) for c in range(KC)]
        prod = [[sp.ps(f"prod{s}{c}", [P, ROWS]) for c in range(KC)] for s in range(2)]
        s_r, s_zero, s_a, s_at, s_deg, s_y = (sp.sems(n) for n in ("r", "zero", "a", "at", "deg", "y"))
        s_par, s_sum, s_turn, s_turned, s_prod, s_lin, s_lift, s_st, s_mv, s_var, s_root, s_coef, s_link, s_mean = (
            sp.sem(n) for n in ("par", "sum", "turn", "turned", "prod", "lin", "lift", "st", "mv", "var", "root",
                                "coef", "link", "mean"))
        done = s_lift if lift is not None else s_lin
        with nc.Block() as block:
            @block.sync
            def _(sync):
                with nc.allow_non_contiguous_dma(reason="vectors by feature"):
                    for j, v in enumerate((gamma, beta, bias)):
                        sync.dma_start(par[:, j, :], v.rearrange("(c p) -> p c", p=P)).then_inc(s_par, 16)
                sync.wait_ge(s_par, 48)

                def move(g, s, u, is_tail):
                    if not first_group(g):
                        wait_alone(sync, s_sum, g - 1, s_held)
                    rows_dma(sync, rows_in, r4[s], g, dm, is_tail, s_r[s])
                    if lift is not None and not first_group(g):
                        load_deg(g - 1, 1 - s)

                def load_deg(g, s):
                    if not first_group(g):
                        wait_alone(sync, s_lift, KC * (g - 1), s_held)
                    sync.dma_start(deg[s][:, :], deg_dram[bass.ds(g * ROWS, ROWS)].rearrange("(a n) -> a n", a=1)
                                   .to_broadcast([P, ROWS])).then_inc(s_deg[s], 16)
                over_groups(sync, dm.FULL, move, tail=True)
                if lift is not None:
                    load_deg(NG - 1, (NG - 1) % 2)

            @block.gpsimd
            def _(pool):
                def fetch(g, s, u, is_tail):
                    if not first_group(g):
                        wait_alone(pool, s_sum, g - 1, s_held)
                    gather_rows(pool, dm, edges, raw, a4, at, g, s, u, s_zero, s_at, s_a, s_held)
                over_groups(pool, dm.FULL, fetch, tail=True)
                pool.wait_ge(s_var, 1)
                pool.tensor_tensor(root[:, 0, :], root[:, 0, :], C.minus_half[:, 0:KC], ALU.pow).then_inc(s_root, 1)

            @block.tensor
            def _(pe):
                def products(g, s):
                    pe.wait_ge(s_turned, KC * g + KC)
                    for o in range(KC):
                        if not first_group(g):
                            pe.wait_ge(s_lin, KC * (g - 1))
                        for k in range(KC):
                            ins = pe.matmul(prod[s][o][:, :], w[:, k, o * P:(o + 1) * P], sumT[s][:, k, :],
                                            start=k == 0, stop=k == KC - 1)
                        ins.then_inc(s_prod, 1)

                def step(g, s, u, is_tail):
                    pe.wait_ge(s_sum, g + 1)
                    for c in range(KC):
                        if not first_group(g):
                            pe.wait_ge(s_turned, KC * (g - 1) + c + 1)
                        turn_rows(pe, C, sum4[s], c, turn[c], s_turn)
                    if not first_group(g):
                        products(g - 1, 1 - s)
                over_groups(pe, dm.FULL, step, tail=True)
                products(NG - 1, (NG - 1) % 2)

            @block.scalar
            def _(act):
                act.wait_ge(s_par, 48)
                def store(g, s, is_tail):
                    n = dm.N - dm.FULL * ROWS if is_tail else ROWS
                    act.wait_ge(done, KC * g + KC)
                    act.dma_start(yT[:, bass.ds(g * ROWS, n)].rearrange("(c p) n -> p c n", p=P),
                                  y[s][:, :, 0:n]).then_inc(s_y[s], 16)

                def linear(g, s, u):
                    act.wait_ge(s_y[s], 16 * u)
                    for o in range(KC):
                        act.wait_ge(s_prod, KC * g + o + 1)
                        if not first_group(g):
                            act.wait_ge(s_mean, KC * (g - 1))
                        act.activation(lin[s][:, o, :], prod[s][o][:, :], ACT.Identity, bias=par[:, 2, o:o + 1]).then_inc(s_lin, 1)

                def step(g, s, u, is_tail):
                    for c in range(KC):
                        act.wait_ge(s_turn, KC * g + c + 1)
                        if not first_group(g):
                            act.wait_ge(s_prod, KC * (g - 1))
                        if scale is None:
                            act.copy(sumT[s][:, c, :], turn[c][:, :]).then_inc(s_turned, 1)
                        else:
                            act.activation(sumT[s][:, c, :], turn[c][:, :], ACT.Copy, scale=scale[:, 0, c:c + 1]).then_inc(s_turned, 1)
                    if not first_group(g):
                        linear(g - 1, 1 - s, u - 1 + s)
                    if not (isinstance(g, int) and g < 2):
                        store(g - 2, s, False)
                over_groups(act, dm.FULL, step, tail=True)
                linear(NG - 1, (NG - 1) % 2, (NG - 1) // 2)
                store(NG - 2, (NG - 2) % 2, False)
                store(NG - 1, (NG - 1) % 2, True)
                for s in range(2):
                    act.wait_ge(s_y[s], 16 * uses(NG, s))

            @block.vector
            def _(dve):
                def finish(g, s, u, is_tail):
                    n = dm.N - dm.FULL * ROWS if is_tail else ROWS
                    if lift is not None:
                        dve.wait_ge(s_deg[s], 16 * (u + 1))
                        dve.wait_ge(s_y[s], 16 * u)
                        for o in range(KC):
                            dve.wait_ge(s_lin, KC * g + o + 1)
                            dve.scalar_tensor_tensor(out=y[s][:, o, :], in0=deg[s][:, :], scalar=lift[:, o:o + 1],
                                                     in1=lin[s][:, o, :], op0=ALU.mult, op1=ALU.add).then_inc(s_lift, 1)
                    for o in range(KC):
                        dve.wait_ge(done, KC * g + o + 1)
                        dve.bn_stats(stats_now[s][:, o, :], y[s][:, o, 0:n]).then_inc(s_mean, 1)
                    dve.wait_ge(s_mean, KC * g + KC)
                    dve.tensor_copy(stats[:, :, bass.ds(g, 1), :].rearrange("p c g n -> p c (g n)"), stats_now[s][:, :, :]).then_inc(s_mv, 1)

                def step(g, s, u, is_tail):
                    dve.wait_ge(s_r[s], 32 * (u + 1))
                    dve.wait_ge(s_a[s], 16 * T * (u + 1))
                    if not first_group(g):
                        dve.wait_ge(s_turn, KC * (g - 1))
                    dve.tensor_tensor(sum4[s][:, :, :], r4[s][:, :, :], a4[s][:, :, :], ALU.add).then_inc(s_sum, 1)
                    if not (isinstance(g, int) and g < 2):
                        finish(g - 2, s, u - 1, False)
                over_groups(dve, dm.FULL, step, tail=True)
                finish(NG - 2, (NG - 2) % 2, (NG - 2) // 2, False)
                finish(NG - 1, (NG - 1) % 2, (NG - 1) // 2, True)
                dve.wait_ge(s_mv, NG)
                link = Link(dve, s_link)
                for o in range(KC):
                    link(dve.bn_aggr(mv[:, o, :], stats[:, o, :, :].rearrange("p g c -> p (g c)")))
                dve.tensor_scalar(root[:, 0, :], mv[:, :, 1], BN_B_EPS, None, ALU.add).then_inc(s_var, 1)
                dve.wait_ge(s_root, 1)
                scale_shift(dve, link, root[:, 0, :], mv[:, :, 0], root[:, 1, :], par, coef, s_coef)
                dve.wait_ge(s_coef, 1)


def gin_out_phase(nc, dm, C, yT, coef, w, bias, x1, out, tag):
    NG = dm.NG
    with ExitStack() as ctx:
        sp = Space(nc, ctx, tag)
        s_held = sp.sem("held")
        yt, aT = ([sp.sb(f"{n}{s}", [P, KC, ROWS]) for s in range(2)] for n in ("yt", "aT"))
        lin, o4 = ([sp.sb(f"{n}{s}", [P, T, D]) for s in range(2)] for n in ("lin", "o"))
        x4 = [sp.sb(f"x{s}", [P, T, D]) for s in range(2)] if x1 is not None else None
        wide = sp.sb("wide", [P, 2, D])
        prod = [[sp.ps(f"prod{s}{j}", [P, 2, D]) for j in range(2)] for s in range(2)]
        s_yt, s_x, s_st = sp.sems("yt"), sp.sems("x"), sp.sems("st")
        s_w, s_aT, s_prod, s_lin, s_o = (sp.sem(n) for n in ("w", "aT", "prod", "lin", "o"))
        with nc.Block() as block:
            @block.sync
            def _(sync):
                for j in range(2):
                    sync.dma_start(wide[:, j, :], bias.rearrange("(a c) -> a c", a=1).to_broadcast([P, D])).then_inc(s_w, 16)

                def move(g, s, u, is_tail):
                    n = dm.N - dm.FULL * ROWS if is_tail else ROWS
                    if not first_group(g):
                        wait_alone(sync, s_aT, KC * (g - 1), s_held)
                    sync.dma_start(yt[s][:, :, 0:n], yT[:, bass.ds(g * ROWS, n)]
                                   .rearrange("(c p) n -> p c n", p=P)).then_inc(s_yt[s], 16)
                    if x1 is not None:
                        if not first_group(g):
                            wait_alone(sync, s_o, g - 1, s_held)
                        rows_dma(sync, x1, x4[s], g, dm, is_tail, s_x[s])
                over_groups(sync, dm.FULL, move, tail=True)

            @block.gpsimd
            def _(pool):
                def store(g, s, u, is_tail):
                    wait_alone(pool, s_o, g + 1, s_held)
                    rows_dma(pool, out, o4[s], g, dm, is_tail, s_st[s], store=True)
                over_groups(pool, dm.FULL, store, tail=True)
                for s in range(2):
                    pool.wait_ge(s_st[s], 32 * uses(NG, s))

            @block.scalar
            def _(act):
                def relu(g, s, u):
                    act.wait_ge(s_lin, 2 * g + 2)
                    act.wait_ge(s_st[s], 32 * u)
                    act.activation(o4[s][:, :, :], lin[s][:, :, :], ACT.Relu).then_inc(s_o, 1)

                def step(g, s, u, is_tail):
                    act.wait_ge(s_yt[s], 16 * (u + 1))
                    if not first_group(g):
                        act.wait_ge(s_prod, 2 * (g - 1))
                    for c in range(KC):
                        act.activation(aT[s][:, c, :], yt[s][:, c, :], ACT.Relu, bias=coef[:, 1, c:c + 1],
                                       scale=coef[:, 0, c:c + 1]).then_inc(s_aT, 1)
                    if x1 is None and not first_group(g):
                        relu(g - 1, 1 - s, u - 1 + s)
                over_groups(act, dm.FULL, step, tail=True)
                if x1 is None:
                    relu(NG - 1, (NG - 1) % 2, (NG - 1) // 2)

            @block.tensor
            def _(pe):
                def step(g, s, u, is_tail):
                    pe.wait_ge(s_aT, KC * g + KC)
                    for j in range(2):
                        if not first_group(g):
                            pe.wait_ge(s_lin, 2 * (g - 1))
                        for k in range(2):
                            for c in range(KC):
                                ins = pe.matmul(prod[s][j][:, k, :], aT[s][:, c, (2 * j + k) * P:(2 * j + k + 1) * P],
                                                w[:, c, :], start=c == 0, stop=c == KC - 1)
                        ins.then_inc(s_prod, 1)
                over_groups(pe, dm.FULL, step, tail=True)

            @block.vector
            def _(dve):
                dve.wait_ge(s_w, 32)
                def step(g, s, u, is_tail):
                    if x1 is None and not first_group(g):
                        dve.wait_ge(s_o, g - 1)
                    for j in range(2):
                        dve.wait_ge(s_prod, 2 * g + j + 1)
                        dve.tensor_tensor(lin[s][:, 2 * j:2 * j + 2, :], prod[s][j][:, :, :], wide[:, :, :],
                                          ALU.add).then_inc(s_lin, 1)
                    if x1 is not None:
                        dve.wait_ge(s_lin, 2 * g + 2)
                        dve.wait_ge(s_x[s], 32 * (u + 1))
                        dve.wait_ge(s_st[s], 32 * u)
                        dve.scalar_tensor_tensor(out=o4[s][:, :, :], in0=lin[s][:, :, :], scalar=0.0,
                                                 in1=x4[s][:, :, :], op0=ALU.max, op1=ALU.add).then_inc(s_o, 1)
                over_groups(dve, dm.FULL, step, tail=True)



class Edges:

    def __init__(self, sp, nc, dm, name):
        self.hi = sp.sb(f"{name}_hi", [P, dm.ET])
        self.lo = sp.sb(f"{name}_lo", [P, dm.ET])
        self.pay = sp.sb(f"{name}_pay", [P, dm.ET, 2])
        self.sorted = nc.dram_tensor(f"{name}_sorted", (dm.EPAD, 2), F32, kind="Internal").ap()
        self.count = sp.sb(f"{name}_count", [P, dm.AC])
        self.last = sp.sb(f"{name}_last", [P, dm.AC], I32)
        self.keyT = sp.sb(f"{name}_keyT", [P, dm.ET])
        self.otherT = sp.sb(f"{name}_otherT", [P, dm.ET], I32)
        self.joins = sp.sb(f"{name}_joins", [P, 2, 2, dm.TH])
        self.first_end = sp.sb(f"{name}_first_end", [P, 2], I32)


class Constants:
    def __init__(self, sp, dm):
        self.ident, self.ident_h = sp.sb("ident", [P, P]), sp.sb("ident_h", [P, P], BF16)
        self.lower, self.upper = sp.sb("lower", [P, P]), sp.sb("upper", [P, P])
        self.iota, self.col = sp.sb("iota", [P, dm.WIDE], F16), sp.sb("col", [P, 1])
        self.minus_half, self.ones = sp.sb("minus_half", [P, T]), sp.sb("ones", [P, T])


def split_weights(nc, jobs, tag):
    with ExitStack() as ctx:
        s_upper = Space(nc, ctx, tag).sem("upper")
        with nc.Block() as block:
            @block.vector
            def _(dve):
                for w, (upper, lower) in jobs:
                    split_upper(dve, upper[:, :, :], w[:, :, :]).then_inc(s_upper, 1)
                for n, (w, (upper, lower)) in enumerate(jobs):
                    dve.wait_ge(s_upper, n + 1)
                    split_lower(dve, lower[:, :, :], w[:, :, :], upper[:, :, :])


def load_weights(nc, jobs, tag):
    with ExitStack() as ctx:
        s_load = Space(nc, ctx, tag).sem("load")
        with nc.Block() as block:
            @block.sync
            def _(sync):
                for w, t in jobs:
                    sync.dma_start(t[:, :, :], w.rearrange("(c p) o -> p c o", p=P)).then_inc(s_load, 16)
                sync.wait_ge(s_load, 16 * len(jobs))


def build(nc, a, out, nodes, edges_n):
    dm = Dims(nodes, edges_n)

    def dram(name, shape):
        return nc.dram_tensor(name, shape, F32, kind="Internal").ap()

    l0 = {k[len("L0_gnn_"):]: v for k, v in a.items() if k.startswith("L0_gnn_")}
    l1 = {k[len("L1_gnn_"):]: v for k, v in a.items() if k.startswith("L1_gnn_")}
    h = dram("h", (dm.N, D))
    x1, h1, z = dram("x1", (dm.N, D)), dram("h1", (dm.N, D)), dram("z", (dm.N, D))
    e_dram = dram("weights", (dm.EPAD,))
    raw0, raw1 = dram("raw0", (dm.EPAD, D + 1)), dram("raw1", (dm.EPAD, D))
    ctx_dram = dram("context", (dm.EPAD, D))
    deg_dram = dram("degrees", (dm.NPAD,))
    yT = dram("yT", (D, dm.NPAD))

    with ExitStack() as ctx:
        sp = Space(nc, ctx, "all")
        C = Constants(sp, dm)
        by_src, by_dst = Edges(sp, nc, dm, "src"), Edges(sp, nc, dm, "dst")
        scores = Scores(sp, nc, dm)
        by_src.weightT = sp.sb("weightT", [P, dm.ET])
        w_att, w_hh, w_ih = sp.sb("w_att", [P, KC, D]), sp.sb("w_hh", [P, KC, 3 * D]), sp.sb("w_ih", [P, KC, 3 * D])
        w_hh_parts, w_ih_parts = ([sp.sb(f"{n}_{part}", [P, KC, 3 * D], ONE_PASS) for part in ("upper", "lower")]
                                  for n in ("w_hh", "w_ih"))
        w1a, w1b, w2a, w2b = (sp.sb(n, [P, KC, D]) for n in ("w1a", "w1b", "w2a", "w2b"))
        factor, offset = sp.sb("factor", [P, D]), sp.sb("offset", [P, D])
        sums, lift = sp.sb("sums", [P, 4]), sp.sb("lift", [P, KC])
        coef = [sp.sb(f"coef{j}", [P, 2, KC]) for j in range(3)]

        constants_phase(nc, dm, C)
        edges_phase(nc, dm, C, a["src"], a["dst"], by_src, by_dst)
        sort_phase(nc, dm, C, by_src, "srt0")
        sorted_phase(nc, dm, C, by_src, "srt0t", scores)
        norm_phase(nc, dm, C, a["x"], l0["W_align"], h, scores.terms)
        sort_phase(nc, dm, C, by_dst, "srt1", scores)
        sorted_phase(nc, dm, C, by_dst, "srt1t")
        load_weights(nc, [(l1["W1a"], w1a), (l1["W1b"], w1b), (l1["W2a"], w2a), (l1["W2b"], w2b)], "lw")
        attention_norm_phase(nc, dm, C, l0["b_att"], l0["bn_t_g"], l0["bn_t_b"], l0["bn_t_m"], l0["bn_t_v"], factor, offset)
        flipped_weights(nc, dm, C, [(l0["W_att"], w_att, factor), (l0["W_hh"], w_hh, None), (l0["W_ih"], w_ih, None)], "fw")
        split_weights(nc, [(w_hh, w_hh_parts), (w_ih, w_ih_parts)], "sw")
        weights_phase(nc, dm, C, by_src, scores,
                      (l0["b_align"], l0["bn_a_g"], l0["bn_a_b"], l0["bn_a_m"], l0["bn_a_v"]), e_dram)
        segment_phase(nc, dm, C, by_src, h, raw0, "sg0", weighted=True)
        context_phase(nc, dm, C, raw0, w_att, offset, ctx_dram)
        gru_phase(nc, dm, C, by_src, a["x"], h, ctx_dram, w_ih_parts, w_hh_parts, l0["b_ih"], l0["b_hh"], x1, h1, sums)
        segment_phase(nc, dm, C, by_dst, h1, raw1, "sg1", weighted=False)
        first_norm_phase(nc, dm, C, sums, l1["g0"], l1["b0"], w1a, by_dst.count, coef[0], lift, deg_dram)
        gin_in_phase(nc, dm, C, by_dst, h1, raw1, w1a, l1["b1a"], coef[0], lift, deg_dram, yT, l1["g1"], l1["bt1"], coef[1], "gi1")
        gin_out_phase(nc, dm, C, yT, coef[1], w1b, l1["b1b"], None, z, "go1")
        segment_phase(nc, dm, C, by_dst, z, raw1, "sg2", weighted=False)
        gin_in_phase(nc, dm, C, by_dst, z, raw1, w2a, l1["b2a"], None, None, None, yT, l1["g2"], l1["bt2"], coef[2], "gi2")
        gin_out_phase(nc, dm, C, yT, coef[2], w2b, l1["b2b"], x1, out, "go2")


NAMES = ["x", "src", "dst"] + ["L0_gnn_" + n for n in (
    "W_align", "b_align", "bn_a_g", "bn_a_b", "bn_a_m", "bn_a_v", "W_att", "b_att", "bn_t_g", "bn_t_b", "bn_t_m",
    "bn_t_v", "W_ih", "W_hh", "b_ih", "b_hh")] + ["L1_gnn_" + n for n in (
        "g0", "b0", "W1a", "b1a", "g1", "bt1", "W1b", "b1b", "W2a", "b2a", "g2", "bt2", "W2b", "b2b")]


def kernel(**inputs):
    import concourse.bacc as bacc
    from concourse.bass_utils import run_bass_kernel_spmd as run

    nc = bacc.Bacc("TRN2", target_bir_lowering=False, num_devices=1)
    arrays, args = {}, {}
    for name in NAMES:
        v = np.ascontiguousarray(inputs[name])
        arrays[f"in_{name}"] = v
        args[name] = nc.dram_tensor(f"in_{name}", v.shape, mybir.dt.from_np(v.dtype), kind="ExternalInput").ap()
    nodes, edges_n = inputs["x"].shape[0], inputs["src"].shape[0]
    out = nc.dram_tensor("out_x", (nodes, D), F32, kind="ExternalOutput").ap()
    build(nc, args, out, nodes, edges_n)
    return run(nc, [arrays], core_ids=[0]).results[0]["out_x"]
```
